# Optimizing a Trainium2 kernel written in Bass

```python
import numpy as np
import jax
import jax.numpy as jnp

def _softmax(x, axis=-1):
    return jax.nn.softmax(x, axis=axis)

def _gelu(x):
    return jax.nn.gelu(x, approximate=True)

def _silu(x):
    return jax.nn.silu(x)

def _sigmoid(x):
    return jax.nn.sigmoid(x)

def _layernorm(x, axis=-1, eps=1e-05):
    m = jnp.mean(x, axis=axis, keepdims=True)
    v = jnp.var(x, axis=axis, keepdims=True)
    return (x - m) / jnp.sqrt(v + eps)

def _scatter_add(tgt, idx, src, axis=0):
    return tgt.at[idx].add(src)

def _segment_sum(src, seg, n):
    return jax.ops.segment_sum(src, seg, n)
kernel_name = 'mk_gps_d1_gnn_r8_e88e23'

def setup_inputs(seed: int=0):
    np.random.seed(seed)
    _w = jnp.asarray

    def _rec_inputs():
        import jax
        import jax.numpy as jnp
        _gk = jax.random.key(seed)
        x = -0.0003713 + 1 * jax.random.normal(jax.random.fold_in(_gk, 1), (6250, 256), jnp.float32)
        src = jax.random.randint(jax.random.fold_in(_gk, 2), (100000,), 0, 6250, jnp.int32)
        dst = jax.random.randint(jax.random.fold_in(_gk, 3), (100000,), 0, 6250, jnp.int32)
        _o = jnp.argsort(dst, stable=True)
        src = src[_o]
        dst = dst[_o]
        return (x, src, dst)
    x, src, dst = _rec_inputs()

    def _L0_gnn_setup():
        import jax, jax.numpy as jnp
        import numpy as np
        N, E = (6250, 100000)
        NFEAT, NHID, NCLASS, HEADS = (256, 256, 64, 4)
        NEG_SLOPE = 0.2

        def gat_conv(x, src, dst, W, a_src, a_dst, b):
            H, C = a_src.shape
            h = (x @ W).reshape(-1, H, C)
            alpha_s = jnp.einsum('nhc,hc->nh', h, a_src)
            alpha_d = jnp.einsum('nhc,hc->nh', h, a_dst)
            e = jax.nn.leaky_relu(alpha_s[src] + alpha_d[dst], NEG_SLOPE)
            m = jax.ops.segment_max(e, dst, num_segments=N)
            ex = jnp.exp(e - m[dst])
            s = jax.ops.segment_sum(ex, dst, num_segments=N)
            alpha = ex / (s[dst] + 1e-16)
            out = jax.ops.segment_sum(h[src] * alpha[:, :, None], dst, num_segments=N)
            return out.reshape(-1, H * C) + b
        key = jax.random.key(seed)
        ks = jax.random.split(key, 12)
        glorot = lambda k, shape: jax.random.normal(k, shape, jnp.float32) * jnp.sqrt(2.0 / (shape[0] + shape[-1]))
        x = jax.random.normal(ks[0], (N, NFEAT), jnp.float32)
        edge_index = jax.random.randint(ks[1], (2, E), 0, N, jnp.int64)
        W1 = glorot(ks[2], (NFEAT, HEADS * NCLASS))
        att_src1 = glorot(ks[3], (HEADS, NCLASS))
        att_dst1 = glorot(ks[4], (HEADS, NCLASS))
        b1 = jnp.zeros((HEADS * NCLASS,), jnp.float32)
        W2 = glorot(ks[5], (NHID, HEADS * NCLASS))
        att_src2 = glorot(ks[6], (HEADS, NCLASS))
        att_dst2 = glorot(ks[7], (HEADS, NCLASS))
        b2 = jnp.zeros((HEADS * NCLASS,), jnp.float32)
        return {'x': x, 'edge_index': edge_index, 'W1': W1, 'att_src1': att_src1, 'att_dst1': att_dst1, 'b1': b1, 'W2': W2, 'att_src2': att_src2, 'att_dst2': att_dst2, 'b2': b2}
    _L0_gnn_all = _L0_gnn_setup()
    _L0_gnn_in = {k: v for k, v in _L0_gnn_all.items() if k in ('W1', 'att_src1', 'att_dst1', 'b1', 'W2', 'att_src2', 'att_dst2', 'b2')}
    del _L0_gnn_all

    def _L0_mix_setup():
        import jax, jax.numpy as jnp
        import numpy as np
        HEADS = 8
        DIM_HEAD = 64
        EPS = 1e-05

        def _inst_norm_lastdim(t):
            mu = jnp.mean(t, axis=-1, keepdims=True)
            var = jnp.mean(jnp.square(t - mu), axis=-1, keepdims=True)
            return (t - mu) * jax.lax.rsqrt(var + EPS)
        key = jax.random.key(seed)
        k1, k2, k3, k4 = jax.random.split(key, 4)
        b, n, dim = (4, 1024, 256)
        inner = HEADS * DIM_HEAD
        x = jax.random.normal(k1, (b, n, dim), dtype=jnp.float32)
        Wqkv = jax.random.normal(k2, (3 * inner, dim), dtype=jnp.float32) * (1.0 / np.sqrt(dim))
        Wout = jax.random.normal(k3, (dim, inner), dtype=jnp.float32) * (1.0 / np.sqrt(inner))
        bout = jax.random.normal(k4, (dim,), dtype=jnp.float32) * 0.01
        return {'x': x, 'Wqkv': Wqkv, 'Wout': Wout, 'bout': bout}
    _L0_mix_all = _L0_mix_setup()
    _L0_mix_in = {k: v for k, v in _L0_mix_all.items() if k in ('Wqkv', 'Wout', 'bout')}
    del _L0_mix_all

    def _L0_ffn_setup():
        import jax, jax.numpy as jnp
        import numpy as np
        B, S, H, F, E, K = (8, 512, 256, 512, 16, 2)
        EPS = 1e-05
        key = jax.random.key(seed)
        ks = jax.random.split(key, 9)
        sc = 0.02
        return {'x': jax.random.normal(ks[0], (B, S, H), dtype=jnp.float32), 'gate_w': jax.random.normal(ks[1], (H, E), dtype=jnp.float32) * sc, 'gate_b': jnp.zeros((E,), dtype=jnp.float32), 'w1': jax.random.normal(ks[2], (E, H, F), dtype=jnp.float32) * sc, 'b1': jnp.zeros((E, F), dtype=jnp.float32), 'w2': jax.random.normal(ks[3], (E, F, H), dtype=jnp.float32) * sc, 'b2': jnp.zeros((E, H), dtype=jnp.float32), 'gamma': jnp.ones((H,), dtype=jnp.float32), 'beta': jnp.zeros((H,), dtype=jnp.float32)}
    _L0_ffn_all = _L0_ffn_setup()
    _L0_ffn_in = {k: v for k, v in _L0_ffn_all.items() if k in ('gate_w', 'gate_b', 'w1', 'b1', 'w2', 'b2', 'gamma', 'beta')}
    del _L0_ffn_all
    return {'x': x, 'src': src, 'dst': dst, 'L0_gnn_W1': _L0_gnn_in['W1'], 'L0_gnn_att_src1': _L0_gnn_in['att_src1'], 'L0_gnn_att_dst1': _L0_gnn_in['att_dst1'], 'L0_gnn_b1': _L0_gnn_in['b1'], 'L0_gnn_W2': _L0_gnn_in['W2'], 'L0_gnn_att_src2': _L0_gnn_in['att_src2'], 'L0_gnn_att_dst2': _L0_gnn_in['att_dst2'], 'L0_gnn_b2': _L0_gnn_in['b2'], 'L0_mix_Wqkv': _L0_mix_in['Wqkv'], 'L0_mix_Wout': _L0_mix_in['Wout'], 'L0_mix_bout': _L0_mix_in['bout'], 'L0_ffn_gate_w': _L0_ffn_in['gate_w'], 'L0_ffn_gate_b': _L0_ffn_in['gate_b'], 'L0_ffn_w1': _L0_ffn_in['w1'], 'L0_ffn_b1': _L0_ffn_in['b1'], 'L0_ffn_w2': _L0_ffn_in['w2'], 'L0_ffn_b2': _L0_ffn_in['b2'], 'L0_ffn_gamma': _L0_ffn_in['gamma'], 'L0_ffn_beta': _L0_ffn_in['beta']}

def reference(x, src, dst, L0_gnn_W1, L0_gnn_att_src1, L0_gnn_att_dst1, L0_gnn_b1, L0_gnn_W2, L0_gnn_att_src2, L0_gnn_att_dst2, L0_gnn_b2, L0_mix_Wqkv, L0_mix_Wout, L0_mix_bout, L0_ffn_gate_w, L0_ffn_gate_b, L0_ffn_w1, L0_ffn_b1, L0_ffn_w2, L0_ffn_b2, L0_ffn_gamma, L0_ffn_beta):
    import jax
    import jax.numpy as jnp

    def _L0_gnn_ref(x, edge_index, W1, att_src1, att_dst1, b1, W2, att_src2, att_dst2, b2):
        import jax, jax.numpy as jnp
        import numpy as np
        N, E = (6250, 100000)
        NFEAT, NHID, NCLASS, HEADS = (256, 256, 64, 4)
        NEG_SLOPE = 0.2

        def gat_conv(x, src, dst, W, a_src, a_dst, b):
            H, C = a_src.shape
            h = (x @ W).reshape(-1, H, C)
            alpha_s = jnp.einsum('nhc,hc->nh', h, a_src)
            alpha_d = jnp.einsum('nhc,hc->nh', h, a_dst)
            e = jax.nn.leaky_relu(alpha_s[src] + alpha_d[dst], NEG_SLOPE)
            m = jax.ops.segment_max(e, dst, num_segments=N)
            ex = jnp.exp(e - m[dst])
            s = jax.ops.segment_sum(ex, dst, num_segments=N)
            alpha = ex / (s[dst] + 1e-16)
            out = jax.ops.segment_sum(h[src] * alpha[:, :, None], dst, num_segments=N)
            return out.reshape(-1, H * C) + b
        loops = jnp.arange(N, dtype=edge_index.dtype)
        src = jnp.concatenate([edge_index[0], loops])
        dst = jnp.concatenate([edge_index[1], loops])
        x0 = jax.nn.relu(gat_conv(x, src, dst, W1, att_src1, att_dst1, b1))
        x2 = gat_conv(x0, src, dst, W2, att_src2, att_dst2, b2)
        return x2

    def _L0_mix_ref(x, Wqkv, Wout, bout):
        import jax, jax.numpy as jnp
        import numpy as np
        HEADS = 8
        DIM_HEAD = 64
        EPS = 1e-05

        def _inst_norm_lastdim(t):
            mu = jnp.mean(t, axis=-1, keepdims=True)
            var = jnp.mean(jnp.square(t - mu), axis=-1, keepdims=True)
            return (t - mu) * jax.lax.rsqrt(var + EPS)
        b, n, dim = x.shape
        qkv = jnp.einsum('bnc,fc->bnf', x, Wqkv)
        q, k, v = jnp.split(qkv, 3, axis=-1)

        def to_heads(t):
            return t.reshape(b, n, HEADS, DIM_HEAD).transpose(0, 2, 1, 3)
        q, k, v = (to_heads(q), to_heads(k), to_heads(v))
        k = _inst_norm_lastdim(k)
        v = _inst_norm_lastdim(v)
        dots = jnp.einsum('bhnd,bhne->bhde', k, v)
        out = jnp.einsum('bhnd,bhde->bhne', q, dots) / n
        out = out.transpose(0, 2, 1, 3).reshape(b, n, HEADS * DIM_HEAD)
        return jnp.einsum('bnf,cf->bnc', out, Wout) + bout

    def _L0_ffn_ref(x, gate_w, gate_b, w1, b1, w2, b2, gamma, beta):
        import jax, jax.numpy as jnp
        import numpy as np
        B, S, H, F, E, K = (8, 512, 256, 512, 16, 2)
        EPS = 1e-05
        gate_logits = x @ gate_w + gate_b
        topk_vals, topk_idx = jax.lax.top_k(gate_logits, K)
        topk_w = jax.nn.softmax(topk_vals, axis=-1)
        h = jax.nn.relu(jnp.einsum('bsh,ehf->bsef', x, w1) + b1)
        expert_out = jnp.einsum('bsef,efh->bseh', h, w2) + b2
        sel = jnp.take_along_axis(expert_out, topk_idx[:, :, :, None], axis=2)
        moe = jnp.sum(topk_w[..., None] * sel, axis=2)
        y = x + moe
        mu = jnp.mean(y, axis=-1, keepdims=True)
        var = jnp.var(y, axis=-1, keepdims=True)
        return (y - mu) / jnp.sqrt(var + EPS) * gamma + beta
    edge_index = jnp.stack([src, dst])
    xn = _layernorm(x, axis=-1)
    x = x + _L0_gnn_ref(xn, edge_index, L0_gnn_W1, L0_gnn_att_src1, L0_gnn_att_dst1, L0_gnn_b1, L0_gnn_W2, L0_gnn_att_src2, L0_gnn_att_dst2, L0_gnn_b2) + _L0_mix_ref(xn[None], L0_mix_Wqkv, L0_mix_Wout, L0_mix_bout)[0]
    x = x + _L0_ffn_ref(_layernorm(x, axis=-1)[None], L0_ffn_gate_w, L0_ffn_gate_b, L0_ffn_w1, L0_ffn_b1, L0_ffn_w2, L0_ffn_b2, L0_ffn_gamma, L0_ffn_beta)[0]
    return x

_drawn_inputs = setup_inputs


def setup_inputs(seed=0):
    import zlib

    import numpy as np

    out = dict(_drawn_inputs(seed))
    spreads = {'L0_gnn_b1': (0.0, 0.1),
     'L0_gnn_b2': (0.0, 0.1),
     'L0_ffn_gate_b': (0.0, 0.1),
     'L0_ffn_b1': (0.0, 0.757),
     'L0_ffn_b2': (0.0, 0.1),
     'L0_ffn_gamma': (1.0, 0.2),
     'L0_ffn_beta': (0.0, 0.1)}
    factors = {'L0_gnn_att_dst1': 3.846,
     'L0_gnn_att_src2': 3.878,
     'L0_gnn_att_dst2': 8.0,
     'L0_mix_bout': 6.023}
    for name, (base, spread) in spreads.items():
        noise = np.random.default_rng([zlib.crc32(name.encode()), seed]).standard_normal(out[name].shape)
        drawn = base * np.exp(spread * noise) if base else spread * noise
        out[name] = jnp.asarray(drawn.astype(out[name].dtype))
    for name, factor in factors.items():
        out[name] = (out[name] * factor).astype(out[name].dtype)
    return out
```

```python
from contextlib import ExitStack

import numpy as np
import concourse.bass as bass
from concourse import mybir

F32 = mybir.dt.float32
BF16 = mybir.dt.bfloat16
I32 = mybir.dt.int32
U32 = mybir.dt.uint32
ALU = mybir.AluOpType
ACT = mybir.ActivationFunctionType
AX = mybir.AxisListType
ds = bass.ds

P = 128
N = 6250
E = 100000
C = 256
H = 4
CH = C // H
NT = (N + P - 1) // P
LAST = N - (NT - 1) * P
KT = 8
CE = KT * P
SLOTS = 3
NC = -(-(-(-E // CE)) // SLOTS) * SLOTS
FULL = E // CE
REST = (E - FULL * CE) // KT
GW = C + H
HW = C + 2 * H
MH = 8
MD = 64
MI = MH * MD
EPS = 1e-5
SLOPE = 0.2
NX = 16
FF = 512
A2 = 2 * N
XT = (A2 + NX * (P - 1)) // P
ROWS = XT * P
assert (E - FULL * CE) % KT == 0 and REST < P


def hold(eng, sem, value, tick):
    eng.wait_ge(sem, value)
    eng.sem_inc(tick, 1)


class Chain:

    def __init__(self, eng, sem):
        self.eng, self.sem, self.base, self.n = eng, sem, 0, 0

    def link(self, ins):
        self.n += 1
        ins.then_inc(self.sem, 1)
        self.eng.wait_ge(self.sem, self.base + self.n)

    def hold(self, ins, tick):
        self.n += 1
        ins.then_inc(self.sem, 1)
        hold(self.eng, self.sem, self.base + self.n, tick)

    def at(self, base):
        self.base, self.n = base, 0


def rows_of(i, tail):
    return LAST if tail else P


def tiles(eng, body):
    body(0, 0, True, False)
    body(1, 1, False, False)
    with eng.Fori(1, NT // 2) as m:
        for q in range(2):
            body(m * 2 + q, q, False, False)
    body(NT - 1, (NT - 1) % 2, False, True)


def later(i, n):
    return not isinstance(i, int) or i >= n


def build(nc, a, out):
    dram = {}

    def scratch(name, shape, dt=F32):
        dram[name] = nc.dram_tensor(name, shape, dt, kind="Internal").ap()
        return dram[name]

    srcp = scratch("srcp", (NC * CE,), I32)
    xnT_d = scratch("xnT_d", (NT, P, C))
    table = [scratch("table0", (NT * P, GW)), scratch("table1", (NT * P, GW))]
    y_d = scratch("y_d", (NT * P, C))
    xf_d = scratch("xf_d", (NT * P, C))
    xs_d = scratch("xs_d", (ROWS, C))
    ys_d = scratch("ys_d", (ROWS, C))

    with ExitStack() as top:
        def sb(name, shape, dt=F32, ctx=top):
            return ctx.enter_context(nc.sbuf_tensor(name, shape, dt))

        def stage(program, *args):
            own = []

            def sem(name):
                own.append(nc.alloc_semaphore(name=name))
                return own[-1]
            program(nc, *args, sem)
            nc.clear_and_free_semaphores(own)
            nc.all_engine_barrier()

        ident = sb("ident", [P, P])
        identb = sb("identb", [P, P], BF16)
        ones = sb("ones", [P, P])
        iota = sb("iota", [P, 2 * P], BF16)
        eps = sb("eps", [P, 1])
        mixM = sb("mixM", [P, 2, C])

        with ExitStack() as gnn:
            acc = sb("acc", [P, NT + 2, GW], F32, gnn)
            dtab = sb("dtab", [P, NT + 2, H], F32, gnn)
            dst_rel = sb("dst_rel", [P, NC * KT], F32, gnn)
            dst_r = sb("dst_r", [P, NC * KT], F32, gnn)
            slot = sb("slot", [1, NC], I32, gnn)
            slot_r = sb("slot_r", [1, NC], I32, gnn)
            passes = sb("passes", [1, 1], I32, gnn)
            cmax = sb("cmax", [P, H], F32, gnn)
            dsplit = sb("dsplit", [P, NT + 2, 3, H], BF16, gnn)
            stage(prepare_edges, a, srcp, ident, identb, ones, iota, eps, dst_rel, slot, passes)
            stage(project_inputs, a, xnT_d, table[0], ident, ones, eps, acc, dtab, mixM)
            stage(self_loops, 0, ident, ones, acc, dtab, cmax, dsplit)
            stage(gat_edges, 0, srcp, table[0], identb, iota, acc, dsplit, cmax, dst_rel, dst_r, slot, slot_r, passes)
            stage(project_hidden, a, table[1], ident, acc, dtab)
            stage(self_loops, 1, ident, ones, acc, dtab, cmax, dsplit)
            stage(gat_edges, 1, srcp, table[1], identb, iota, acc, dsplit, cmax, dst_rel, dst_r, slot, slot_r, passes)
            stage(combine, a, xnT_d, y_d, ones, acc, mixM)
        place = sb("place", [P, NT, 2], I32)
        share = sb("share", [P, NT, 2])
        expert = sb("expert", [1, XT], I32)
        hot = sb("pair_hot", [P, NT, 2, NX])
        with ExitStack() as routing:
            xf = sb("xf", [P, NT, C], F32, routing)
            stage(route, a, y_d, xf_d, xs_d, ident, eps, xf, hot, share)
            stage(order, ones, hot, place, expert)
            stage(dispatch, xs_d, xf, place)
        stage(experts, a, xs_d, ys_d, ident, expert)
        stage(finish, a, y_d, xf_d, ys_d, out, ident, eps, hot, place, share)


def prepare_edges(nc, a, srcp, ident, identb, ones, iota, eps, dst_rel, slot, passes, sem):
    with ExitStack() as ctx:
        def sb(name, shape, dt=F32):
            return ctx.enter_context(nc.sbuf_tensor(name, shape, dt))

        NCK = FULL + 1
        iota_i = sb("iota_i", [P, 2 * P], I32)
        zero_i = sb("zero_i", [P, KT], I32)
        dst_i = sb("dst_i", [P, NC * KT], I32)
        by_chunk_i = sb("by_chunk_i", [NCK, CE], I32)
        low = sb("low", [NCK, CE])
        high = sb("high", [NCK, CE])
        ends = sb("ends", [P, 2])
        ends_i = sb("ends_i", [P, 2], I32)
        tiles_i = sb("tiles_i", [P, 2], I32)
        tiles = sb("tiles", [P, 2])
        rows = sb("rows", [1, 2 * P])
        span = sb("span", [1, P])
        count = sb("count", [1, 2])
        count_i = sb("count_i", [1, 1], I32)
        base = sb("base", [P, NC])
        ps = ctx.enter_context(nc.psum_tensor("pe_ps", [P, 512], F32))
        ps2 = ctx.enter_context(nc.psum_tensor("pe_ps2", [P, 512], F32))
        filled, loaded, stored = sem("e_filled"), sem("e_loaded"), sem("e_stored")
        consts, steps, turned, rowed, spread = (sem("e_consts"), sem("e_steps"), sem("e_turned"),
                                                sem("e_rowed"), sem("e_spread"))
        tiled, diag = sem("e_tiled"), sem("e_diag")
        block = ctx.enter_context(nc.Block())
        whole = a["dst"][0:FULL * CE].rearrange("(k p t) -> p k t", p=P, t=KT)
        part = a["dst"][FULL * CE:E].rearrange("(p t) -> p t", t=KT)

        @block.sync
        def _(sp):
            sp.dma_start(srcp[0:E].rearrange("(p f) -> p f", p=P // 4), a["src"].rearrange("(p f) -> p f", p=P // 4)).then_inc(stored, 16)
            sp.wait_ge(filled, 3)
            sp.dma_start(srcp[E:E + (P - REST) * KT].rearrange("(p t) -> p t", t=KT), zero_i[0:P - REST, :]).then_inc(stored, 16)
            for k in range(FULL + 1, NC):
                sp.dma_start(srcp[k * CE:(k + 1) * CE].rearrange("(p t) -> p t", t=KT), zero_i[:, :]).then_inc(stored, 16)
            sp.dma_start(dst_i[:, 0:FULL * KT].rearrange("p (k t) -> p k t", t=KT), whole).then_inc(loaded, 16)
            sp.dma_start(dst_i[0:REST, FULL * KT:(FULL + 1) * KT], part).then_inc(loaded, 16)
            sp.dma_start(by_chunk_i[0:FULL, :], a["dst"][0:FULL * CE].rearrange("(k e) -> k e", e=CE)).then_inc(loaded, 16)
            sp.dma_start(by_chunk_i[FULL:NCK, 0:REST * KT], a["dst"][FULL * CE:E].rearrange("(k e) -> k e", k=1)).then_inc(loaded, 16)
            sp.wait_ge(stored, 16 * (2 + NC - FULL - 1))

        @block.gpsimd
        def _(pool):
            pool.memset(ones[:], 1.0)
            pool.memset(eps[:], EPS)
            pool.memset(ident[:], 0.0).then_inc(diag, 1)
            pool.iota(iota_i[:], pattern=[[1, 2 * P]], base=0, channel_multiplier=0).then_inc(diag, 1)
            pool.wait_ge(diag, 2)
            pool.affine_select(out=ident[:], in_=ident[:], compare_op=ALU.not_equal, fill=1.0, base=0,
                               pattern=[[-1, P]], channel_multiplier=1).then_inc(consts, 1)

        @block.vector
        def _(dve):
            chain = Chain(dve, steps)
            dve.memset(zero_i[:], 0).then_inc(filled, 1)
            dve.memset(dst_i[:], 1 << 20).then_inc(filled, 1)
            dve.memset(by_chunk_i[:], 1 << 20).then_inc(filled, 1)
            dve.wait_ge(consts, 1)
            dve.tensor_copy(iota[:], iota_i[:])
            dve.tensor_copy(identb[:], ident[:])
            dve.wait_ge(loaded, 64)
            dve.tensor_copy(dst_rel[:], dst_i[:])
            dve.tensor_copy(low[:], by_chunk_i[:])
            chain.link(dve.memset(ends[:], 0.0))
            chain.link(dve.tensor_scalar(high[:], low[:], float(1 << 19), -float(1 << 20), ALU.is_ge, ALU.mult))
            chain.link(dve.tensor_tensor(high[:], high[:], low[:], ALU.add))
            chain.link(dve.tensor_reduce(ends[0:NCK, 0:1], low[:], AX.X, ALU.min))
            chain.link(dve.tensor_reduce(ends[0:NCK, 1:2], high[:], AX.X, ALU.max))
            chain.link(dve.tensor_copy(ends_i[:], ends[:]))
            chain.link(dve.tensor_scalar(tiles_i[:], ends_i[:], 7, None, ALU.arith_shift_right))
            dve.tensor_copy(tiles[:], tiles_i[:]).then_inc(tiled, 1)
            dve.wait_ge(turned, 1)
            chain.link(dve.tensor_copy(rows[:], ps[0:1, 0:2 * P]))
            dve.tensor_copy(slot[:], rows[:, 0:NC])
            chain.link(dve.tensor_tensor(span[:], rows[:, P:2 * P], rows[:, 0:P], ALU.subtract))
            chain.link(dve.tensor_reduce(count[:, 0:1], span[:], AX.X, ALU.max))
            chain.link(dve.tensor_copy(count_i[:], count[:, 0:1]))
            chain.link(dve.tensor_scalar(passes[:], count_i[:], 1, None, ALU.arith_shift_right))
            chain.link(dve.tensor_copy(count[:, 1:2], passes[:]))
            chain.link(dve.tensor_scalar(count[:, 1:2], count[:, 1:2], 1.0, None, ALU.add))
            chain.link(dve.tensor_copy(passes[:], count[:, 1:2]))
            dve.tensor_scalar(rows[:, 0:P], rows[:, 0:P], float(P), None, ALU.mult).then_inc(rowed, 1)
            dve.wait_ge(spread, 1)
            chain.link(dve.tensor_copy(base[:], ps2[:, 0:NC]))
            chain.link(dve.tensor_tensor(dst_rel[:].rearrange("p (k t) -> p k t", t=KT), dst_rel[:].rearrange("p (k t) -> p k t", t=KT),
                                         base[:].rearrange("p (k t) -> p k t", t=1).to_broadcast([P, NC, KT]), ALU.subtract))

        @block.tensor
        def _(pe):
            pe.wait_ge(consts, 1)
            pe.wait_ge(tiled, 1)
            pe.transpose(ps[0:1, 0:P], tiles[:, 0:1], ident[:])
            pe.transpose(ps[0:1, P:2 * P], tiles[:, 1:2], ident[:]).then_inc(turned, 1)
            pe.wait_ge(rowed, 1)
            pe.matmul(ps2[:, 0:NC], ones[0:1, :], rows[:, 0:NC], start=True, stop=True).then_inc(spread, 1)


def project_inputs(nc, a, xnT_d, table, ident, ones, eps, acc, dtab, mixM, sem):
    with ExitStack() as ctx:
        def sb(name, shape, dt=F32):
            return ctx.enter_context(nc.sbuf_tensor(name, shape, dt))

        def pb(name, shape):
            return ctx.enter_context(nc.psum_tensor(name, shape, F32))

        wext = sb("wext0", [P, 2, HW])
        att = sb("att0", [P, 2, C])
        attw = sb("attw0", [P, 2, C])
        wkv = sb("wkv", [P, 8, C])
        wkvT = sb("wkvT", [P, 2, 2 * MI])
        wmean = sb("wmean", [P, 2 * MH])
        wq = sb("wq", [P, 4, C])
        wout = sb("wout", [P, 2, MI])
        woutT = sb("woutT", [P, 4, C])
        dotsT = sb("dotsT", [P, 4, P])
        z = sb("zmix", [P, 4, C])
        x = sb("x_in", [P, 2, C])
        st = sb("st", [P, 2, 6])
        mv = sb("mv", [P, 2, 2])
        rs = sb("rs", [P, 2, 2])
        xn = sb("xn", [P, 2, C])
        xnT = sb("xnT", [P, 2, 2, P])
        sq = sb("sq", [P, 2 * MI])
        ss = sb("ss", [P, 3, 2 * MH])
        rkv = sb("rkv", [P, MH])
        ks = sb("ks", [P, 2, MI])
        vs = sb("vs", [P, 2, MI])
        psX = pb("psX", [P, 512])
        psH = pb("psH", [P, 512])
        psKV = pb("psKV", [P, 2 * MI])
        psD = pb("psD", [P, 512])
        psW = pb("psW", [P, 512])
        loaded, steps, turned, moved = sem("i_loaded"), sem("i_steps"), sem("i_turned"), sem("i_moved")
        first_block = ExitStack()
        block = first_block.enter_context(nc.Block())

        @block.sync
        def _(sp):
            sp.dma_start(wext[:, :, 0:C], a["L0_gnn_W1"].rearrange("(k p) n -> p k n", p=P)).then_inc(loaded, 16)
            sp.dma_start(att[:, 0, :], a["L0_gnn_att_src1"].rearrange("(o h) c -> o (h c)", o=1).to_broadcast([P, C])).then_inc(loaded, 16)
            sp.dma_start(att[:, 1, :], a["L0_gnn_att_dst1"].rearrange("(o h) c -> o (h c)", o=1).to_broadcast([P, C])).then_inc(loaded, 16)
            sp.dma_start(wkv[:], a["L0_mix_Wqkv"][MI:3 * MI, :].rearrange("(k p) c -> p k c", p=P)).then_inc(loaded, 16)
            sp.dma_start(wq[:], a["L0_mix_Wqkv"][0:MI, :].rearrange("(k p) c -> p k c", p=P)).then_inc(loaded, 16)
            sp.dma_start(wout[:], a["L0_mix_Wout"].rearrange("(k p) c -> p k c", p=P)).then_inc(loaded, 16)

        @block.vector
        def _(dve):
            chain = Chain(dve, steps)
            dve.memset(acc[:, NT:NT + 2, :], 0.0)
            dve.memset(dtab[:, NT:NT + 2, :], 0.0)
            dve.memset(dotsT[:], 0.0)
            dve.wait_ge(loaded, 96)
            attention_columns(dve, chain, wext, att, attw)
            for g in range(6):
                dve.wait_ge(turned, g + 1)
                if g < 4:
                    kc, q = g // 2, g % 2
                    dve.tensor_copy(wkvT[:, kc, q * 512:(q + 1) * 512], psW[:, :]).then_inc(moved, 1)
                else:
                    dve.tensor_copy(woutT[:, :, (g - 4) * P:(g - 3) * P], psW[:, :].rearrange("p (k f) -> p k f", k=4)).then_inc(moved, 1)
            dve.wait_ge(moved, 6)
            for kc in range(2):
                w = wkvT[:, kc, :].rearrange("p (g d) -> p g d", d=MD)
                chain.link(dve.tensor_reduce(wmean[:], w, AX.X, ALU.add))
                chain.link(dve.tensor_scalar(wmean[:], wmean[:], 1.0 / MD, None, ALU.mult))
                chain.link(dve.tensor_tensor(w, w, wmean[:].rearrange("p (g d) -> p g d", d=1).to_broadcast([P, 2 * MH, MD]), ALU.subtract))

        @block.tensor
        def _(pe):
            pe.wait_ge(loaded, 96)
            for g in range(6):
                if g:
                    pe.wait_ge(moved, g)
                for j in range(4):
                    if g < 4:
                        kc, q = g // 2, g % 2
                        ins = pe.transpose(psW[:, j * P:(j + 1) * P], wkv[:, 4 * q + j, kc * P:(kc + 1) * P], ident[:])
                    else:
                        ins = pe.transpose(psW[:, j * P:(j + 1) * P], wout[:, g - 4, j * P:(j + 1) * P], ident[:])
                ins.then_inc(turned, 1)

        first_block.close()
        names = ("x_in0", "x_in1", "xT_out0", "xT_out1", "xT_ps", "xT", "h_ps", "h_out", "h_stored", "kv_ps", "squared", "ks", "vs", "dots", "lnsum", "root", "xn", "kvsum", "kvroot", "tick")
        s = {n: sem("i_" + n) for n in names}
        vsteps = sem("i_vsteps")
        asteps = sem("i_asteps")
        block2 = ctx.enter_context(nc.Block())

        @block2.sync
        def _(sp):
            def load(i, q, first, tail):
                r = rows_of(i, tail)
                if later(i, 2):
                    sp.wait_ge(s["xn"], i - 1)
                sp.dma_start(x[0:r, q, :], a["x"][ds(i * P, r), :]).then_inc(s[f"x_in{q}"], 16)

            tiles(sp, load)

        @block2.gpsimd
        def _(pool):
            def store(i, q, first, tail):
                pool.wait_ge(s["xT"], i + 1)
                pool.dma_start(xnT_d[ds(i, 1), :, :].rearrange("o p f -> (o p) f"), xnT[:, q, :, :].rearrange("p k f -> p (k f)")).then_inc(s[f"xT_out{q}"], 16)
                pool.wait_ge(s["h_out"], i * 2 + 2)
                pool.dma_start(table[ds(i * P, P), :], acc[:, ds(i, 1), :].rearrange("p o f -> p (o f)")).then_inc(s["h_stored"], 16)
            tiles(pool, store)
            pool.wait_ge(s["xT_out0"], 16 * (NT - NT // 2))
            pool.wait_ge(s["xT_out1"], 16 * (NT // 2))
            pool.wait_ge(s["h_stored"], 16 * NT)

        @block2.vector
        def _(dve):
            chain = Chain(dve, vsteps)
            STEPS = 4

            def body(i, q, first, tail):
                chain.at(i * STEPS)
                dve.wait_ge(s[f"x_in{q}"], 8 * (i - q) + 16)
                chain.hold(dve.bn_stats(st[:, q, :], x[:, q, :]), s["tick"])
                dve.bn_aggr(mv[:, q, :], st[:, q, :]).then_inc(s["lnsum"], 1)
                dve.wait_ge(s["root"], i + 1)
                chain.link(dve.reciprocal(rs[:, q, 1:2], rs[:, q, 0:1]))
                if later(i, 2):
                    dve.wait_ge(s["xT_ps"], i - 1)
                dve.tensor_scalar(xn[:, q, :], x[:, q, :], mv[:, q, 0:1], rs[:, q, 1:2], ALU.subtract, ALU.mult).then_inc(s["xn"], 1)
                hold(dve, s["h_ps"], i + 1, s["tick"])
                dve.tensor_copy(acc[:, ds(i, 1), :].rearrange("p o f -> p (o f)"), psH[:, 0:GW]).then_inc(s["h_out"], 1)
                dve.tensor_copy(dtab[:, ds(i, 1), :].rearrange("p o f -> p (o f)"), psH[:, GW:HW]).then_inc(s["h_out"], 1)
                dve.wait_ge(s["squared"], i + 1)
                dve.tensor_reduce(ss[:, 0, :], sq[:].rearrange("p (g d) -> p g d", d=MD), AX.X, ALU.add).then_inc(s["kvsum"], 1)
                dve.wait_ge(s["kvroot"], i + 1)
                chain.link(dve.reciprocal(ss[:, 2, :], ss[:, 1, :]))
                chain.link(dve.tensor_tensor(rkv[:], ss[:, 2, 0:MH], ss[:, 2, MH:2 * MH], ALU.mult))
                if later(i, 2):
                    dve.wait_ge(s["dots"], i - 1)
                dve.tensor_tensor(ks[:, q, :].rearrange("p (g d) -> p g d", d=MD), psKV[:, 0:MI].rearrange("p (g d) -> p g d", d=MD),
                                  rkv[:].rearrange("p (g d) -> p g d", d=1).to_broadcast([P, MH, MD]), ALU.mult).then_inc(s["ks"], 1)
                assert chain.n == STEPS, chain.n
            tiles(dve, body)
            dve.wait_ge(s["dots"], NT)
            for hp in range(4):
                for d in range(2):
                    last = dve.tensor_scalar(dotsT[d * MD:(d + 1) * MD, hp, d * MD:(d + 1) * MD], psD[d * MD:(d + 1) * MD, hp * P + d * MD:hp * P + (d + 1) * MD],
                                             1.0 / N, None, ALU.mult)
            last.then_inc(s["dots"], 1)
            dve.wait_ge(s["dots"], NT + 2)
            dve.tensor_copy(z[:, 0:2, :].rearrange("p k f -> p (k f)"), psKV[:, 0:512])
            dve.tensor_copy(z[:, 2:4, :].rearrange("p k f -> p (k f)"), psKV[:, 512:1024]).then_inc(s["dots"], 1)
            dve.wait_ge(s["dots"], NT + 4)
            dve.tensor_copy(mixM[:].rearrange("p k f -> p (k f)"), psD[:, 0:2 * C])

        @block2.scalar
        def _(act):
            def body(i, q, first, tail):
                act.wait_ge(s["lnsum"], i + 1)
                act.activation(rs[:, q, 0:1], mv[:, q, 1:2], ACT.Sqrt, bias=eps[:, 0:1]).then_inc(s["root"], 1)
                act.wait_ge(s["xT_ps"], i + 1)
                if later(i, 2):
                    act.wait_ge(s[f"xT_out{q}"], 8 * (i - q))
                act.activation(xnT[:, q, :, :].rearrange("p k f -> p (k f)"), psX[:, 0:2 * P], ACT.Copy).then_inc(s["xT"], 1)
                act.wait_ge(s["kv_ps"], i + 1)
                if later(i, 1):
                    act.wait_ge(s["kvsum"], i)
                act.activation(sq[:], psKV[:], ACT.Square).then_inc(s["squared"], 1)
                if later(i, 2):
                    act.wait_ge(s["dots"], i - 1)
                act.activation(vs[:, q, :], psKV[:, MI:2 * MI], ACT.Copy).then_inc(s["vs"], 1)
                act.wait_ge(s["kvsum"], i + 1)
                act.activation(ss[:, 1, :], ss[:, 0, :], ACT.Sqrt, bias=eps[:, 0:1], scale=1.0 / MD).then_inc(s["kvroot"], 1)
            tiles(act, body)

        @block2.tensor
        def _(pe):
            def body(i, q, first, tail):
                pe.wait_ge(s["xn"], i + 1)
                if later(i, 1):
                    pe.wait_ge(s["xT"], i)
                for kc in range(2):
                    ins = pe.transpose(psX[:, kc * P:(kc + 1) * P], xn[:, q, kc * P:(kc + 1) * P], ident[:])
                ins.then_inc(s["xT_ps"], 1)
                pe.wait_ge(s["xT"], i + 1)
                if later(i, 1):
                    pe.wait_ge(s["h_out"], i * 2)
                r = rows_of(i, tail)
                for kc in range(2):
                    ins = pe.matmul(psH[:, 0:HW], xnT[:, q, kc, :], wext[:, kc, :], start=(kc == 0), stop=(kc == 1))
                ins.then_inc(s["h_ps"], 1)
                if later(i, 1):
                    pe.wait_ge(s["ks"], i)
                    pe.wait_ge(s["vs"], i)
                for half in range(2):
                    for kc in range(2):
                        ins = pe.matmul(psKV[:, half * 512:(half + 1) * 512], xnT[:, q, kc, :], wkvT[:, kc, half * 512:(half + 1) * 512],
                                        start=(kc == 0), stop=(kc == 1))
                ins.then_inc(s["kv_ps"], 1)
                pe.wait_ge(s["ks"], i + 1)
                pe.wait_ge(s["vs"], i + 1)
                for hp in range(4):
                    ins = pe.matmul(psD[:, hp * P:(hp + 1) * P], vs[0:r, q, hp * P:(hp + 1) * P], ks[0:r, q, hp * P:(hp + 1) * P],
                                    start=(first and hp == 0), stop=tail, skip_group_check=True)
                ins.then_inc(s["dots"], 1)
            tiles(pe, body)
            pe.wait_ge(s["dots"], NT + 1)
            for hp in range(4):
                ins = pe.matmul(psKV[:, hp * C:(hp + 1) * C], dotsT[:, hp, :], woutT[:, hp, :], start=True, stop=True)
            ins.then_inc(s["dots"], 1)
            pe.wait_ge(s["dots"], NT + 3)
            for kc in range(2):
                for hp in range(4):
                    ins = pe.matmul(psD[:, kc * C:(kc + 1) * C], wq[:, hp, kc * P:(kc + 1) * P], z[:, hp, :], start=(hp == 0), stop=(hp == 3))
            ins.then_inc(s["dots"], 1)


def attention_columns(dve, chain, wext, att, attw):
    for j in range(2):
        for kc in range(2):
            chain.link(dve.tensor_tensor(attw[:, kc, :], wext[:, kc, 0:C], att[:, j, :], ALU.mult))
            chain.link(dve.tensor_reduce(wext[:, kc, C + j * H:C + (j + 1) * H], attw[:, kc, :].rearrange("p (h c) -> p h c", h=H), AX.X, ALU.add))


def self_loops(nc, layer, ident, ones, acc, dtab, cmax, dsplit, sem):
    with ExitStack() as ctx:
        def sb(name, shape, dt=F32):
            return ctx.enter_context(nc.sbuf_tensor(f"{name}_{layer}", shape, dt))

        top = sb("sl_top", [P, H])
        head = sb("sl_head", [H, 1])
        diag = sb("sl_diag", [H, H])
        z = sb("sl_z", [P, NT, H])
        y = sb("sl_y", [P, NT, H])
        rest = sb("sl_rest", [P, NT + 2, H])
        ps = ctx.enter_context(nc.psum_tensor(f"sl_ps{layer}", [P, 512], F32))
        steps, topped, turned, diagonal, spread, logits, weights = (sem(f"sl_{n}{layer}") for n in (
            "steps", "topped", "turned", "diagonal", "spread", "logits", "weights"))
        block = ctx.enter_context(nc.Block())

        def wide(t):
            return t[:].rearrange("p (o h) -> p o h", o=1).to_broadcast([P, NT, H])

        @block.vector
        def _(dve):
            chain = Chain(dve, steps)
            chain.link(dve.tensor_reduce(top[:], acc[:, 0:NT - 1, C:GW].rearrange("p i h -> p h i"), AX.X, ALU.max))
            dve.tensor_tensor(top[0:LAST, :], top[0:LAST, :], acc[0:LAST, NT - 1, C:GW], ALU.max).then_inc(topped, 1)
            dve.wait_ge(turned, 1)
            chain.link(dve.tensor_reduce(head[:], ps[0:H, 0:P], AX.X, ALU.max))
            dve.tensor_scalar(diag[:], ident[0:H, 0:H], head[:, 0:1], None, ALU.mult).then_inc(diagonal, 1)
            dve.tensor_copy(dsplit[:, :, 0, :], dtab[:])
            chain.link(dve.tensor_tensor(z[:], acc[:, 0:NT, C:GW], dtab[:, 0:NT, :], ALU.add))
            chain.link(dve.tensor_tensor(rest[:], dtab[:], dsplit[:, :, 0, :], ALU.subtract))
            chain.link(dve.tensor_copy(dsplit[:, :, 1, :], rest[:]))
            chain.link(dve.tensor_tensor(rest[:], rest[:], dsplit[:, :, 1, :], ALU.subtract))
            chain.link(dve.tensor_copy(dsplit[:, :, 2, :], rest[:]))
            dve.wait_ge(spread, 1)
            chain.link(dve.tensor_copy(cmax[:], ps[:, 256:256 + H]))
            chain.link(dve.tensor_tensor(y[:], dtab[:, 0:NT, :], wide(cmax), ALU.add))
            chain.link(dve.scalar_tensor_tensor(z[:], z[:], SLOPE, z[:], ALU.mult, ALU.max))
            chain.link(dve.scalar_tensor_tensor(y[:], y[:], SLOPE, y[:], ALU.mult, ALU.max))
            dve.tensor_tensor(z[:], z[:], y[:], ALU.subtract).then_inc(logits, 1)
            dve.wait_ge(weights, 1)
            for h in range(H):
                f = acc[:, 0:NT, h * CH:(h + 1) * CH]
                dve.tensor_tensor(f, f, acc[:, 0:NT, C + h:C + h + 1].to_broadcast([P, NT, CH]), ALU.mult)

        @block.scalar
        def _(act):
            act.wait_ge(logits, 1)
            act.activation(acc[:, 0:NT, C:GW], z[:], ACT.Exp).then_inc(weights, 1)

        @block.tensor
        def _(pe):
            pe.wait_ge(topped, 1)
            pe.transpose(ps[0:H, 0:P], top[:], ident[:]).then_inc(turned, 1)
            pe.wait_ge(diagonal, 1)
            pe.matmul(ps[:, 256:256 + H], ones[0:H, :], diag[:], start=True, stop=True).then_inc(spread, 1)


def gat_edges(nc, layer, srcp, table, identb, iota, acc, dsplit, cmax, dst_rel, dst_r, slot, slot_r, passes, sem):
    with ExitStack() as ctx:
        def sb(name, shape, dt=F32):
            return ctx.enter_context(nc.sbuf_tensor(f"{name}_{layer}", shape, dt))

        def pb(name, shape, dt=F32):
            return ctx.enter_context(nc.psum_tensor(f"{name}_{layer}", shape, dt))

        idx = sb("idx", [P, SLOTS, KT], I32)
        G = sb("gathered", [P, SLOTS, KT, GW])
        hot = sb("hot", [P, SLOTS, KT, 2 * P], BF16)
        hotf = sb("hotf", [P, SLOTS, KT, 2 * P])
        hotT = sb("hotT", [P, SLOTS, KT, 2, P], BF16)
        d = sb("d_e", [P, KT, H])
        z = sb("z_e", [P, KT, H])
        y = sb("y_e", [P, KT, H])
        t = sb("t_e", [P, KT, H])
        psT = pb("psT", [P, KT, 2, P], BF16)
        psD = pb("psD_e", [P, KT, 3, H])
        psA = pb("psA_e", [P, 2, 512])
        names = ("idx_in0", "idx_in1", "idx_in2", "g_in0", "g_in1", "g_in2", "hot", "turned", "hotT", "hotf", "targets", "target_read",
                 "logits", "weights", "scaled", "added", "acc", "pass", "vsteps", "tick")
        s = {n: sem(f"g{layer}_{n}") for n in names}
        block = ctx.enter_context(nc.Block())
        TURNS = NC // SLOTS

        def chunks(eng, rounds, before, step):
            with eng.Fori(0, rounds) as r:
                base = r * NC
                before(base, r)
                with eng.Fori(0, TURNS - 1) as m:
                    for q in range(SLOTS):
                        step(base + m * SLOTS + q, m * SLOTS + q, q, 2, r * TURNS + m)
                for q in range(SLOTS):
                    step(base + (NC - SLOTS + q), NC - SLOTS + q, q, SLOTS - 1 - q, r * TURNS + (TURNS - 1))

        @block.sync
        def _(sp):
            rounds = sp.value_load(passes[0:1, 0:1], min_val=1, max_val=NT)

            def step(g, c, q, after, turn):
                sp.wait_ge(s["logits"], g + 1)
                sp.dma_start(idx[:, q, :], srcp[ds(c * CE, CE)].rearrange("(p t) -> p t", t=KT)).then_inc(s[f"idx_in{q}"], 16)
            chunks(sp, rounds, lambda base, r: None, step)

        @block.gpsimd
        def _(pool):
            rounds = pool.value_load(passes[0:1, 0:1], min_val=1, max_val=NT)

            def step(g, c, q, after, turn):
                pool.wait_ge(s[f"idx_in{q}"], 16 * turn + 16)
                hold(pool, s["added"], g + 1, s["tick"])
                for k in range(KT):
                    pool.indirect_dma_start(out=G[:, q, k, :], out_offset=None, in_=table,
                                            in_offset=bass.IndirectOffsetOnAxis(ap=idx[:, q, k:k + 1], axis=0)).then_inc(s[f"g_in{q}"], 16)
            chunks(pool, rounds, lambda base, r: None, step)

        @block.vector
        def _(dve):
            dve.sem_inc(s["logits"], SLOTS)
            dve.sem_inc(s["target_read"], 1)
            dve.sem_inc(s["acc"], 1)
            dve.tensor_copy(dst_r[:], dst_rel[:]).then_inc(s["pass"], 1)
            dve.tensor_copy(slot_r[:], slot[:]).then_inc(s["pass"], 1)
            rounds = dve.value_load(passes[0:1, 0:1], min_val=1, max_val=NT)
            chain = Chain(dve, s["vsteps"])
            STEPS = 5

            def one_hot(c, q, g):
                for k in range(KT):
                    ins = dve.tensor_scalar(hot[:, q, k, :], iota[:], dst_r[:, ds(c * KT + k, 1)], None, ALU.is_equal)
                ins.then_inc(s["hot"], 1)

            def weigh(c, q, g, turn):
                chain.at(g * STEPS)
                dve.wait_ge(s["targets"], g + 1)
                chain.link(dve.tensor_reduce(d[:], psD[:].rearrange("p k c h -> p k h c"), AX.X, ALU.add))
                chain.link(dve.tensor_tensor(y[:], d[:], cmax[:].rearrange("p (o h) -> p o h", o=1).to_broadcast([P, KT, H]), ALU.add))
                dve.sem_inc(s["target_read"], 1)
                chain.link(dve.scalar_tensor_tensor(y[:], y[:], SLOPE, y[:], ALU.mult, ALU.max))
                dve.wait_ge(s[f"g_in{q}"], 16 * KT * turn + 16 * KT)
                chain.link(dve.tensor_tensor(z[:], d[:], G[:, q, :, C:GW], ALU.add))
                chain.link(dve.scalar_tensor_tensor(z[:], z[:], SLOPE, z[:], ALU.mult, ALU.max))
                dve.tensor_tensor(t[:], z[:], y[:], ALU.subtract).then_inc(s["logits"], 1)
                dve.wait_ge(s["weights"], g + 1)
                f = G[:, q, :, 0:C].rearrange("p k (h c) -> p k h c", h=H)
                w = G[:, q, :, C:GW].rearrange("p k (h c) -> p k h c", c=1).to_broadcast([P, KT, H, CH])
                dve.tensor_tensor(f, f, w, ALU.mult).then_inc(s["scaled"], 1)
                assert chain.n == STEPS

            def before(base, r):
                dve.wait_ge(s["pass"], r * 2 + 2)
                one_hot(0, 0, base)
                one_hot(1, 1, base + 1)
                weigh(0, 0, base, r * TURNS)

            def step(g, c, q, after, turn):
                if after >= 2:
                    one_hot(c + 2, (q + 2) % SLOTS, g + 2)
                if after >= 1:
                    weigh(c + 1, (q + 1) % SLOTS, g + 1, turn + (1 if q == SLOTS - 1 else 0))
                first = dve.value_load(slot_r[0:1, ds(c, 1)], min_val=0, max_val=NT)
                dve.wait_ge(s["acc"], g + 1)
                dve.wait_ge(s["added"], g + 1 + SLOTS)
                dve.tensor_tensor(acc[:, ds(first, 2), :], acc[:, ds(first, 2), :], psA[:, :, 0:GW], ALU.add).then_inc(s["acc"], 1)
                if after == 0:
                    dve.tensor_scalar(dst_r[:], dst_r[:], -2.0 * P, None, ALU.add).then_inc(s["pass"], 1)
                    dve.tensor_scalar(slot_r[:], slot_r[:], 2, NT, ALU.add, ALU.min).then_inc(s["pass"], 1)
            chunks(dve, rounds, before, step)

        @block.scalar
        def _(act):
            act.sem_inc(s["hotT"], 1)
            rounds = act.value_load(passes[0:1, 0:1], min_val=1, max_val=NT)

            def copies(c, q, g):
                act.wait_ge(s["hot"], g + 1)
                act.wait_ge(s["added"], g + 1)
                act.activation(hotf[:, q, :, :], hot[:, q, :, :], ACT.Copy).then_inc(s["hotf"], 1)
                act.wait_ge(s["turned"], g + 1)
                act.activation(hotT[:, q, :, :, :].rearrange("p k j e -> p (k j e)"), psT[:].rearrange("p k j e -> p (k j e)"), ACT.Copy).then_inc(s["hotT"], 1)

            def exps(c, q, g):
                act.wait_ge(s["logits"], g + 1 + SLOTS)
                act.activation(G[:, q, :, C:GW], t[:], ACT.Exp).then_inc(s["weights"], 1)

            def before(base, r):
                copies(0, 0, base)
                copies(1, 1, base + 1)
                exps(0, 0, base)

            def step(g, c, q, after, turn):
                if after >= 1:
                    exps(c + 1, (q + 1) % SLOTS, g + 1)
                if after >= 2:
                    copies(c + 2, (q + 2) % SLOTS, g + 2)
            chunks(act, rounds, before, step)

        @block.tensor
        def _(pe):
            pe.sem_inc(s["added"], SLOTS)
            rounds = pe.value_load(passes[0:1, 0:1], min_val=1, max_val=NT)

            def turn_hot(c, q, g):
                pe.wait_ge(s["hot"], g + 1)
                pe.wait_ge(s["hotT"], g + 1)
                for k in range(KT):
                    for j in range(2):
                        ins = pe.transpose(psT[:, k, j, :], hot[:, q, k, j * P:(j + 1) * P], identb[:])
                ins.then_inc(s["turned"], 1)

            def targets(c, q, g):
                first = pe.value_load(slot_r[0:1, ds(c, 1)], min_val=0, max_val=NT)
                pe.wait_ge(s["hotT"], g + 2)
                pe.wait_ge(s["target_read"], g + 1)
                for k in range(KT):
                    for j in range(2):
                        ins = pe.matmul(psD[:, k, :, :].rearrange("p c h -> p (c h)"), hotT[:, q, k, j, :],
                                        dsplit[:, ds(first + j, 1), :, :].rearrange("p o c h -> p (o c h)"), start=(j == 0), stop=(j == 1))
                ins.then_inc(s["targets"], 1)

            def add(c, q, g):
                pe.wait_ge(s["hotf"], g + 1)
                pe.wait_ge(s["scaled"], g + 1)
                pe.wait_ge(s["acc"], g + 1)
                for j in range(2):
                    for k in range(KT):
                        ins = pe.matmul(psA[:, j, 0:GW], hotf[:, q, k, j * P:(j + 1) * P], G[:, q, k, :], start=(k == 0), stop=(k == KT - 1))
                ins.then_inc(s["added"], 1)

            def before(base, r):
                pe.wait_ge(s["pass"], r * 2 + 2)
                turn_hot(0, 0, base)
                turn_hot(1, 1, base + 1)
                targets(0, 0, base)

            def step(g, c, q, after, turn):
                if after >= 1:
                    targets(c + 1, (q + 1) % SLOTS, g + 1)
                if after >= 2:
                    turn_hot(c + 2, (q + 2) % SLOTS, g + 2)
                add(c, q, g)
            chunks(pe, rounds, before, step)


def project_hidden(nc, a, table, ident, acc, dtab, sem):
    with ExitStack() as ctx:
        def sb(name, shape, dt=F32):
            return ctx.enter_context(nc.sbuf_tensor(name, shape, dt))

        wext = sb("wext1", [P, 2, HW])
        att = sb("att1", [P, 2, C])
        attw = sb("attw1", [P, 2, C])
        bias = sb("bias1", [P, C])
        rden = sb("rden1", [P, H])
        h = sb("h1", [P, 2, C])
        hT = sb("hT1", [P, 2, 2, P])
        psX = ctx.enter_context(nc.psum_tensor("psX1", [P, 512], F32))
        psH = ctx.enter_context(nc.psum_tensor("psH1", [P, 512], F32))
        s = {n: sem("h_" + n) for n in ("loaded", "steps", "hidden", "turned", "relu", "projected", "out", "stored", "tick")}
        block = ctx.enter_context(nc.Block())

        @block.sync
        def _(sp):
            sp.dma_start(wext[:, :, 0:C], a["L0_gnn_W2"].rearrange("(k p) n -> p k n", p=P)).then_inc(s["loaded"], 16)
            sp.dma_start(att[:, 0, :], a["L0_gnn_att_src2"].rearrange("(o h) c -> o (h c)", o=1).to_broadcast([P, C])).then_inc(s["loaded"], 16)
            sp.dma_start(att[:, 1, :], a["L0_gnn_att_dst2"].rearrange("(o h) c -> o (h c)", o=1).to_broadcast([P, C])).then_inc(s["loaded"], 16)
            sp.dma_start(bias[:], a["L0_gnn_b1"].rearrange("(o c) -> o c", o=1).to_broadcast([P, C])).then_inc(s["loaded"], 16)

            def store(i, q, first, tail):
                sp.wait_ge(s["out"], i * 2 + 2)
                sp.dma_start(table[ds(i * P, P), :], acc[:, ds(i, 1), :].rearrange("p o f -> p (o f)")).then_inc(s["stored"], 16)
            tiles(sp, store)
            sp.wait_ge(s["stored"], 16 * NT)

        @block.vector
        def _(dve):
            chain = Chain(dve, s["steps"])
            dve.wait_ge(s["loaded"], 64)
            attention_columns(dve, chain, wext, att, attw)
            start = chain.n
            STEPS = 2

            def body(i, q, first, tail):
                chain.at(i * STEPS + start)
                chain.link(dve.reciprocal(rden[:], acc[:, ds(i, 1), C:GW].rearrange("p o h -> p (o h)")))
                if later(i, 2):
                    dve.wait_ge(s["turned"], i - 1)
                v = h[:, q, :].rearrange("p (h c) -> p h c", h=H)
                chain.link(dve.tensor_tensor(v, acc[:, ds(i, 1), 0:C].rearrange("p o (h c) -> p (o h) c", h=H),
                                             rden[:].rearrange("p (h c) -> p h c", c=1).to_broadcast([P, H, CH]), ALU.mult))
                dve.tensor_tensor(h[:, q, :], h[:, q, :], bias[:], ALU.add).then_inc(s["hidden"], 1)
                hold(dve, s["projected"], i + 1, s["tick"])
                dve.tensor_copy(acc[:, ds(i, 1), :].rearrange("p o f -> p (o f)"), psH[:, 0:GW]).then_inc(s["out"], 1)
                dve.tensor_copy(dtab[:, ds(i, 1), :].rearrange("p o f -> p (o f)"), psH[:, GW:HW]).then_inc(s["out"], 1)
                assert chain.n == STEPS
            tiles(dve, body)

        @block.scalar
        def _(act):
            def body(i, q, first, tail):
                act.wait_ge(s["turned"], i + 1)
                if later(i, 2):
                    act.wait_ge(s["projected"], i - 1)
                act.activation(hT[:, q, :, :].rearrange("p k f -> p (k f)"), psX[:, 0:2 * P], ACT.Relu).then_inc(s["relu"], 1)
            tiles(act, body)

        @block.tensor
        def _(pe):
            def body(i, q, first, tail):
                pe.wait_ge(s["hidden"], i + 1)
                if later(i, 1):
                    pe.wait_ge(s["relu"], i)
                for kc in range(2):
                    ins = pe.transpose(psX[:, kc * P:(kc + 1) * P], h[:, q, kc * P:(kc + 1) * P], ident[:])
                ins.then_inc(s["turned"], 1)
                pe.wait_ge(s["relu"], i + 1)
                if later(i, 1):
                    pe.wait_ge(s["out"], i * 2)
                for kc in range(2):
                    ins = pe.matmul(psH[:, 0:HW], hT[:, q, kc, :], wext[:, kc, :], start=(kc == 0), stop=(kc == 1))
                ins.then_inc(s["projected"], 1)
            tiles(pe, body)


def combine(nc, a, xnT_d, y_d, ones, acc, mixM, sem):
    with ExitStack() as ctx:
        def sb(name, shape, dt=F32):
            return ctx.enter_context(nc.sbuf_tensor(name, shape, dt))

        bias = sb("cbias", [P, 2, C])
        x = sb("cx", [P, 2, C])
        xnT = sb("cxnT", [P, 2, 2, P])
        rden = sb("crden", [P, H])
        y = sb("cy", [P, 2, C])
        ps = ctx.enter_context(nc.psum_tensor("cps", [P, 2, 512], F32))
        s = {n: sem("c_" + n) for n in ("loaded", "steps", "x0", "x1", "mixed", "y", "stored0", "stored1")}
        block = ctx.enter_context(nc.Block())

        @block.sync
        def _(sp):
            sp.dma_start(bias[:, 0, :], a["L0_gnn_b2"].rearrange("(o c) -> o c", o=1).to_broadcast([P, C])).then_inc(s["loaded"], 16)
            sp.dma_start(bias[:, 1, :], a["L0_mix_bout"].rearrange("(o c) -> o c", o=1).to_broadcast([P, C])).then_inc(s["loaded"], 16)

            def load(i, q, first, tail):
                r = rows_of(i, tail)
                if later(i, 2):
                    sp.wait_ge(s["y"], i - 1)
                sp.dma_start(x[0:r, q, :], a["x"][ds(i * P, r), :]).then_inc(s[f"x{q}"], 16)
                sp.dma_start(xnT[:, q, :, :].rearrange("p k f -> p (k f)"), xnT_d[ds(i, 1), :, :].rearrange("o p f -> (o p) f")).then_inc(s[f"x{q}"], 16)
            tiles(sp, load)

        @block.tensor
        def _(pe):
            def body(i, q, first, tail):
                pe.wait_ge(s[f"x{q}"], 16 * (i - q) + 32)
                if later(i, 2):
                    pe.wait_ge(s["y"], i - 1)
                for kc in range(2):
                    ins = pe.matmul(ps[:, q, 0:C], xnT[:, q, kc, :], mixM[:, kc, :], start=(kc == 0), stop=(kc == 1))
                ins.then_inc(s["mixed"], 1)
            tiles(pe, body)

        @block.vector
        def _(dve):
            chain = Chain(dve, s["steps"])
            dve.wait_ge(s["loaded"], 32)
            chain.link(dve.tensor_tensor(bias[:, 0, :], bias[:, 0, :], bias[:, 1, :], ALU.add))
            STEPS = 4

            def body(i, q, first, tail):
                chain.at(i * STEPS + 1)
                chain.link(dve.reciprocal(rden[:], acc[:, ds(i, 1), C:GW].rearrange("p o h -> p (o h)")))
                if later(i, 2):
                    dve.wait_ge(s[f"stored{q}"], 8 * (i - q))
                chain.link(dve.tensor_tensor(y[:, q, :].rearrange("p (h c) -> p h c", h=H), acc[:, ds(i, 1), 0:C].rearrange("p o (h c) -> p (o h) c", h=H),
                                             rden[:].rearrange("p (h c) -> p h c", c=1).to_broadcast([P, H, CH]), ALU.mult))
                chain.link(dve.tensor_tensor(y[:, q, :], y[:, q, :], bias[:, 0, :], ALU.add))
                dve.wait_ge(s[f"x{q}"], 16 * (i - q) + 32)
                chain.link(dve.tensor_tensor(y[:, q, :], y[:, q, :], x[:, q, :], ALU.add))
                dve.wait_ge(s["mixed"], i + 1)
                dve.tensor_tensor(y[:, q, :], y[:, q, :], ps[:, q, 0:C], ALU.add).then_inc(s["y"], 1)
                assert chain.n == STEPS
            tiles(dve, body)

        @block.gpsimd
        def _(pool):
            def body(i, q, first, tail):
                pool.wait_ge(s["y"], i + 1)
                pool.dma_start(y_d[ds(i * P, P), :], y[:, q, :]).then_inc(s[f"stored{q}"], 16)
            tiles(pool, body)
            pool.wait_ge(s["stored0"], 16 * (NT - NT // 2))
            pool.wait_ge(s["stored1"], 16 * (NT // 2))


def normalize(dve, chain, tick, x, st, mv, rs, lnsum, root, count):
    chain.hold(dve.bn_stats(st, x), tick)
    dve.bn_aggr(mv, st).then_inc(lnsum, 1)
    dve.wait_ge(root, count)
    chain.link(dve.reciprocal(rs[:, 1:2], rs[:, 0:1]))


def route(nc, a, y_d, xf_d, xs_d, ident, eps, xf, hot, share, sem):
    with ExitStack() as ctx:
        def sb(name, shape, dt=F32):
            return ctx.enter_context(nc.sbuf_tensor(name, shape, dt))

        gate = sb("gate", [P, 2, NX])
        bias = sb("gbias", [P, NX])
        zero = sb("zero_rows", [P, C])
        y = sb("ry", [P, 2, C])
        st = sb("rst", [P, 2, 6])
        mv = sb("rmv", [P, 2, 2])
        rs = sb("rrs", [P, 2, 2])
        xT = sb("rxT", [P, 2, 2, P])
        xt = sb("rxt", [P, 2, C])
        logits = sb("rlogits", [P, NX])
        top_v = sb("top_v", [P, 8])
        top_i = sb("top_i", [P, 8], U32)
        top_if = sb("top_if", [P, NT, 2])
        top_vf = sb("top_vf", [P, NT, 2])
        number_i = sb("number_i", [P, NX], I32)
        number = sb("number", [P, NX])
        ex = sb("rex", [P, NT])
        one = sb("rone", [P, NT])
        ps = ctx.enter_context(nc.psum_tensor("rps", [P, 512], F32))
        psG = ctx.enter_context(nc.psum_tensor("rpsG", [P, 512], F32))
        s = {n: sem("r_" + n) for n in ("loaded", "y0", "y1", "steps", "lnsum", "root", "xf", "turned", "xT", "gated", "gate_read", "picked",
                                        "stored", "cleared", "zero", "number", "gap", "exp", "tick", "end")}
        block = ctx.enter_context(nc.Block())

        @block.sync
        def _(sp):
            sp.dma_start(gate[:], a["L0_ffn_gate_w"].rearrange("(k p) e -> p k e", p=P)).then_inc(s["loaded"], 16)
            sp.dma_start(bias[:], a["L0_ffn_gate_b"].rearrange("(o e) -> o e", o=1).to_broadcast([P, NX])).then_inc(s["loaded"], 16)

            def load(i, q, first, tail):
                if later(i, 2):
                    sp.wait_ge(s["xf"], i - 1)
                sp.dma_start(y[:, q, :], y_d[ds(i * P, P), :]).then_inc(s[f"y{q}"], 16)
            tiles(sp, load)
            sp.wait_ge(s["zero"], 1)
            sp.dma_start(xs_d.rearrange("(t p) c -> p t c", p=P), zero[:].rearrange("p (o c) -> p o c", o=1).to_broadcast([P, XT, C])).then_inc(s["cleared"], 16)
            sp.wait_ge(s["cleared"], 16)

        @block.gpsimd
        def _(pool):
            pool.memset(zero[:], 0.0).then_inc(s["zero"], 1)
            pool.iota(number_i[:], pattern=[[1, NX]], base=0, channel_multiplier=0).then_inc(s["number"], 1)

            def store(i, q, first, tail):
                pool.wait_ge(s["xf"], i + 1)
                pool.dma_start(xf_d[ds(i * P, P), :], xf[:, ds(i, 1), :].rearrange("p o f -> p (o f)")).then_inc(s["stored"], 16)
            tiles(pool, store)
            pool.wait_ge(s["stored"], 16 * NT)

        @block.vector
        def _(dve):
            chain = Chain(dve, s["steps"])
            dve.wait_ge(s["number"], 1)
            chain.link(dve.tensor_copy(number[:], number_i[:]))
            dve.wait_ge(s["loaded"], 32)
            STEPS = 5

            def body(i, q, first, tail):
                chain.at(i * STEPS + 1)
                dve.wait_ge(s[f"y{q}"], 8 * (i - q) + 16)
                normalize(dve, chain, s["tick"], y[:, q, :], st[:, q, :], mv[:, q, :], rs[:, q, :], s["lnsum"], s["root"], i + 1)
                if later(i, 2):
                    dve.wait_ge(s["turned"], i - 1)
                chain.hold(dve.tensor_scalar(xt[:, q, :], y[:, q, :], mv[:, q, 0:1], rs[:, q, 1:2], ALU.subtract, ALU.mult), s["tick"])
                dve.tensor_copy(xf[:, ds(i, 1), :].rearrange("p o f -> p (o f)"), xt[:, q, :]).then_inc(s["xf"], 1)
                dve.wait_ge(s["gated"], i + 1)
                chain.hold(dve.tensor_tensor(logits[:], psG[:, 0:NX], bias[:], ALU.add), s["tick"])
                chain.hold(dve.max(top_v[:], logits[:]), s["tick"])
                hold(dve, s["xf"], i + 1, s["tick"])
                dve.tensor_copy(top_vf[:, ds(i, 1), :].rearrange("p o f -> p (o f)"), top_v[:, 0:2])
                dve.max_index(top_i[:], top_v[:], logits[:]).then_inc(s["picked"], 1)
                hold(dve, s["picked"], i + 1, s["tick"])
                dve.tensor_copy(top_if[:, ds(i, 1), :].rearrange("p o f -> p (o f)"), top_i[:, 0:2]).then_inc(s["gate_read"], 1)
                assert chain.n == STEPS, chain.n
            tiles(dve, body)
            dve.wait_ge(s["gate_read"], NT)
            dve.tensor_tensor(ex[:], top_vf[:, :, 1], top_vf[:, :, 0], ALU.subtract).then_inc(s["gap"], 1)
            dve.tensor_tensor(hot[:], number[:].rearrange("p (a b e) -> p a b e", a=1, b=1).to_broadcast([P, NT, 2, NX]),
                              top_if[:].rearrange("p t (s e) -> p t s e", e=1).to_broadcast([P, NT, 2, NX]), ALU.is_equal)
            dve.wait_ge(s["exp"], 1)
            chain.at(NT * STEPS + 1)
            chain.link(dve.tensor_scalar(one[:], ex[:], 1.0, None, ALU.add))
            chain.link(dve.reciprocal(share[:, :, 0], one[:]))
            chain.link(dve.tensor_tensor(share[:, :, 1], share[:, :, 0], ex[:], ALU.mult))

        @block.scalar
        def _(act):
            def body(i, q, first, tail):
                act.wait_ge(s["lnsum"], i + 1)
                act.activation(rs[:, q, 0:1], mv[:, q, 1:2], ACT.Sqrt, bias=eps[:, 0:1]).then_inc(s["root"], 1)
                act.wait_ge(s["turned"], i + 1)
                if later(i, 2):
                    act.wait_ge(s["gated"], i - 1)
                act.activation(xT[:, q, :, :].rearrange("p k f -> p (k f)"), ps[:, 0:2 * P], ACT.Copy).then_inc(s["xT"], 1)
            tiles(act, body)
            act.wait_ge(s["gap"], 1)
            act.activation(ex[:], ex[:], ACT.Exp).then_inc(s["exp"], 1)

        @block.tensor
        def _(pe):
            pe.wait_ge(s["loaded"], 32)

            def body(i, q, first, tail):
                pe.wait_ge(s["xf"], i + 1)
                if later(i, 1):
                    pe.wait_ge(s["xT"], i)
                for kc in range(2):
                    ins = pe.transpose(ps[:, kc * P:(kc + 1) * P], xt[:, q, kc * P:(kc + 1) * P], ident[:])
                ins.then_inc(s["turned"], 1)
                pe.wait_ge(s["xT"], i + 1)
                if later(i, 1):
                    pe.wait_ge(s["gate_read"], i)
                for kc in range(2):
                    ins = pe.matmul(psG[:, 0:NX], xT[:, q, kc, :], gate[:, kc, :], start=(kc == 0), stop=(kc == 1))
                ins.then_inc(s["gated"], 1)
            tiles(pe, body)


def order(nc, ones, hot, place, expert, sem):
    with ExitStack() as ctx:
        def sb(name, shape, dt=F32):
            return ctx.enter_context(nc.sbuf_tensor(name, shape, dt))

        before = sb("before", [P, P])
        both = sb("both", [P, NT, NX])
        rank = sb("rank", [P, NT, NX])
        total = sb("total", [P, NX, NT])
        carry = sb("carry", [P, NX, NT])
        keep = sb("keep", [P, NX, NT])
        count = sb("xcount", [P, NX])
        count_i = sb("xcount_i", [P, NX], I32)
        ntiles = sb("ntiles", [P, NX])
        upto = sb("upto", [P, NX])
        first = sb("xfirst", [P, NX])
        picked = sb("picked", [P, NT, NX])
        row = sb("row", [P, NT, 2])
        numbers_i = sb("numbers_i", [1, XT], I32)
        numbers = sb("numbers", [1, XT])
        past = sb("past", [1, XT, NX])
        owner = sb("owner", [1, XT])
        ps = [ctx.enter_context(nc.psum_tensor(f"ops{n}", [P, 512], F32)) for n in range(4)]
        s = {n: sem("o_" + n) for n in ("consts", "steps", "both", "ranked", "pads")}
        block = ctx.enter_context(nc.Block())
        HALF = (NT + 1) // 2
        parts = ((0, HALF), (HALF, NT))

        @block.gpsimd
        def _(pool):
            pool.memset(before[:], 1.0).then_inc(s["pads"], 1)
            pool.iota(numbers_i[:], pattern=[[1, XT]], base=0, channel_multiplier=0).then_inc(s["consts"], 1)
            pool.wait_ge(s["pads"], 1)
            pool.affine_select(out=before[:], in_=before[:], compare_op=ALU.is_gt, fill=0.0, base=0,
                               pattern=[[1, P]], channel_multiplier=-1).then_inc(s["consts"], 1)

        @block.vector
        def _(dve):
            chain = Chain(dve, s["steps"])
            dve.wait_ge(s["consts"], 2)
            chain.link(dve.tensor_copy(numbers[:], numbers_i[:]))
            end = hot[:, NT - 1, :, :].rearrange("p s e -> p (s e)")
            chain.link(dve.tensor_scalar(end, end, before[:, LAST:LAST + 1], None, ALU.mult))
            chain.link(dve.tensor_tensor(both[:], hot[:, :, 0, :], hot[:, :, 1, :], ALU.add))
            chain.link(dve.memset(keep[:], 1.0))
            dve.memset(keep[:, :, 0], 0.0).then_inc(s["both"], 1)
            dve.wait_ge(s["ranked"], 1)
            for n, (lo, hi) in enumerate(parts):
                w = (hi - lo) * NX
                chain.link(dve.tensor_copy(rank[:, lo:hi, :].rearrange("p t e -> p (t e)"), ps[n][:, 0:w]))
                chain.link(dve.tensor_copy(total[:, :, lo:hi].rearrange("p e t -> p t e"), ps[2 + n][:, 0:w].rearrange("p (t e) -> p t e", e=NX)))
            chain.link(dve.tensor_tensor_scan(carry[:].rearrange("p e t -> p (e t)"), keep[:].rearrange("p e t -> p (e t)"),
                                              total[:].rearrange("p e t -> p (e t)"), 0.0, ALU.mult, ALU.add))
            chain.link(dve.tensor_scalar(count[:], carry[:, :, NT - 1], float(P - 1), None, ALU.add))
            chain.link(dve.tensor_tensor(carry[:], carry[:], total[:], ALU.subtract))
            chain.link(dve.tensor_copy(count_i[:], count[:]))
            chain.link(dve.tensor_scalar(count_i[:], count_i[:], 7, None, ALU.arith_shift_right))
            chain.link(dve.tensor_copy(ntiles[:], count_i[:]))
            chain.link(dve.memset(first[:], 1.0))
            chain.link(dve.tensor_tensor_scan(upto[:], first[:], ntiles[:], 0.0, ALU.mult, ALU.add))
            chain.link(dve.tensor_tensor(first[:], upto[:], ntiles[:], ALU.subtract))
            chain.link(dve.tensor_scalar(first[:], first[:], float(P), None, ALU.mult))
            chain.link(dve.tensor_tensor(rank[:], rank[:], carry[:].rearrange("p e t -> p t e"), ALU.add))
            chain.link(dve.tensor_tensor(rank[:], rank[:], first[:].rearrange("p (o e) -> p o e", o=1).to_broadcast([P, NT, NX]), ALU.add))
            for k in range(2):
                chain.link(dve.tensor_tensor(picked[:], rank[:], hot[:, :, k, :], ALU.mult))
                chain.link(dve.tensor_reduce(row[:, :, k], picked[:], AX.X, ALU.add))
            chain.link(dve.tensor_copy(place[:], row[:]))
            chain.link(dve.tensor_tensor(past[:], numbers[:].rearrange("o (t e) -> o t e", e=1).to_broadcast([1, XT, NX]),
                                         upto[0:1, :].rearrange("o (t e) -> o t e", t=1).to_broadcast([1, XT, NX]), ALU.is_ge))
            chain.link(dve.tensor_reduce(owner[:], past[:], AX.X, ALU.add))
            chain.link(dve.tensor_scalar(owner[:], owner[:], float(NX - 1), None, ALU.min))
            chain.link(dve.tensor_copy(expert[:], owner[:]))

        @block.tensor
        def _(pe):
            pe.wait_ge(s["consts"], 2)
            pe.wait_ge(s["both"], 1)
            for n, (lo, hi) in enumerate(parts):
                w = (hi - lo) * NX
                rhs = both[:, lo:hi, :].rearrange("p t e -> p (t e)")
                pe.matmul(ps[n][:, 0:w], before[:], rhs, start=True, stop=True)
                ins = pe.matmul(ps[2 + n][:, 0:w], ones[:], rhs, start=True, stop=True)
            ins.then_inc(s["ranked"], 1)


def dispatch(nc, xs_d, xf, place, sem):
    with ExitStack() as ctx:
        rows = ctx.enter_context(nc.sbuf_tensor("disp_rows", [P, 2, C], F32))
        idx = ctx.enter_context(nc.sbuf_tensor("disp_idx", [P, 2, 2], I32))
        s = {n: sem("d_" + n) for n in ("rows", "idx", "sent0", "sent1", "tick")}
        block = ctx.enter_context(nc.Block())

        @block.scalar
        def _(act):
            def body(i, q, first, tail):
                if later(i, 2):
                    act.wait_ge(s[f"sent{q}"], 16 * (i - q))
                act.activation(rows[:, q, :], xf[:, ds(i, 1), :].rearrange("p o f -> p (o f)"), ACT.Copy).then_inc(s["rows"], 1)
            tiles(act, body)

        @block.vector
        def _(dve):
            def body(i, q, first, tail):
                if later(i, 2):
                    hold(dve, s[f"sent{q}"], 16 * (i - q), s["tick"])
                dve.tensor_copy(idx[:, q, :], place[:, ds(i, 1), :].rearrange("p o f -> p (o f)")).then_inc(s["idx"], 1)
            tiles(dve, body)

        @block.gpsimd
        def _(pool):
            def body(i, q, first, tail):
                r = rows_of(i, tail)
                pool.wait_ge(s["rows"], i + 1)
                hold(pool, s["idx"], i + 1, s["tick"])
                for k in range(2):
                    pool.indirect_dma_start(out=xs_d, out_offset=bass.IndirectOffsetOnAxis(ap=idx[0:r, q, k:k + 1], axis=0),
                                            in_=rows[0:r, q, :], in_offset=None).then_inc(s[f"sent{q}"], 16)
            tiles(pool, body)
            pool.wait_ge(s["sent0"], 32 * (NT - NT // 2))
            pool.wait_ge(s["sent1"], 32 * (NT // 2))


def experts(nc, a, xs_d, ys_d, ident, expert, sem):
    with ExitStack() as ctx:
        def sb(name, shape, dt=F32):
            return ctx.enter_context(nc.sbuf_tensor(name, shape, dt))

        KF = FF // P
        w1 = sb("w1", [P, NX, 2, FF])
        w2 = sb("w2", [P, NX, KF, C])
        b1 = sb("b1", [P, NX, FF])
        x = sb("xx", [P, 2, C])
        xT = sb("xxT", [P, 2, 2, P])
        hid = sb("hid", [P, FF])
        hidT = sb("hidT", [P, FF])
        o = sb("xo", [P, 2, C])
        psX = ctx.enter_context(nc.psum_tensor("xpsX", [P, 512], F32))
        psH = ctx.enter_context(nc.psum_tensor("xpsH", [P, 512], F32))
        psT = ctx.enter_context(nc.psum_tensor("xpsT", [P, 512], F32))
        psO = ctx.enter_context(nc.psum_tensor("xpsO", [P, 512], F32))
        s = {n: sem("x_" + n) for n in ("loaded", "x0", "x1", "turned", "xT", "hid_ps", "hid", "hid_turned", "hidT", "o_ps", "o", "st0", "st1")}
        block = ctx.enter_context(nc.Block())

        def pairs(eng, body, lead=None):
            if lead:
                lead()
            body(0, 0, True)
            body(1, 1, True)
            with eng.Fori(1, XT // 2) as m:
                for q in range(2):
                    body(m * 2 + q, q, True)
            body(XT - 1, (XT - 1) % 2, False)
        assert XT % 2 == 1

        @block.sync
        def _(sp):
            for e in range(0, NX, 4):
                sp.dma_start(w1[:, e:e + 4, :, :], a["L0_ffn_w1"][e:e + 4].rearrange("e (k p) f -> p e k f", p=P)).then_inc(s["loaded"], 16)
                sp.dma_start(w2[:, e:e + 4, :, :], a["L0_ffn_w2"][e:e + 4].rearrange("e (k p) f -> p e k f", p=P)).then_inc(s["loaded"], 16)
            sp.dma_start(b1[:].rearrange("p e f -> p (e f)"), a["L0_ffn_b1"].rearrange("(o e) f -> o (e f)", o=1).to_broadcast([P, NX * FF])).then_inc(s["loaded"], 16)

            def load(j, q, more):
                if later(j, 2):
                    sp.wait_ge(s["turned"], j - 1)
                sp.dma_start(x[:, q, :], xs_d[ds(j * P, P), :]).then_inc(s[f"x{q}"], 16)
            pairs(sp, load)

        @block.scalar
        def _(act):
            def turned(j, q):
                act.wait_ge(s["turned"], j + 1)
                act.activation(xT[:, q, :, :].rearrange("p k f -> p (k f)"), psX[:, 0:2 * P], ACT.Copy).then_inc(s["xT"], 1)

            def body(j, q, more):
                if more:
                    turned(j + 1, 1 - q)
                act.wait_ge(s["hid_turned"], j + 1)
                if later(j, 1):
                    act.wait_ge(s["o_ps"], j)
                act.activation(hidT[:], psT[:], ACT.Relu).then_inc(s["hidT"], 1)
            pairs(act, body, lambda: turned(0, 0))

        @block.vector
        def _(dve):
            def bias(j, q):
                e = dve.value_load(expert[0:1, ds(j, 1)], min_val=0, max_val=NX - 1)
                dve.wait_ge(s["hid_ps"], j + 1)
                if later(j, 1):
                    dve.wait_ge(s["hid_turned"], j)
                dve.tensor_tensor(hid[:], psH[:], b1[:, ds(e, 1), :].rearrange("p o f -> p (o f)"), ALU.add).then_inc(s["hid"], 1)

            def body(j, q, more):
                if more:
                    bias(j + 1, 1 - q)
                dve.wait_ge(s["o_ps"], j + 1)
                if later(j, 2):
                    dve.wait_ge(s[f"st{q}"], 8 * (j - q))
                dve.tensor_copy(o[:, q, :], psO[:, 0:C]).then_inc(s["o"], 1)
            dve.wait_ge(s["loaded"], 144)
            pairs(dve, body, lambda: bias(0, 0))

        @block.tensor
        def _(pe):
            def turn(j, q):
                pe.wait_ge(s[f"x{q}"], 8 * (j - q) + 16)
                if later(j, 1):
                    pe.wait_ge(s["xT"], j)
                for kc in range(2):
                    ins = pe.transpose(psX[:, kc * P:(kc + 1) * P], x[:, q, kc * P:(kc + 1) * P], ident[:])
                ins.then_inc(s["turned"], 1)

            def up(j, q):
                e = pe.value_load(expert[0:1, ds(j, 1)], min_val=0, max_val=NX - 1)
                pe.wait_ge(s["xT"], j + 1)
                if later(j, 1):
                    pe.wait_ge(s["hid"], j)
                for kc in range(2):
                    ins = pe.matmul(psH[:], xT[:, q, kc, :], w1[:, ds(e, 1), kc, :].rearrange("p o f -> p (o f)"), start=(kc == 0), stop=(kc == 1))
                ins.then_inc(s["hid_ps"], 1)

            def body(j, q, more):
                e = pe.value_load(expert[0:1, ds(j, 1)], min_val=0, max_val=NX - 1)
                if more:
                    turn(j + 1, 1 - q)
                pe.wait_ge(s["hid"], j + 1)
                if later(j, 1):
                    pe.wait_ge(s["hidT"], j)
                for k in range(KF):
                    ins = pe.transpose(psT[:, k * P:(k + 1) * P], hid[:, k * P:(k + 1) * P], ident[:])
                ins.then_inc(s["hid_turned"], 1)
                if more:
                    up(j + 1, 1 - q)
                pe.wait_ge(s["hidT"], j + 1)
                if later(j, 1):
                    pe.wait_ge(s["o"], j)
                for k in range(KF):
                    ins = pe.matmul(psO[:, 0:C], hidT[:, k * P:(k + 1) * P], w2[:, ds(e, 1), k, :].rearrange("p o f -> p (o f)"),
                                    start=(k == 0), stop=(k == KF - 1))
                ins.then_inc(s["o_ps"], 1)

            def lead():
                pe.wait_ge(s["loaded"], 144)
                turn(0, 0)
                up(0, 0)
            pairs(pe, body, lead)

        @block.gpsimd
        def _(pool):
            def body(j, q, more):
                pool.wait_ge(s["o"], j + 1)
                pool.dma_start(ys_d[ds(j * P, P), :], o[:, q, :]).then_inc(s[f"st{q}"], 16)
            pairs(pool, body)
            pool.wait_ge(s["st0"], 16 * (XT - XT // 2))
            pool.wait_ge(s["st1"], 16 * (XT // 2))


def finish(nc, a, y_d, xf_d, ys_d, out, ident, eps, hot, place, share, sem):
    with ExitStack() as ctx:
        def sb(name, shape, dt=F32):
            return ctx.enter_context(nc.sbuf_tensor(name, shape, dt))

        b2 = sb("fb2", [NX, C])
        gamma = sb("gamma", [P, C])
        beta = sb("beta", [P, C])
        mass = sb("mass", [P, NT, NX])
        mass2 = sb("mass2", [P, NT, NX])
        idx = sb("fidx", [P, 2, 2], I32)
        massT = sb("massT", [NX, 2, P])
        y = sb("fy", [P, 2, C])
        xf = sb("fxf", [P, 2, C])
        e1 = sb("fe1", [P, 2, C])
        e2 = sb("fe2", [P, 2, C])
        st = sb("fst", [P, 2, 6])
        mv = sb("fmv", [P, 2, 2])
        rs = sb("frs", [P, 2, 2])
        o = sb("fo", [P, 2, C])
        m1 = sb("m1", [P, 2, NX])
        psM = ctx.enter_context(nc.psum_tensor("fpsM", [P, 512], F32))
        psB = ctx.enter_context(nc.psum_tensor("fpsB", [P, 512], F32))
        s = {n: sem("f_" + n) for n in ("loaded", "steps", "y0", "y1", "idx", "e0", "e1", "mass", "m1", "mass_turned", "massT", "bias",
                                        "bias_read", "lnsum", "root", "o", "out0", "out1", "tick", "moe")}
        block = ctx.enter_context(nc.Block())

        @block.sync
        def _(sp):
            sp.dma_start(b2[:], a["L0_ffn_b2"]).then_inc(s["loaded"], 16)
            sp.dma_start(gamma[:], a["L0_ffn_gamma"].rearrange("(o e) -> o e", o=1).to_broadcast([P, C])).then_inc(s["loaded"], 16)
            sp.dma_start(beta[:], a["L0_ffn_beta"].rearrange("(o e) -> o e", o=1).to_broadcast([P, C])).then_inc(s["loaded"], 16)

            def load(i, q, first, tail):
                if later(i, 2):
                    sp.wait_ge(s["o"], i - 1)
                sp.dma_start(y[:, q, :], y_d[ds(i * P, P), :]).then_inc(s[f"y{q}"], 16)
                sp.dma_start(xf[:, q, :], xf_d[ds(i * P, P), :]).then_inc(s[f"y{q}"], 16)
            tiles(sp, load)

        @block.gpsimd
        def _(pool):
            def body(i, q, first, tail):
                if later(i, 2):
                    pool.wait_ge(s["moe"], i - 1)
                hold(pool, s["idx"], i + 1, s["tick"])
                for k, dst in enumerate((e1, e2)):
                    pool.indirect_dma_start(out=dst[:, q, :], out_offset=None, in_=ys_d,
                                            in_offset=bass.IndirectOffsetOnAxis(ap=idx[:, q, k:k + 1], axis=0)).then_inc(s[f"e{q}"], 16)
            tiles(pool, body)

        @block.scalar
        def _(act):
            def store(i, q, first, tail):
                r = rows_of(i, tail)
                act.wait_ge(s["mass_turned"], i + 1)
                if later(i, 2):
                    act.wait_ge(s["bias"], i - 1)
                act.activation(massT[:, q, :], psM[0:NX, 0:P], ACT.Copy).then_inc(s["massT"], 1)
                act.wait_ge(s["lnsum"], i + 1)
                act.activation(rs[:, q, 0:1], mv[:, q, 1:2], ACT.Sqrt, bias=eps[:, 0:1]).then_inc(s["root"], 1)
                act.wait_ge(s["o"], i + 1)
                act.dma_start(out[ds(i * P, r), :], o[0:r, q, :]).then_inc(s[f"out{q}"], 16)
            tiles(act, store)
            act.wait_ge(s["out0"], 16 * (NT - NT // 2))
            act.wait_ge(s["out1"], 16 * (NT // 2))

        @block.tensor
        def _(pe):
            pe.wait_ge(s["loaded"], 48)

            def body(i, q, first, tail):
                pe.wait_ge(s["m1"], i + 1)
                if later(i, 1):
                    pe.wait_ge(s["massT"], i)
                pe.transpose(psM[0:NX, 0:P], m1[:, q, :], ident[:]).then_inc(s["mass_turned"], 1)
                pe.wait_ge(s["massT"], i + 1)
                if later(i, 1):
                    pe.wait_ge(s["bias_read"], i)
                pe.matmul(psB[:, 0:C], massT[:, q, :], b2[:], start=True, stop=True).then_inc(s["bias"], 1)
            tiles(pe, body)

        @block.vector
        def _(dve):
            chain = Chain(dve, s["steps"])
            dve.wait_ge(s["loaded"], 48)
            for k, m in enumerate((mass, mass2)):
                chain.link(dve.tensor_tensor(m[:], hot[:, :, k, :], share[:, :, k:k + 1].to_broadcast([P, NT, NX]), ALU.mult))
            chain.link(dve.tensor_tensor(mass[:], mass[:], mass2[:], ALU.add))
            STEPS = 6

            def fetch(i, q):
                if later(i, 2):
                    hold(dve, s[f"e{q}"], 16 * (i - q), s["tick"])
                dve.tensor_copy(idx[:, q, :], place[:, ds(i, 1), :].rearrange("p o f -> p (o f)")).then_inc(s["idx"], 1)
                if later(i, 2):
                    hold(dve, s["mass_turned"], i - 1, s["tick"])
                dve.tensor_copy(m1[:, q, :], mass[:, ds(i, 1), :].rearrange("p o f -> p (o f)")).then_inc(s["m1"], 1)

            def body(i, q, first, tail):
                if not tail:
                    fetch(i + 1, 1 - q)
                chain.at(i * STEPS + 3)
                dve.wait_ge(s[f"y{q}"], 16 * (i - q) + 32)
                dve.wait_ge(s[f"e{q}"], 16 * (i - q) + 32)
                dve.wait_ge(s["bias"], i + 1)
                z = xf[:, q, :]
                dve.tensor_tensor(z, z, psB[:, 0:C], ALU.add).then_inc(s["bias_read"], 1)
                dve.wait_ge(s["bias_read"], i + 1)
                chain.link(dve.scalar_tensor_tensor(z, e1[:, q, :], share[:, ds(i, 1), 0:1].rearrange("p o f -> p (o f)"), z, ALU.mult, ALU.add))
                dve.scalar_tensor_tensor(z, e2[:, q, :], share[:, ds(i, 1), 1:2].rearrange("p o f -> p (o f)"), z, ALU.mult, ALU.add).then_inc(s["moe"], 1)
                hold(dve, s["moe"], i + 1, s["tick"])
                normalize(dve, chain, s["tick"], z, st[:, q, :], mv[:, q, :], rs[:, q, :], s["lnsum"], s["root"], i + 1)
                chain.link(dve.tensor_scalar(z, z, mv[:, q, 0:1], rs[:, q, 1:2], ALU.subtract, ALU.mult))
                chain.link(dve.tensor_tensor(z, z, gamma[:], ALU.mult))
                chain.link(dve.tensor_tensor(z, z, beta[:], ALU.add))
                if later(i, 2):
                    dve.wait_ge(s[f"out{q}"], 8 * (i - q))
                dve.tensor_tensor(o[:, q, :], z, y[:, q, :], ALU.add).then_inc(s["o"], 1)
                assert chain.n == STEPS, chain.n
            fetch(0, 0)
            tiles(dve, body)


_INS = ["x", "src", "dst", "L0_gnn_W1", "L0_gnn_att_src1", "L0_gnn_att_dst1", "L0_gnn_b1", "L0_gnn_W2", "L0_gnn_att_src2",
        "L0_gnn_att_dst2", "L0_gnn_b2", "L0_mix_Wqkv", "L0_mix_Wout", "L0_mix_bout", "L0_ffn_gate_w", "L0_ffn_gate_b",
        "L0_ffn_w1", "L0_ffn_b1", "L0_ffn_w2", "L0_ffn_b2", "L0_ffn_gamma", "L0_ffn_beta"]


def kernel(**inputs):
    import numpy as _np
    import concourse.bacc as _bacc
    from concourse import mybir as _mybir
    from concourse.bass_utils import run_bass_kernel_spmd as _run

    nc = _bacc.Bacc("TRN2", target_bir_lowering=False, num_devices=1)
    arrays, args = {}, {}
    for name in _INS:
        array = _np.ascontiguousarray(inputs[name])
        arrays[f"in_{name}"] = array
        args[name] = nc.dram_tensor(f"in_{name}", array.shape, _mybir.dt.from_np(array.dtype), kind="ExternalInput").ap()
    out = nc.dram_tensor("out_0", (N, C), _mybir.dt.float32, kind="ExternalOutput").ap()
    build(nc, args, out)
    r = _run(nc, [arrays], core_ids=[0])
    return r.results[0]["out_0"]
```

```python
from contextlib import ExitStack

import numpy as np
import concourse.bass as bass
from concourse import mybir

F32 = mybir.dt.float32
BF16 = mybir.dt.bfloat16
I32 = mybir.dt.int32
U32 = mybir.dt.uint32
ALU = mybir.AluOpType
ACT = mybir.ActivationFunctionType
AX = mybir.AxisListType
ds = bass.ds

P = 128
N = 6250
E = 100000
C = 256
H = 4
CH = C // H
NT = (N + P - 1) // P
LAST = N - (NT - 1) * P
KT = 8
CE = KT * P
SLOTS = 3
NC = -(-E // CE)
FULL = E // CE
REST = (E - FULL * CE) // KT
GW = C + H
HW = C + 2 * H
MH = 8
MD = 64
MI = MH * MD
EPS = 1e-5
SLOPE = 0.2
NX = 16
FF = 512
A2 = 2 * N
XT = (A2 + NX * (P - 1)) // P
ROWS = XT * P
assert (E - FULL * CE) % KT == 0 and REST < P


def hold(eng, sem, value, tick):
    eng.wait_ge(sem, value)
    eng.sem_inc(tick, 1)


class Chain:

    def __init__(self, eng, sem):
        self.eng, self.sem, self.base, self.n = eng, sem, 0, 0

    def link(self, ins):
        self.n += 1
        ins.then_inc(self.sem, 1)
        self.eng.wait_ge(self.sem, self.base + self.n)

    def hold(self, ins, tick):
        self.n += 1
        ins.then_inc(self.sem, 1)
        hold(self.eng, self.sem, self.base + self.n, tick)

    def at(self, base):
        self.base, self.n = base, 0


def rows_of(i):
    return LAST if isinstance(i, int) and i == NT - 1 else P


def skewed(eng, n, period, head, tail, stages):
    most, least = max(o for o, _ in stages), min(o for o, _ in stages)
    start = head + most
    turns = max(0, n - tail + least - start) // period

    def whole(t):
        for o, step in stages:
            if 0 <= t - o < n:
                step(t - o, (t - o) % period, (t - o) // period)
    for t in range(start):
        whole(t)
    if turns:
        with eng.Fori(0, turns) as m:
            for r in range(period):
                for o, step in stages:
                    k = start + r - o
                    step(m * period + k, k % period, m + k // period)
    for t in range(start + turns * period, n + most):
        whole(t)


BUFS = 4


def tiles(eng, *stages):
    def told(step):
        return lambda i, q, u: step(i, q)
    skewed(eng, NT, BUFS, BUFS, 1, [(o, told(step)) for o, step in stages])


def uses(q, n=NT):
    return len(range(q, n, BUFS))


def later(i, n):
    return not isinstance(i, int) or i >= n


def build(nc, a, out):
    dram = {}

    def scratch(name, shape, dt=F32):
        dram[name] = nc.dram_tensor(name, shape, dt, kind="Internal").ap()
        return dram[name]

    srcp = scratch("srcp", (NC * CE,), I32)
    xnT_d = scratch("xnT_d", (NT, P, C))
    table = [scratch("table0", (NT * P, GW)), scratch("table1", (NT * P, GW))]
    dtab_d = scratch("dtab_d", ((NT + 2) * P, 3 * H), BF16)
    y_d = scratch("y_d", (NT * P, C))
    xf_d = scratch("xf_d", (NT * P, C))
    xs_d = scratch("xs_d", (ROWS, C))
    ys_d = scratch("ys_d", (ROWS, C))
    weights_in = nc.alloc_semaphore(name="weights_in")

    with ExitStack() as top:
        def sb(name, shape, dt=F32, ctx=top):
            return ctx.enter_context(nc.sbuf_tensor(name, shape, dt))

        def stage(program, *args):
            own = []

            def sem(name):
                own.append(nc.alloc_semaphore(name=name))
                return own[-1]
            program(nc, *args, sem)
            nc.clear_and_free_semaphores(own)
            nc.all_engine_barrier()

        ident = sb("ident", [P, P])
        ones = sb("ones", [P, P])
        eps = sb("eps", [P, 1])
        place = sb("place", [P, NT, 2], I32)
        share = sb("share", [P, NT, 2])
        expert = sb("expert", [1, XT], I32)
        hot = sb("pair_hot", [P, NT, 2, NX])
        w1 = sb("w1", [P, NX, 2, FF])

        with ExitStack() as gnn:
            identb = sb("identb", [P, P], BF16, gnn)
            iota = sb("iota", [P, P], BF16, gnn)
            distance = sb("distance", [P, 2 * P], F32, gnn)
            mixM = sb("mixM", [P, 2, C], F32, gnn)
            acc = sb("acc", [P, NT + 2, GW], F32, gnn)
            dtab = sb("dtab", [P, NT + 2, H], F32, gnn)
            dst_rel = sb("dst_rel", [P, NC * KT], F32, gnn)
            dst_r = sb("dst_r", [P, NC * KT], F32, gnn)
            offset = sb("offset", [P, NC], F32, gnn)
            first_node = sb("first_node", [1, NC], I32, gnn)
            window = sb("window", [1, NC], I32, gnn)
            window_tile = sb("window_tile", [1, NC], I32, gnn)
            passes = sb("passes", [1, 1], I32, gnn)
            cmax = sb("cmax", [P, H], F32, gnn)
            dsplit = sb("dsplit", [P, NT + 2, 3, H], BF16, gnn)
            edges = (identb, iota, distance, acc, cmax, dst_rel, dst_r, offset, first_node, window, window_tile, passes)
            stage(prepare_edges, a, srcp, ident, identb, ones, iota, distance, eps, dst_rel, offset, first_node, passes)
            stage(project_inputs, a, xnT_d, table[0], ident, ones, eps, acc, dtab, mixM)
            stage(self_loops, 0, ident, ones, acc, dtab, cmax, dsplit, dtab_d)
            stage(gat_edges, 0, srcp, table[0], dtab_d, *edges)
            stage(project_hidden, a, table[1], ident, acc, dtab, w1, weights_in)
            stage(self_loops, 1, ident, ones, acc, dtab, cmax, dsplit, dtab_d)
            stage(gat_edges, 1, srcp, table[1], dtab_d, *edges)
            stage(combine, a, xnT_d, y_d, xf_d, xs_d, ident, ones, eps, acc, mixM, hot, share)
        with ExitStack() as ffn:
            w2 = sb("w2", [P, NX, FF // P, C], F32, ffn)
            stage(order, ones, hot, place, expert)
            b1 = sb("b1", [P, NX, FF], F32, ffn)
            b2 = sb("b2", [P, NX, C], F32, ffn)
            stage(dispatch, a, xf_d, xs_d, place, w2, b1, b2, weights_in)
            stage(experts, xs_d, ys_d, ident, expert, w1, w2, b1, b2, weights_in)
        stage(finish, a, y_d, xf_d, ys_d, out, eps, place, share)
    nc.clear_and_free_semaphores([weights_in])


def prepare_edges(nc, a, srcp, ident, identb, ones, iota, distance, eps, dst_rel, offset, first_node, passes, sem):
    with ExitStack() as ctx:
        def sb(name, shape, dt=F32):
            return ctx.enter_context(nc.sbuf_tensor(name, shape, dt))

        iota_i = sb("iota_i", [P, 2 * P], I32)
        distance_i = sb("distance_i", [P, 2 * P], I32)
        zero_i = sb("zero_i", [P, KT], I32)
        dst_i = sb("dst_i", [P, NC * KT], I32)
        by_chunk_i = sb("by_chunk_i", [NC, CE], I32)
        low = sb("low", [NC, CE])
        high = sb("high", [NC, CE])
        ends = sb("ends", [P, 2])
        rows = sb("rows", [1, 2 * P])
        rows_i = sb("rows_i", [1, P], I32)
        tile_i = sb("tile_i", [1, P], I32)
        spread_row = sb("spread_row", [1, 2, NC])
        span = sb("span", [1, P])
        count = sb("count", [1, 1])
        count_i = sb("count_i", [1, 1], I32)
        base = sb("base", [P, NC])
        ps = ctx.enter_context(nc.psum_tensor("pe_ps", [P, 512], F32))
        ps2 = ctx.enter_context(nc.psum_tensor("pe_ps2", [P, 512], F32))
        s = {n: sem("e_" + n) for n in ("filled", "loaded", "stored", "consts", "steps", "turned", "rowed", "spread", "tiled", "zeroed")}
        block = ctx.enter_context(nc.Block())
        whole = a["dst"][0:FULL * CE].rearrange("(k p t) -> p k t", p=P, t=KT)
        part = a["dst"][FULL * CE:E].rearrange("(p t) -> p t", t=KT)

        @block.sync
        def _(sp):
            sp.dma_start(srcp[0:E].rearrange("(p f) -> p f", p=P // 4), a["src"].rearrange("(p f) -> p f", p=P // 4)).then_inc(s["stored"], 16)
            sp.wait_ge(s["filled"], 3)
            sp.dma_start(srcp[E:NC * CE].rearrange("(p t) -> p t", t=KT), zero_i[0:P - REST, :]).then_inc(s["stored"], 16)
            sp.dma_start(dst_i[:, 0:FULL * KT].rearrange("p (k t) -> p k t", t=KT), whole).then_inc(s["loaded"], 16)
            sp.dma_start(dst_i[0:REST, FULL * KT:NC * KT], part).then_inc(s["loaded"], 16)
            sp.dma_start(by_chunk_i[0:FULL, :], a["dst"][0:FULL * CE].rearrange("(k e) -> k e", e=CE)).then_inc(s["loaded"], 16)
            sp.dma_start(by_chunk_i[FULL:NC, 0:REST * KT], a["dst"][FULL * CE:E].rearrange("(k e) -> k e", k=1)).then_inc(s["loaded"], 16)
            sp.wait_ge(s["stored"], 32)

        @block.gpsimd
        def _(pool):
            pool.memset(ones[:], 1.0)
            pool.memset(eps[:], EPS)
            pool.memset(ident[:], 0.0).then_inc(s["zeroed"], 1)
            pool.iota(iota_i[:], pattern=[[1, 2 * P]], base=0, channel_multiplier=0)
            pool.iota(distance_i[:], pattern=[[1, 2 * P]], base=0, channel_multiplier=-1)
            pool.wait_ge(s["zeroed"], 1)
            pool.affine_select(out=ident[:], in_=ident[:], compare_op=ALU.not_equal, fill=1.0, base=0,
                               pattern=[[-1, P]], channel_multiplier=1).then_inc(s["consts"], 1)

        @block.vector
        def _(dve):
            chain = Chain(dve, s["steps"])
            dve.memset(zero_i[:], 0).then_inc(s["filled"], 1)
            dve.memset(dst_i[:], 1 << 20).then_inc(s["filled"], 1)
            dve.memset(by_chunk_i[:], 1 << 20).then_inc(s["filled"], 1)
            dve.wait_ge(s["consts"], 1)
            dve.tensor_copy(iota[:], iota_i[:, 0:P])
            dve.tensor_copy(distance[:], distance_i[:])
            dve.tensor_copy(identb[:], ident[:])
            dve.wait_ge(s["loaded"], 64)
            dve.tensor_copy(dst_rel[:], dst_i[:])
            dve.tensor_copy(low[:], by_chunk_i[:])
            chain.link(dve.memset(ends[:], 0.0))
            chain.link(dve.tensor_scalar(high[:], low[:], float(1 << 19), -float(1 << 20), ALU.is_ge, ALU.mult))
            chain.link(dve.tensor_tensor(high[:], high[:], low[:], ALU.add))
            chain.link(dve.tensor_reduce(ends[0:NC, 0:1], low[:], AX.X, ALU.min))
            dve.tensor_reduce(ends[0:NC, 1:2], high[:], AX.X, ALU.max).then_inc(s["tiled"], 1)
            dve.wait_ge(s["turned"], 1)
            chain.link(dve.tensor_copy(rows[:], ps[0:1, 0:2 * P]))
            chain.link(dve.tensor_copy(rows_i[:], rows[:, 0:P]))
            chain.link(dve.tensor_copy(first_node[:], rows_i[:, 0:NC]))
            chain.link(dve.tensor_tensor(span[:], rows[:, P:2 * P], rows[:, 0:P], ALU.subtract))
            chain.link(dve.tensor_reduce(count[:], span[:], AX.X, ALU.max))
            chain.link(dve.tensor_copy(count_i[:], count[:]))
            chain.link(dve.tensor_scalar(count_i[:], count_i[:], 7, None, ALU.arith_shift_right))
            chain.link(dve.tensor_scalar(passes[:], count_i[:], 1, None, ALU.add))
            chain.link(dve.tensor_scalar(tile_i[:], rows_i[:], P - 1, None, ALU.bitwise_and))
            chain.link(dve.tensor_copy(spread_row[:, 0, :], rows[:, 0:NC]))
            dve.tensor_copy(spread_row[:, 1, :], tile_i[:, 0:NC]).then_inc(s["rowed"], 1)
            dve.wait_ge(s["spread"], 1)
            chain.link(dve.tensor_copy(base[:], ps2[:, 0:NC]))
            dve.tensor_copy(offset[:], ps2[:, NC:2 * NC])
            rel = dst_rel[:].rearrange("p (k t) -> p k t", t=KT)
            chain.link(dve.tensor_tensor(rel, rel, base[:].rearrange("p (k t) -> p k t", t=1).to_broadcast([P, NC, KT]), ALU.subtract))

        @block.tensor
        def _(pe):
            pe.wait_ge(s["consts"], 1)
            pe.wait_ge(s["tiled"], 1)
            pe.transpose(ps[0:1, 0:P], ends[:, 0:1], ident[:])
            pe.transpose(ps[0:1, P:2 * P], ends[:, 1:2], ident[:]).then_inc(s["turned"], 1)
            pe.wait_ge(s["rowed"], 1)
            pe.matmul(ps2[:, 0:2 * NC], ones[0:1, :], spread_row[:].rearrange("o a k -> o (a k)"), start=True, stop=True).then_inc(s["spread"], 1)


def project_inputs(nc, a, xnT_d, table, ident, ones, eps, acc, dtab, mixM, sem):
    with ExitStack() as ctx:
        def sb(name, shape, dt=F32):
            return ctx.enter_context(nc.sbuf_tensor(name, shape, dt))

        def pb(name, shape):
            return ctx.enter_context(nc.psum_tensor(name, shape, F32))

        wext = sb("wext0", [P, 2, HW])
        att = sb("att0", [P, 2, C])
        attw = sb("attw0", [P, 2, C])
        wkv = sb("wkv", [P, 8, C])
        wkvT = sb("wkvT", [P, 2, 2 * MI])
        wmean = sb("wmean", [P, 2 * MH])
        wq = sb("wq", [P, 4, C])
        wout = sb("wout", [P, 2, MI])
        woutT = sb("woutT", [P, 4, C])
        dotsT = sb("dotsT", [P, 4, P])
        z = sb("zmix", [P, 4, C])
        x = sb("x_in", [P, BUFS, C])
        st = sb("st", [P, 2, 6])
        mv = sb("mv", [P, 2, 2])
        rs = sb("rs", [P, 2, 2])
        xn = sb("xn", [P, 2, C])
        xnT = sb("xnT", [P, BUFS, 2, P])
        sq = sb("sq", [P, 2 * MI])
        ss = sb("ss", [P, 3, 2 * MH])
        rkv = sb("rkv", [P, MH])
        ks = sb("ks", [P, 2, MI])
        vs = sb("vs", [P, 2, MI])
        psX = pb("psX", [P, 512])
        psH = pb("psH", [P, 512])
        psKV = pb("psKV", [P, 2, 2 * MI])
        psD = pb("psD", [P, 512])
        psW = pb("psW", [P, 512])
        loaded, steps, turned, moved = sem("i_loaded"), sem("i_steps"), sem("i_turned"), sem("i_moved")
        first_block = ExitStack()
        block = first_block.enter_context(nc.Block())

        @block.sync
        def _(sp):
            sp.dma_start(wext[:, :, 0:C], a["L0_gnn_W1"].rearrange("(k p) n -> p k n", p=P)).then_inc(loaded, 16)
            sp.dma_start(att[:, 0, :], a["L0_gnn_att_src1"].rearrange("(o h) c -> o (h c)", o=1).to_broadcast([P, C])).then_inc(loaded, 16)
            sp.dma_start(att[:, 1, :], a["L0_gnn_att_dst1"].rearrange("(o h) c -> o (h c)", o=1).to_broadcast([P, C])).then_inc(loaded, 16)
            sp.dma_start(wkv[:], a["L0_mix_Wqkv"][MI:3 * MI, :].rearrange("(k p) c -> p k c", p=P)).then_inc(loaded, 16)
            sp.dma_start(wq[:], a["L0_mix_Wqkv"][0:MI, :].rearrange("(k p) c -> p k c", p=P)).then_inc(loaded, 16)
            sp.dma_start(wout[:], a["L0_mix_Wout"].rearrange("(k p) c -> p k c", p=P)).then_inc(loaded, 16)

        @block.vector
        def _(dve):
            chain = Chain(dve, steps)
            dve.memset(acc[:, NT:NT + 2, :], 0.0)
            dve.memset(dtab[:, NT:NT + 2, :], 0.0)
            dve.memset(dotsT[:], 0.0)
            dve.wait_ge(loaded, 96)
            attention_columns(dve, chain, wext, att, attw)
            for g in range(6):
                dve.wait_ge(turned, g + 1)
                if g < 4:
                    kc, q = g // 2, g % 2
                    dve.tensor_copy(wkvT[:, kc, q * 512:(q + 1) * 512], psW[:, :]).then_inc(moved, 1)
                else:
                    dve.tensor_copy(woutT[:, :, (g - 4) * P:(g - 3) * P], psW[:, :].rearrange("p (k f) -> p k f", k=4)).then_inc(moved, 1)
            dve.wait_ge(moved, 6)
            for kc in range(2):
                w = wkvT[:, kc, :].rearrange("p (g d) -> p g d", d=MD)
                chain.link(dve.tensor_reduce(wmean[:], w, AX.X, ALU.add))
                chain.link(dve.tensor_scalar(wmean[:], wmean[:], 1.0 / MD, None, ALU.mult))
                chain.link(dve.tensor_tensor(w, w, wmean[:].rearrange("p (g d) -> p g d", d=1).to_broadcast([P, 2 * MH, MD]), ALU.subtract))

        @block.tensor
        def _(pe):
            pe.wait_ge(loaded, 96)
            for g in range(6):
                if g:
                    pe.wait_ge(moved, g)
                for j in range(4):
                    if g < 4:
                        kc, q = g // 2, g % 2
                        ins = pe.transpose(psW[:, j * P:(j + 1) * P], wkv[:, 4 * q + j, kc * P:(kc + 1) * P], ident[:])
                    else:
                        ins = pe.transpose(psW[:, j * P:(j + 1) * P], wout[:, g - 4, j * P:(j + 1) * P], ident[:])
                ins.then_inc(turned, 1)

        first_block.close()
        s = {n: sem("i_" + n) for n in ("x_in0", "x_in1", "x_in2", "x_in3", "xT_out0", "xT_out1", "xT_out2", "xT_out3", "xT_ps", "xT", "h_ps", "h_out",
                                        "h_stored", "kv_ps", "squared", "ks", "vs", "dots", "stats", "root", "xn", "kvsum", "kvroot",
                                        "first", "norm", "key", "end", "tick")}
        block2 = ctx.enter_context(nc.Block())

        @block2.sync
        def _(sp):
            def load(i, q):
                r = rows_of(i)
                if later(i, BUFS):
                    sp.wait_ge(s["xn"], i - BUFS + 1)
                sp.dma_start(x[0:r, q, :], a["x"][ds(i * P, r), :]).then_inc(s[f"x_in{q}"], 16)
            tiles(sp, (0, load))

        @block2.gpsimd
        def _(pool):
            def store_x(i, q):
                pool.wait_ge(s["xT"], i + 1)
                pool.dma_start(xnT_d[ds(i, 1), :, :].rearrange("o p f -> (o p) f"), xnT[:, q, :, :].rearrange("p k f -> p (k f)")).then_inc(s[f"xT_out{q}"], 16)

            def store_h(i, q):
                pool.wait_ge(s["h_out"], i * 2 + 2)
                pool.dma_start(table[ds(i * P, P), :], acc[:, ds(i, 1), :].rearrange("p o f -> p (o f)")).then_inc(s["h_stored"], 16)
            tiles(pool, (0, store_x), (0, store_h))
            for q in range(BUFS):
                pool.wait_ge(s[f"xT_out{q}"], 16 * uses(q))
            pool.wait_ge(s["h_stored"], 16 * NT)

        @block2.vector
        def _(dve):
            first, norm, key = Chain(dve, s["first"]), Chain(dve, s["norm"]), Chain(dve, s["key"])

            def stats(i, q):
                first.at(i)
                dve.wait_ge(s[f"x_in{q}"], (i - q) * 16 // BUFS + 16)
                first.hold(dve.bn_stats(st[:, q % 2, :], x[:, q, :]), s["tick"])
                dve.bn_aggr(mv[:, q % 2, :], st[:, q % 2, :]).then_inc(s["stats"], 1)

            def normalise(i, q):
                norm.at(i)
                dve.wait_ge(s["root"], i + 1)
                norm.link(dve.reciprocal(rs[:, q % 2, 1:2], rs[:, q % 2, 0:1]))
                if later(i, 2):
                    dve.wait_ge(s["xT_ps"], i - 1)
                dve.tensor_scalar(xn[:, q % 2, :], x[:, q, :], mv[:, q % 2, 0:1], rs[:, q % 2, 1:2], ALU.subtract, ALU.mult).then_inc(s["xn"], 1)

            def sums(i, q):
                dve.wait_ge(s["squared"], i + 1)
                dve.tensor_reduce(ss[:, 0, :], sq[:].rearrange("p (g d) -> p g d", d=MD), AX.X, ALU.add).then_inc(s["kvsum"], 1)

            def keys(i, q):
                key.at(i * 2)
                dve.wait_ge(s["kvroot"], i + 1)
                key.link(dve.reciprocal(ss[:, 2, :], ss[:, 1, :]))
                key.link(dve.tensor_tensor(rkv[:], ss[:, 2, 0:MH], ss[:, 2, MH:2 * MH], ALU.mult))
                if later(i, 2):
                    dve.wait_ge(s["dots"], i - 1)
                dve.tensor_tensor(ks[:, q % 2, :].rearrange("p (g d) -> p g d", d=MD), psKV[:, q % 2, 0:MI].rearrange("p (g d) -> p g d", d=MD),
                                  rkv[:].rearrange("p (g d) -> p g d", d=1).to_broadcast([P, MH, MD]), ALU.mult).then_inc(s["ks"], 1)
            tiles(dve, (3, keys), (1, normalise), (0, stats), (2, sums))
            dve.wait_ge(s["dots"], NT)
            for hp in range(4):
                for d in range(2):
                    last = dve.tensor_scalar(dotsT[d * MD:(d + 1) * MD, hp, d * MD:(d + 1) * MD], psD[d * MD:(d + 1) * MD, hp * P + d * MD:hp * P + (d + 1) * MD],
                                             1.0 / N, None, ALU.mult)
            last.then_inc(s["end"], 1)
            dve.wait_ge(s["end"], 2)
            dve.tensor_copy(z[:].rearrange("p k f -> p (k f)"), psKV[:, 0, :]).then_inc(s["end"], 1)
            dve.wait_ge(s["end"], 4)
            dve.tensor_copy(mixM[:].rearrange("p k f -> p (k f)"), psD[:, 0:2 * C])

        @block2.scalar
        def _(act):
            def project(i, q):
                act.wait_ge(s["h_ps"], i + 1)
                act.activation(acc[:, ds(i, 1), :].rearrange("p o f -> p (o f)"), psH[:, 0:GW], ACT.Copy).then_inc(s["h_out"], 1)
                act.activation(dtab[:, ds(i, 1), :].rearrange("p o f -> p (o f)"), psH[:, GW:HW], ACT.Copy).then_inc(s["h_out"], 1)

            def squares(i, q):
                act.wait_ge(s["kv_ps"], i + 1)
                if later(i, 1):
                    act.wait_ge(s["kvsum"], i)
                act.activation(sq[:], psKV[:, q % 2, :], ACT.Square).then_inc(s["squared"], 1)
                if later(i, 2):
                    act.wait_ge(s["dots"], i - 1)
                act.activation(vs[:, q % 2, :], psKV[:, q % 2, MI:2 * MI], ACT.Copy).then_inc(s["vs"], 1)

            def root(i, q):
                act.wait_ge(s["stats"], i + 1)
                act.activation(rs[:, q % 2, 0:1], mv[:, q % 2, 1:2], ACT.Sqrt, bias=eps[:, 0:1]).then_inc(s["root"], 1)

            def roots(i, q):
                act.wait_ge(s["kvsum"], i + 1)
                act.activation(ss[:, 1, :], ss[:, 0, :], ACT.Sqrt, bias=eps[:, 0:1], scale=1.0 / MD).then_inc(s["kvroot"], 1)

            def turned(i, q):
                act.wait_ge(s["xT_ps"], i + 1)
                if later(i, BUFS):
                    act.wait_ge(s[f"xT_out{q}"], (i - q) * 16 // BUFS)
                act.activation(xnT[:, q, :, :].rearrange("p k f -> p (k f)"), psX[:, 0:2 * P], ACT.Copy).then_inc(s["xT"], 1)
            tiles(act, (2, project), (0, root), (2, squares), (1, turned), (2, roots))

        @block2.tensor
        def _(pe):
            def project(i, q):
                pe.wait_ge(s["xT"], i + 1)
                if later(i, 1):
                    pe.wait_ge(s["h_out"], i * 2)
                for kc in range(2):
                    ins = pe.matmul(psH[:, 0:HW], xnT[:, q, kc, :], wext[:, kc, :], start=(kc == 0), stop=(kc == 1))
                ins.then_inc(s["h_ps"], 1)
                if later(i, 2):
                    pe.wait_ge(s["ks"], i - 1)
                    pe.wait_ge(s["vs"], i - 1)
                for half in range(2):
                    for kc in range(2):
                        ins = pe.matmul(psKV[:, q % 2, half * 512:(half + 1) * 512], xnT[:, q, kc, :], wkvT[:, kc, half * 512:(half + 1) * 512],
                                        start=(kc == 0), stop=(kc == 1))
                ins.then_inc(s["kv_ps"], 1)

            def turn(i, q):
                pe.wait_ge(s["xn"], i + 1)
                if later(i, 1):
                    pe.wait_ge(s["xT"], i)
                for kc in range(2):
                    ins = pe.transpose(psX[:, kc * P:(kc + 1) * P], xn[:, q % 2, kc * P:(kc + 1) * P], ident[:])
                ins.then_inc(s["xT_ps"], 1)

            def dots(i, q):
                pe.wait_ge(s["ks"], i + 1)
                pe.wait_ge(s["vs"], i + 1)
                r = rows_of(i)
                for hp in range(4):
                    ins = pe.matmul(psD[:, hp * P:(hp + 1) * P], vs[0:r, q % 2, hp * P:(hp + 1) * P], ks[0:r, q % 2, hp * P:(hp + 1) * P],
                                    start=(not later(i, 1) and hp == 0), stop=(r == LAST), skip_group_check=True)
                ins.then_inc(s["dots"], 1)
            tiles(pe, (2, project), (1, turn), (3, dots))
            pe.wait_ge(s["end"], 1)
            for hp in range(4):
                ins = pe.matmul(psKV[:, 0, hp * C:(hp + 1) * C], dotsT[:, hp, :], woutT[:, hp, :], start=True, stop=True)
            ins.then_inc(s["end"], 1)
            pe.wait_ge(s["end"], 3)
            for kc in range(2):
                for hp in range(4):
                    ins = pe.matmul(psD[:, kc * C:(kc + 1) * C], wq[:, hp, kc * P:(kc + 1) * P], z[:, hp, :], start=(hp == 0), stop=(hp == 3))
            ins.then_inc(s["end"], 1)


def attention_columns(dve, chain, wext, att, attw):
    for j in range(2):
        for kc in range(2):
            chain.link(dve.tensor_tensor(attw[:, kc, :], wext[:, kc, 0:C], att[:, j, :], ALU.mult))
            chain.link(dve.tensor_reduce(wext[:, kc, C + j * H:C + (j + 1) * H], attw[:, kc, :].rearrange("p (h c) -> p h c", h=H), AX.X, ALU.add))


def self_loops(nc, layer, ident, ones, acc, dtab, cmax, dsplit, dtab_d, sem):
    with ExitStack() as ctx:
        def sb(name, shape, dt=F32):
            return ctx.enter_context(nc.sbuf_tensor(f"{name}_{layer}", shape, dt))

        top = sb("sl_top", [P, H])
        head = sb("sl_head", [H, 1])
        diag = sb("sl_diag", [H, H])
        z = sb("sl_z", [P, NT, H])
        y = sb("sl_y", [P, NT, H])
        rest = sb("sl_rest", [P, NT + 2, H])
        ps = ctx.enter_context(nc.psum_tensor(f"sl_ps{layer}", [P, 512], F32))
        steps, topped, turned, diagonal, spread, logits, weights = (sem(f"sl_{n}{layer}") for n in (
            "steps", "topped", "turned", "diagonal", "spread", "logits", "weights"))
        split, stored = sem(f"sl_split{layer}"), sem(f"sl_stored{layer}")
        block = ctx.enter_context(nc.Block())

        @block.sync
        def _(sp):
            sp.wait_ge(split, 1)
            sp.dma_start(dtab_d.rearrange("(t p) f -> p t f", p=P), dsplit[:].rearrange("p t c h -> p t (c h)")).then_inc(stored, 16)
            sp.wait_ge(stored, 16)

        def wide(t):
            return t[:].rearrange("p (o h) -> p o h", o=1).to_broadcast([P, NT, H])

        @block.vector
        def _(dve):
            chain = Chain(dve, steps)
            chain.link(dve.tensor_reduce(top[:], acc[:, 0:NT - 1, C:GW].rearrange("p i h -> p h i"), AX.X, ALU.max))
            dve.tensor_tensor(top[0:LAST, :], top[0:LAST, :], acc[0:LAST, NT - 1, C:GW], ALU.max).then_inc(topped, 1)
            dve.wait_ge(turned, 1)
            chain.link(dve.tensor_reduce(head[:], ps[0:H, 0:P], AX.X, ALU.max))
            dve.tensor_scalar(diag[:], ident[0:H, 0:H], head[:, 0:1], None, ALU.mult).then_inc(diagonal, 1)
            dve.tensor_copy(dsplit[:, :, 0, :], dtab[:])
            chain.link(dve.tensor_tensor(z[:], acc[:, 0:NT, C:GW], dtab[:, 0:NT, :], ALU.add))
            chain.link(dve.tensor_tensor(rest[:], dtab[:], dsplit[:, :, 0, :], ALU.subtract))
            chain.link(dve.tensor_copy(dsplit[:, :, 1, :], rest[:]))
            chain.link(dve.tensor_tensor(rest[:], rest[:], dsplit[:, :, 1, :], ALU.subtract))
            dve.tensor_copy(dsplit[:, :, 2, :], rest[:]).then_inc(split, 1)
            dve.wait_ge(spread, 1)
            chain.link(dve.tensor_copy(cmax[:], ps[:, 256:256 + H]))
            chain.link(dve.tensor_tensor(y[:], dtab[:, 0:NT, :], wide(cmax), ALU.add))
            chain.link(dve.scalar_tensor_tensor(z[:], z[:], SLOPE, z[:], ALU.mult, ALU.max))
            chain.link(dve.scalar_tensor_tensor(y[:], y[:], SLOPE, y[:], ALU.mult, ALU.max))
            dve.tensor_tensor(z[:], z[:], y[:], ALU.subtract).then_inc(logits, 1)
            dve.wait_ge(weights, 1)
            for h in range(H):
                f = acc[:, 0:NT, h * CH:(h + 1) * CH]
                dve.tensor_tensor(f, f, acc[:, 0:NT, C + h:C + h + 1].to_broadcast([P, NT, CH]), ALU.mult)

        @block.scalar
        def _(act):
            act.wait_ge(logits, 1)
            act.activation(acc[:, 0:NT, C:GW], z[:], ACT.Exp).then_inc(weights, 1)

        @block.tensor
        def _(pe):
            pe.wait_ge(topped, 1)
            pe.transpose(ps[0:H, 0:P], top[:], ident[:]).then_inc(turned, 1)
            pe.wait_ge(diagonal, 1)
            pe.matmul(ps[:, 256:256 + H], ones[0:H, :], diag[:], start=True, stop=True).then_inc(spread, 1)


def gat_edges(nc, layer, srcp, table, dtab_d, identb, iota, distance, acc, cmax, dst_rel, dst_r, offset, first_node, window, window_tile, passes, sem):
    with ExitStack() as ctx:
        def sb(name, shape, dt=F32):
            return ctx.enter_context(nc.sbuf_tensor(f"{name}_{layer}", shape, dt))

        def pb(name, shape, dt=F32):
            return ctx.enter_context(nc.psum_tensor(f"{name}_{layer}", shape, dt))

        idx = sb("idx", [P, SLOTS, KT], I32)
        dwin = sb("dwin", [P, SLOTS, 3 * H], BF16)
        G = sb("gathered", [P, SLOTS, KT, GW])
        hot = sb("hot", [P, SLOTS, KT, P], BF16)
        hotf = sb("hotf", [P, SLOTS, KT, P])
        hotT = sb("hotT", [P, SLOTS, KT, P], BF16)
        shift = sb("shift", [P, SLOTS, 2 * P])
        win = sb("win", [P, GW])
        d = sb("d_e", [P, KT, H])
        z = sb("z_e", [P, KT, H])
        y = sb("y_e", [P, KT, H])
        t = sb("t_e", [P, KT, H])
        psT = pb("psT", [P, KT, P], BF16)
        psD = pb("psD_e", [P, KT, 3, H])
        psA = pb("psA_e", [P, 512])
        psB = pb("psB_e", [P, 2, 512])
        names = ("idx_in0", "idx_in1", "idx_in2", "d_in0", "d_in1", "d_in2", "g_in0", "g_in1", "g_in2", "hot", "turned", "hotT", "hotf", "targets", "shift",
                 "target_read", "logits", "weights", "scaled", "added", "win", "shifted", "acc", "pass", "vsteps", "tick")
        s = {n: sem(f"g{layer}_{n}") for n in names}
        block = ctx.enter_context(nc.Block())

        def chunks(eng, begin, end, *stages):
            rounds = eng.value_load(passes[0:1, 0:1], min_val=1, max_val=NT)
            with eng.Fori(0, rounds) as r:
                def told(step):
                    return lambda c, q, u: step(r * NC + c, c, q, r * len(range(q, NC, SLOTS)) + u)
                begin(r)
                skewed(eng, NC, SLOTS, 0, 0, [(o, told(step)) for o, step in stages])
                end(r)

        def nothing(r):
            pass

        def new_pass(eng):
            return lambda r: hold(eng, s["pass"], r * 3 + 3, s["tick"])

        @block.sync
        def _(sp):
            def load(g, c, q, use):
                node = sp.value_load(window[0:1, ds(c, 1)], min_val=0, max_val=NT * P)
                sp.wait_ge(s["logits"], g + 1)
                sp.dma_start(idx[:, q, :], srcp[ds(c * CE, CE)].rearrange("(p t) -> p t", t=KT)).then_inc(s[f"idx_in{q}"], 16)
                sp.dma_start(dwin[:, q, :], dtab_d[ds(node, P), :]).then_inc(s[f"d_in{q}"], 16)
            chunks(sp, new_pass(sp), nothing, (0, load))

        @block.gpsimd
        def _(pool):
            def gather(g, c, q, use):
                pool.wait_ge(s[f"idx_in{q}"], 16 * use + 16)
                hold(pool, s["added"], g + 1, s["tick"])
                for k in range(KT):
                    pool.indirect_dma_start(out=G[:, q, k, :], out_offset=None, in_=table,
                                            in_offset=bass.IndirectOffsetOnAxis(ap=idx[:, q, k:k + 1], axis=0)).then_inc(s[f"g_in{q}"], 16)
            chunks(pool, nothing, nothing, (0, gather))

        @block.vector
        def _(dve):
            dve.sem_inc(s["logits"], SLOTS)
            dve.sem_inc(s["target_read"], 1)
            dve.sem_inc(s["acc"], 1)
            dve.tensor_copy(dst_r[:], dst_rel[:]).then_inc(s["pass"], 1)
            dve.tensor_copy(window[:], first_node[:]).then_inc(s["pass"], 1)
            dve.tensor_scalar(window_tile[:], first_node[:], 7, None, ALU.arith_shift_right).then_inc(s["pass"], 1)
            chain = Chain(dve, s["vsteps"])
            STEPS = 4

            def one_hot(g, c, q, use):
                for k in range(KT):
                    dve.tensor_scalar(hot[:, q, k, :], iota[:], dst_r[:, ds(c * KT + k, 1)], None, ALU.is_equal).then_inc(s["hot"], 1)

            def weigh(g, c, q, use):
                chain.at(g * STEPS)
                dve.tensor_scalar(shift[:, q, :], distance[:], offset[:, ds(c, 1)], None, ALU.is_equal).then_inc(s["shift"], 1)
                dve.wait_ge(s["targets"], g + 1)
                dve.tensor_reduce(d[:], psD[:].rearrange("p k c h -> p k h c"), AX.X, ALU.add).then_inc(s["target_read"], 1)
                dve.wait_ge(s["target_read"], g + 2)
                chain.link(dve.tensor_tensor(y[:], d[:], cmax[:].rearrange("p (o h) -> p o h", o=1).to_broadcast([P, KT, H]), ALU.add))
                chain.link(dve.scalar_tensor_tensor(y[:], y[:], SLOPE, y[:], ALU.mult, ALU.max))
                dve.wait_ge(s[f"g_in{q}"], 16 * KT * use + 16 * KT)
                chain.link(dve.tensor_tensor(z[:], d[:], G[:, q, :, C:GW], ALU.add))
                chain.link(dve.scalar_tensor_tensor(z[:], z[:], SLOPE, z[:], ALU.mult, ALU.max))
                dve.tensor_tensor(t[:], z[:], y[:], ALU.subtract).then_inc(s["logits"], 1)
                dve.wait_ge(s["weights"], g + 1)
                f = G[:, q, :, 0:C].rearrange("p k (h c) -> p k h c", h=H)
                w = G[:, q, :, C:GW].rearrange("p k (h c) -> p k h c", c=1).to_broadcast([P, KT, H, CH])
                dve.tensor_tensor(f, f, w, ALU.mult).then_inc(s["scaled"], 1)
                assert chain.n == STEPS

            def gain(g, c, q, use):
                first = dve.value_load(window_tile[0:1, ds(c, 1)], min_val=0, max_val=NT)
                dve.wait_ge(s["acc"], g + 1)
                dve.wait_ge(s["shifted"], g + 1)
                dve.tensor_tensor(acc[:, ds(first, 2), :], acc[:, ds(first, 2), :], psB[:, :, 0:GW], ALU.add).then_inc(s["acc"], 1)

            def next_pass(r):
                dve.wait_ge(s["acc"], r * NC + NC + 1)
                dve.tensor_scalar(dst_r[:], dst_r[:], -float(P), None, ALU.add).then_inc(s["pass"], 1)
                dve.tensor_scalar(window[:], window[:], P, NT * P, ALU.add, ALU.min).then_inc(s["pass"], 1)
                dve.wait_ge(s["pass"], r * 3 + 5)
                dve.tensor_scalar(window_tile[:], window[:], 7, None, ALU.arith_shift_right).then_inc(s["pass"], 1)
            chunks(dve, new_pass(dve), next_pass, (0, one_hot), (1, weigh), (3, gain))

        @block.scalar
        def _(act):
            act.sem_inc(s["hotT"], 1)

            def floats(g, c, q, use):
                act.wait_ge(s["hot"], g * KT + KT)
                act.wait_ge(s["added"], g + 1)
                act.activation(hotf[:, q, :, :], hot[:, q, :, :], ACT.Copy).then_inc(s["hotf"], 1)

            def turned(g, c, q, use):
                act.wait_ge(s["turned"], g + 1)
                act.activation(hotT[:, q, :, :], psT[:], ACT.Copy).then_inc(s["hotT"], 1)

            def exps(g, c, q, use):
                act.wait_ge(s["logits"], g + 1 + SLOTS)
                act.activation(G[:, q, :, C:GW], t[:], ACT.Exp).then_inc(s["weights"], 1)

            def windows(g, c, q, use):
                act.wait_ge(s["added"], g + 1 + SLOTS)
                act.activation(win[:], psA[:, 0:GW], ACT.Copy).then_inc(s["win"], 1)
            chunks(act, nothing, nothing, (3, windows), (0, floats), (0, turned), (1, exps))

        @block.tensor
        def _(pe):
            pe.sem_inc(s["added"], SLOTS)

            def targets(g, c, q, use):
                pe.wait_ge(s[f"d_in{q}"], 16 * use + 16)
                pe.wait_ge(s["hotT"], g + 2)
                pe.wait_ge(s["target_read"], g + 1)
                for k in range(KT):
                    ins = pe.matmul(psD[:, k, :, :].rearrange("p c h -> p (c h)"), hotT[:, q, k, :], dwin[:, q, :], start=True, stop=True)
                ins.then_inc(s["targets"], 1)

            def turn(g, c, q, use):
                pe.wait_ge(s["hot"], g * KT + KT)
                pe.wait_ge(s["hotT"], g + 1)
                for k in range(KT):
                    ins = pe.transpose(psT[:, k, :], hot[:, q, k, :], identb[:])
                ins.then_inc(s["turned"], 1)

            def shifts(g, c, q, use):
                pe.wait_ge(s["shift"], g + 1)
                pe.wait_ge(s["win"], g + 1)
                pe.wait_ge(s["acc"], g + 1)
                for j in range(2):
                    ins = pe.matmul(psB[:, j, 0:GW], shift[:, q, j * P:(j + 1) * P], win[:], start=True, stop=True)
                ins.then_inc(s["shifted"], 1)

            def add(g, c, q, use):
                pe.wait_ge(s["hotf"], g + 1)
                pe.wait_ge(s["scaled"], g + 1)
                for k in range(KT):
                    ins = pe.matmul(psA[:, 0:GW], hotf[:, q, k, :], G[:, q, k, :], start=(k == 0), stop=(k == KT - 1))
                ins.then_inc(s["added"], 1)
            chunks(pe, nothing, nothing, (1, targets), (0, turn), (3, shifts), (2, add))


def project_hidden(nc, a, table, ident, acc, dtab, w1, weights_in, sem):
    with ExitStack() as ctx:
        def sb(name, shape, dt=F32):
            return ctx.enter_context(nc.sbuf_tensor(name, shape, dt))

        wext = sb("wext1", [P, 2, HW])
        att = sb("att1", [P, 2, C])
        attw = sb("attw1", [P, 2, C])
        bias = sb("bias1", [P, 2])
        rden = sb("rden1", [P, NT, H])
        h = sb("h1", [P, 2, C])
        hT = sb("hT1", [P, 2, 2, P])
        psX = ctx.enter_context(nc.psum_tensor("psX1", [P, 2, 512], F32))
        psH = ctx.enter_context(nc.psum_tensor("psH1", [P, 2, 512], F32))
        s = {n: sem("h_" + n) for n in ("loaded", "steps", "hidden", "turned", "relu", "projected", "out", "stored")}
        block = ctx.enter_context(nc.Block())

        @block.sync
        def _(sp):
            sp.dma_start(wext[:, :, 0:C], a["L0_gnn_W2"].rearrange("(k p) n -> p k n", p=P)).then_inc(s["loaded"], 16)
            sp.dma_start(att[:, 0, :], a["L0_gnn_att_src2"].rearrange("(o h) c -> o (h c)", o=1).to_broadcast([P, C])).then_inc(s["loaded"], 16)
            sp.dma_start(att[:, 1, :], a["L0_gnn_att_dst2"].rearrange("(o h) c -> o (h c)", o=1).to_broadcast([P, C])).then_inc(s["loaded"], 16)
            for kc in range(2):
                sp.dma_start(bias[:, kc:kc + 1], a["L0_gnn_b1"][kc * P:(kc + 1) * P].rearrange("(p o) -> p o", o=1)).then_inc(s["loaded"], 16)

            def store(i, q):
                sp.wait_ge(s["out"], i * 2 + 2)
                sp.dma_start(table[ds(i * P, P), :], acc[:, ds(i, 1), :].rearrange("p o f -> p (o f)")).then_inc(s["stored"], 16)
            tiles(sp, (0, store))
            sp.wait_ge(s["stored"], 16 * NT)

        @block.vector
        def _(dve):
            chain = Chain(dve, s["steps"])
            dve.wait_ge(s["loaded"], 80)
            attention_columns(dve, chain, wext, att, attw)
            chain.link(dve.reciprocal(rden[:], acc[:, 0:NT, C:GW]))

            def scale(i, q):
                if later(i, 2):
                    dve.wait_ge(s["turned"], i - 1)
                dve.tensor_tensor(h[:, q % 2, :].rearrange("p (h c) -> p h c", h=H), acc[:, ds(i, 1), 0:C].rearrange("p o (h c) -> p (o h) c", h=H),
                                  rden[:, ds(i, 1), :].rearrange("p o (h c) -> p (o h) c", c=1).to_broadcast([P, H, CH]), ALU.mult).then_inc(s["hidden"], 1)
            tiles(dve, (0, scale))

        @block.scalar
        def _(act):
            for e in range(0, NX, 4):
                act.dma_start(w1[:, e:e + 4, :, :], a["L0_ffn_w1"][e:e + 4].rearrange("e (k p) f -> p e k f", p=P)).then_inc(weights_in, 16)
            act.wait_ge(s["loaded"], 80)

            def relu(i, q):
                act.wait_ge(s["turned"], i + 1)
                if later(i, 2):
                    act.wait_ge(s["projected"], i - 1)
                for kc in range(2):
                    act.activation(hT[:, q % 2, kc, :], psX[:, q % 2, kc * P:(kc + 1) * P], ACT.Relu, bias=bias[:, kc:kc + 1]).then_inc(s["relu"], 1)

            def copies(i, q):
                act.wait_ge(s["projected"], i + 1)
                act.activation(acc[:, ds(i, 1), :].rearrange("p o f -> p (o f)"), psH[:, q % 2, 0:GW], ACT.Copy).then_inc(s["out"], 1)
                act.activation(dtab[:, ds(i, 1), :].rearrange("p o f -> p (o f)"), psH[:, q % 2, GW:HW], ACT.Copy).then_inc(s["out"], 1)
            tiles(act, (1, copies), (0, relu))

        @block.tensor
        def _(pe):
            def turn(i, q):
                pe.wait_ge(s["hidden"], i + 1)
                if later(i, 2):
                    pe.wait_ge(s["relu"], i * 2 - 2)
                for kc in range(2):
                    ins = pe.transpose(psX[:, q % 2, kc * P:(kc + 1) * P], h[:, q % 2, kc * P:(kc + 1) * P], ident[:])
                ins.then_inc(s["turned"], 1)

            def project(i, q):
                pe.wait_ge(s["relu"], i * 2 + 2)
                if later(i, 2):
                    pe.wait_ge(s["out"], i * 2 - 2)
                for kc in range(2):
                    ins = pe.matmul(psH[:, q % 2, 0:HW], hT[:, q % 2, kc, :], wext[:, kc, :], start=(kc == 0), stop=(kc == 1))
                ins.then_inc(s["projected"], 1)
            tiles(pe, (0, turn), (1, project))


def combine(nc, a, xnT_d, y_d, xf_d, xs_d, ident, ones, eps, acc, mixM, hot, share, sem):
    with ExitStack() as ctx:
        def sb(name, shape, dt=F32):
            return ctx.enter_context(nc.sbuf_tensor(name, shape, dt))

        bias = sb("cbias", [2, C])
        beta = sb("cbeta", [P, C])
        gate = sb("gate", [P, 2, NX])
        gbias = sb("gbias", [1, NX])
        zero = sb("zero_rows", [P, C])
        x = sb("cx", [P, BUFS, C])
        xnT = sb("cxnT", [P, BUFS, 2, P])
        rden = sb("crden", [P, NT, H])
        gat = sb("cgat", [P, 2, C])
        y = sb("cy", [P, 2, C])
        yb = sb("cyb", [P, BUFS, C])
        st = sb("cst", [P, 2, 6])
        mv = sb("cmv", [P, 2, 2])
        rs = sb("crs", [P, 2, 2])
        xf = sb("cxf", [P, BUFS, C])
        xfT = sb("cxfT", [P, 2, 2, P])
        logits = sb("logits", [P, NT, NX])
        masked = sb("masked", [P, NT, NX])
        number_i = sb("number_i", [P, NX], I32)
        number = sb("number", [P, NX])
        top = sb("top", [P, NT, 2])
        which = sb("which", [P, NT, 2])
        gap = sb("gap", [P, NT])
        one = sb("one", [P, NT])
        ps = ctx.enter_context(nc.psum_tensor("cps", [P, 2, 512], F32))
        psT = ctx.enter_context(nc.psum_tensor("cpsT", [P, 2, 512], F32))
        psG = ctx.enter_context(nc.psum_tensor("cpsG", [P, 2, 512], F32))
        s = {n: sem("c_" + n) for n in ("loaded", "steps", "x0", "x1", "x2", "x3", "mixed", "gat", "y", "yb", "stored0", "stored1", "stored2", "stored3",
                                        "first", "norm", "stats", "root", "xf", "xf_out0", "xf_out1", "xf_out2", "xf_out3", "turned", "xfT",
                                        "gated", "logits", "zero", "cleared", "gap", "exp", "tick")}
        block = ctx.enter_context(nc.Block())

        @block.sync
        def _(sp):
            sp.dma_start(bias[0:1, :], a["L0_gnn_b2"].rearrange("(o c) -> o c", o=1)).then_inc(s["loaded"], 16)
            sp.dma_start(bias[1:2, :], a["L0_mix_bout"].rearrange("(o c) -> o c", o=1)).then_inc(s["loaded"], 16)
            sp.dma_start(beta[:], a["L0_ffn_beta"].rearrange("(o c) -> o c", o=1).to_broadcast([P, C])).then_inc(s["loaded"], 16)
            sp.dma_start(gate[:], a["L0_ffn_gate_w"].rearrange("(k p) e -> p k e", p=P)).then_inc(s["loaded"], 16)
            sp.dma_start(gbias[:], a["L0_ffn_gate_b"].rearrange("(o e) -> o e", o=1)).then_inc(s["loaded"], 16)

            def load(i, q):
                r = rows_of(i)
                if later(i, BUFS):
                    sp.wait_ge(s["gat"], i - BUFS + 1)
                    sp.wait_ge(s["mixed"], i - BUFS + 1)
                sp.dma_start(x[0:r, q, :], a["x"][ds(i * P, r), :]).then_inc(s[f"x{q}"], 16)
                sp.dma_start(xnT[:, q, :, :].rearrange("p k f -> p (k f)"), xnT_d[ds(i, 1), :, :].rearrange("o p f -> (o p) f")).then_inc(s[f"x{q}"], 16)

            def store(i, q):
                sp.wait_ge(s["yb"], i + 1)
                sp.dma_start(y_d[ds(i * P, P), :], yb[:, q, :]).then_inc(s[f"stored{q}"], 16)
                sp.wait_ge(s["xf"], i + 1)
                sp.dma_start(xf_d[ds(i * P, P), :], xf[:, q, :]).then_inc(s[f"xf_out{q}"], 16)
            tiles(sp, (0, load), (3, store))
            sp.wait_ge(s["zero"], 1)
            sp.dma_start(xs_d.rearrange("(t p) c -> p t c", p=P), zero[:].rearrange("p (o c) -> p o c", o=1).to_broadcast([P, XT, C])).then_inc(s["cleared"], 16)
            sp.wait_ge(s["cleared"], 16)
            for q in range(BUFS):
                sp.wait_ge(s[f"stored{q}"], 16 * uses(q))
                sp.wait_ge(s[f"xf_out{q}"], 16 * uses(q))

        @block.tensor
        def _(pe):
            pe.wait_ge(s["loaded"], 80)

            def mix(i, q):
                pe.wait_ge(s[f"x{q}"], (i - q) * 8 + 32)
                if later(i, 2):
                    pe.wait_ge(s["y"], i - 1)
                for kc in range(2):
                    pe.matmul(ps[:, q % 2, 0:C], xnT[:, q, kc, :], mixM[:, kc, :], start=(kc == 0), stop=False)
                pe.matmul(ps[:, q % 2, 0:C], ones[0:2, :], bias[:], start=False, stop=True).then_inc(s["mixed"], 1)

            def turn(i, q):
                pe.wait_ge(s["xf"], i + 1)
                if later(i, 2):
                    pe.wait_ge(s["xfT"], i - 1)
                for kc in range(2):
                    ins = pe.transpose(psT[:, q % 2, kc * P:(kc + 1) * P], xf[:, q, kc * P:(kc + 1) * P], ident[:])
                ins.then_inc(s["turned"], 1)

            def gates(i, q):
                pe.wait_ge(s["xfT"], i + 1)
                if later(i, 2):
                    pe.wait_ge(s["logits"], i - 1)
                for kc in range(2):
                    pe.matmul(psG[:, q % 2, 0:NX], xfT[:, q % 2, kc, :], gate[:, kc, :], start=(kc == 0), stop=False)
                pe.matmul(psG[:, q % 2, 0:NX], ones[0:1, :], gbias[:], start=False, stop=True).then_inc(s["gated"], 1)
            tiles(pe, (0, mix), (3, gates), (2, turn))

        @block.gpsimd
        def _(pool):
            pool.memset(zero[:], 0.0).then_inc(s["zero"], 1)
            pool.iota(number_i[:], pattern=[[1, NX]], base=0, channel_multiplier=0).then_inc(s["zero"], 1)
            pool.wait_ge(s["loaded"], 80)

            def with_beta(i, q):
                pool.wait_ge(s["y"], i + 1)
                if later(i, BUFS):
                    pool.wait_ge(s[f"stored{q}"], (i - q) * 4)
                pool.tensor_tensor(yb[:, q, :], y[:, q % 2, :], beta[:], ALU.add).then_inc(s["yb"], 1)
            tiles(pool, (1, with_beta))

        @block.vector
        def _(dve):
            chain, first, norm = Chain(dve, s["steps"]), Chain(dve, s["first"]), Chain(dve, s["norm"])
            dve.wait_ge(s["zero"], 2)
            chain.link(dve.tensor_copy(number[:], number_i[:]))
            chain.link(dve.reciprocal(rden[:], acc[:, 0:NT, C:GW]))

            def add(i, q):
                first.at(i * 2)
                first.link(dve.tensor_tensor(gat[:, q % 2, :].rearrange("p (h c) -> p h c", h=H), acc[:, ds(i, 1), 0:C].rearrange("p o (h c) -> p (o h) c", h=H),
                                             rden[:, ds(i, 1), :].rearrange("p o (h c) -> p (o h) c", c=1).to_broadcast([P, H, CH]), ALU.mult))
                dve.wait_ge(s[f"x{q}"], (i - q) * 8 + 32)
                dve.tensor_tensor(gat[:, q % 2, :], gat[:, q % 2, :], x[:, q, :], ALU.add).then_inc(s["gat"], 1)
                dve.wait_ge(s["mixed"], i + 1)
                dve.wait_ge(s["gat"], i + 1)
                if later(i, 2):
                    dve.wait_ge(s["xf"], i - 1)
                    dve.wait_ge(s["yb"], i - 1)
                dve.tensor_tensor(y[:, q % 2, :], gat[:, q % 2, :], ps[:, q % 2, 0:C], ALU.add).then_inc(s["y"], 1)
                hold(dve, s["y"], i + 1, s["tick"])
                first.hold(dve.bn_stats(st[:, q % 2, :], y[:, q % 2, :]), s["tick"])
                dve.bn_aggr(mv[:, q % 2, :], st[:, q % 2, :]).then_inc(s["stats"], 1)

            def normalise(i, q):
                norm.at(i)
                dve.wait_ge(s["root"], i + 1)
                norm.link(dve.reciprocal(rs[:, q % 2, 1:2], rs[:, q % 2, 0:1]))
                if later(i, BUFS):
                    dve.wait_ge(s["turned"], i - BUFS + 1)
                    dve.wait_ge(s[f"xf_out{q}"], (i - q) * 4)
                dve.tensor_scalar(xf[:, q, :], y[:, q % 2, :], mv[:, q % 2, 0:1], rs[:, q % 2, 1:2], ALU.subtract, ALU.mult).then_inc(s["xf"], 1)
            tiles(dve, (2, normalise), (1, add))
            dve.wait_ge(s["logits"], NT)
            wide = number[:].rearrange("p (t e) -> p t e", t=1).to_broadcast([P, NT, NX])
            for k in range(2):
                l = masked if k else logits
                h = hot[:, :, k, :]
                chain.link(dve.tensor_reduce(top[:, :, k], l[:], AX.X, ALU.max))
                chain.link(dve.tensor_tensor(h, l[:], top[:, :, k:k + 1].to_broadcast([P, NT, NX]), ALU.not_equal))
                chain.link(dve.scalar_tensor_tensor(h, h, float(NX), wide, ALU.mult, ALU.add))
                chain.link(dve.tensor_reduce(which[:, :, k], h, AX.X, ALU.min))
                chain.link(dve.tensor_tensor(h, wide, which[:, :, k:k + 1].to_broadcast([P, NT, NX]), ALU.is_equal))
                if k == 0:
                    chain.link(dve.scalar_tensor_tensor(masked[:], h, -3e38, logits[:], ALU.mult, ALU.add))
            dve.tensor_tensor(gap[:], top[:, :, 1], top[:, :, 0], ALU.subtract).then_inc(s["gap"], 1)
            dve.wait_ge(s["exp"], 1)
            chain.link(dve.tensor_scalar(one[:], gap[:], 1.0, None, ALU.add))
            chain.link(dve.reciprocal(share[:, :, 0], one[:]))
            chain.link(dve.tensor_tensor(share[:, :, 1], share[:, :, 0], gap[:], ALU.mult))

        @block.scalar
        def _(act):
            def root(i, q):
                act.wait_ge(s["stats"], i + 1)
                act.activation(rs[:, q % 2, 0:1], mv[:, q % 2, 1:2], ACT.Sqrt, bias=eps[:, 0:1]).then_inc(s["root"], 1)

            def turned(i, q):
                act.wait_ge(s["turned"], i + 1)
                if later(i, 2):
                    act.wait_ge(s["gated"], i - 1)
                act.activation(xfT[:, q % 2, :, :].rearrange("p k f -> p (k f)"), psT[:, q % 2, 0:2 * P], ACT.Copy).then_inc(s["xfT"], 1)

            def gates(i, q):
                act.wait_ge(s["gated"], i + 1)
                act.activation(logits[:, ds(i, 1), :].rearrange("p o f -> p (o f)"), psG[:, q % 2, 0:NX], ACT.Copy).then_inc(s["logits"], 1)
            tiles(act, (3, gates), (1, root), (2, turned))
            act.wait_ge(s["gap"], 1)
            act.activation(gap[:], gap[:], ACT.Exp).then_inc(s["exp"], 1)


def order(nc, ones, hot, place, expert, sem):
    with ExitStack() as ctx:
        def sb(name, shape, dt=F32):
            return ctx.enter_context(nc.sbuf_tensor(name, shape, dt))

        before = sb("before", [P, P])
        both = sb("both", [P, NT, NX])
        rank = sb("rank", [P, NT, NX])
        total = sb("total", [P, NX, NT])
        carry = sb("carry", [P, NX, NT])
        keep = sb("keep", [P, NX, NT])
        count = sb("xcount", [P, NX])
        count_i = sb("xcount_i", [P, NX], I32)
        ntiles = sb("ntiles", [P, NX])
        upto = sb("upto", [P, NX])
        first = sb("xfirst", [P, NX])
        picked = sb("picked", [P, NT, NX])
        row = sb("row", [P, NT, 2])
        numbers_i = sb("numbers_i", [1, XT], I32)
        numbers = sb("numbers", [1, XT])
        past = sb("past", [1, XT, NX])
        owner = sb("owner", [1, XT])
        ps = [ctx.enter_context(nc.psum_tensor(f"ops{n}", [P, 512], F32)) for n in range(4)]
        s = {n: sem("o_" + n) for n in ("consts", "steps", "both", "ranked", "pads")}
        block = ctx.enter_context(nc.Block())
        HALF = (NT + 1) // 2
        parts = ((0, HALF), (HALF, NT))

        @block.gpsimd
        def _(pool):
            pool.memset(before[:], 1.0).then_inc(s["pads"], 1)
            pool.iota(numbers_i[:], pattern=[[1, XT]], base=0, channel_multiplier=0).then_inc(s["consts"], 1)
            pool.wait_ge(s["pads"], 1)
            pool.affine_select(out=before[:], in_=before[:], compare_op=ALU.is_gt, fill=0.0, base=0,
                               pattern=[[1, P]], channel_multiplier=-1).then_inc(s["consts"], 1)

        @block.vector
        def _(dve):
            chain = Chain(dve, s["steps"])
            dve.wait_ge(s["consts"], 2)
            chain.link(dve.tensor_copy(numbers[:], numbers_i[:]))
            end = hot[:, NT - 1, :, :].rearrange("p s e -> p (s e)")
            chain.link(dve.tensor_scalar(end, end, before[:, LAST:LAST + 1], None, ALU.mult))
            chain.link(dve.tensor_tensor(both[:], hot[:, :, 0, :], hot[:, :, 1, :], ALU.add))
            chain.link(dve.memset(keep[:], 1.0))
            dve.memset(keep[:, :, 0], 0.0).then_inc(s["both"], 1)
            dve.wait_ge(s["ranked"], 1)
            for n, (lo, hi) in enumerate(parts):
                w = (hi - lo) * NX
                chain.link(dve.tensor_copy(rank[:, lo:hi, :].rearrange("p t e -> p (t e)"), ps[n][:, 0:w]))
                chain.link(dve.tensor_copy(total[:, :, lo:hi].rearrange("p e t -> p t e"), ps[2 + n][:, 0:w].rearrange("p (t e) -> p t e", e=NX)))
            chain.link(dve.tensor_tensor_scan(carry[:].rearrange("p e t -> p (e t)"), keep[:].rearrange("p e t -> p (e t)"),
                                              total[:].rearrange("p e t -> p (e t)"), 0.0, ALU.mult, ALU.add))
            chain.link(dve.tensor_scalar(count[:], carry[:, :, NT - 1], float(P - 1), None, ALU.add))
            chain.link(dve.tensor_tensor(carry[:], carry[:], total[:], ALU.subtract))
            chain.link(dve.tensor_copy(count_i[:], count[:]))
            chain.link(dve.tensor_scalar(count_i[:], count_i[:], 7, None, ALU.arith_shift_right))
            chain.link(dve.tensor_copy(ntiles[:], count_i[:]))
            chain.link(dve.memset(first[:], 1.0))
            chain.link(dve.tensor_tensor_scan(upto[:], first[:], ntiles[:], 0.0, ALU.mult, ALU.add))
            chain.link(dve.tensor_tensor(first[:], upto[:], ntiles[:], ALU.subtract))
            chain.link(dve.tensor_scalar(first[:], first[:], float(P), None, ALU.mult))
            chain.link(dve.tensor_tensor(rank[:], rank[:], carry[:].rearrange("p e t -> p t e"), ALU.add))
            chain.link(dve.tensor_tensor(rank[:], rank[:], first[:].rearrange("p (o e) -> p o e", o=1).to_broadcast([P, NT, NX]), ALU.add))
            for k in range(2):
                chain.link(dve.tensor_tensor(picked[:], rank[:], hot[:, :, k, :], ALU.mult))
                chain.link(dve.tensor_reduce(row[:, :, k], picked[:], AX.X, ALU.add))
            chain.link(dve.tensor_copy(place[:], row[:]))
            chain.link(dve.tensor_tensor(past[:], numbers[:].rearrange("o (t e) -> o t e", e=1).to_broadcast([1, XT, NX]),
                                         upto[0:1, :].rearrange("o (t e) -> o t e", t=1).to_broadcast([1, XT, NX]), ALU.is_ge))
            chain.link(dve.tensor_reduce(owner[:], past[:], AX.X, ALU.add))
            chain.link(dve.tensor_scalar(owner[:], owner[:], float(NX - 1), None, ALU.min))
            chain.link(dve.tensor_copy(expert[:], owner[:]))

        @block.tensor
        def _(pe):
            pe.wait_ge(s["consts"], 2)
            pe.wait_ge(s["both"], 1)
            for n, (lo, hi) in enumerate(parts):
                w = (hi - lo) * NX
                rhs = both[:, lo:hi, :].rearrange("p t e -> p (t e)")
                pe.matmul(ps[n][:, 0:w], before[:], rhs, start=True, stop=True)
                ins = pe.matmul(ps[2 + n][:, 0:w], ones[:], rhs, start=True, stop=True)
            ins.then_inc(s["ranked"], 1)


def dispatch(nc, a, xf_d, xs_d, place, w2, b1, b2, weights_in, sem):
    with ExitStack() as ctx:
        rows = ctx.enter_context(nc.sbuf_tensor("disp_rows", [P, BUFS, C], F32))
        idx = ctx.enter_context(nc.sbuf_tensor("disp_idx", [P, BUFS, 2], I32))
        s = {n: sem("d_" + n) for n in ("row0", "row1", "row2", "row3", "idx", "sent0", "sent1", "sent2", "sent3", "tick")}
        block = ctx.enter_context(nc.Block())

        @block.sync
        def _(sp):
            def load(i, q):
                if later(i, BUFS):
                    sp.wait_ge(s[f"sent{q}"], (i - q) * 8)
                sp.dma_start(rows[:, q, :], xf_d[ds(i * P, P), :]).then_inc(s[f"row{q}"], 16)
            tiles(sp, (0, load))

        @block.scalar
        def _(act):
            for e in range(0, NX, 4):
                act.dma_start(w2[:, e:e + 4, :, :], a["L0_ffn_w2"][e:e + 4].rearrange("e (k p) f -> p e k f", p=P)).then_inc(weights_in, 16)
            act.dma_start(b1[:].rearrange("p e f -> p (e f)"), a["L0_ffn_b1"].rearrange("(o e) f -> o (e f)", o=1).to_broadcast([P, NX * FF])).then_inc(weights_in, 16)
            act.dma_start(b2[:].rearrange("p e f -> p (e f)"), a["L0_ffn_b2"].rearrange("(o e) f -> o (e f)", o=1).to_broadcast([P, NX * C])).then_inc(weights_in, 16)

        @block.vector
        def _(dve):
            def number(i, q):
                if later(i, BUFS):
                    hold(dve, s[f"sent{q}"], (i - q) * 8, s["tick"])
                dve.tensor_copy(idx[:, q, :], place[:, ds(i, 1), :].rearrange("p o f -> p (o f)")).then_inc(s["idx"], 1)
            tiles(dve, (0, number))

        @block.gpsimd
        def _(pool):
            def send(i, q):
                r = rows_of(i)
                pool.wait_ge(s[f"row{q}"], (i - q) * 4 + 16)
                hold(pool, s["idx"], i + 1, s["tick"])
                for k in range(2):
                    pool.indirect_dma_start(out=xs_d, out_offset=bass.IndirectOffsetOnAxis(ap=idx[0:r, q, k:k + 1], axis=0),
                                            in_=rows[0:r, q, :], in_offset=None).then_inc(s[f"sent{q}"], 16)
            tiles(pool, (0, send))
            for q in range(BUFS):
                pool.wait_ge(s[f"sent{q}"], 32 * uses(q))


def experts(nc, xs_d, ys_d, ident, expert, w1, w2, b1, b2, weights_in, sem):
    with ExitStack() as ctx:
        def sb(name, shape, dt=F32):
            return ctx.enter_context(nc.sbuf_tensor(name, shape, dt))

        def pb(name):
            return ctx.enter_context(nc.psum_tensor(name, [P, 2, 512], F32))

        x = sb("xx", [P, BUFS, C])
        xT = sb("xxT", [P, 2, 2, P])
        hid = sb("hid", [P, 2, FF])
        hidT = sb("hidT", [P, 2, FF])
        o = sb("xo", [P, BUFS, C])
        psX, psH, psT, psO = pb("xpsX"), pb("xpsH"), pb("xpsT"), pb("xpsO")
        s = {n: sem("x_" + n) for n in ("x0", "x1", "x2", "x3", "turned", "xT", "hid_ps", "hid", "hid_turned", "hidT", "o_ps", "o",
                                        "st0", "st1", "st2", "st3")}
        block = ctx.enter_context(nc.Block())

        def pairs(eng, *stages):
            def told(step):
                return lambda j, q, u: step(j, q)
            skewed(eng, XT, BUFS, BUFS, 0, [(n, told(step)) for n, step in stages])

        def expert_of(eng, j):
            return eng.value_load(expert[0:1, ds(j, 1)], min_val=0, max_val=NX - 1)

        @block.sync
        def _(sp):
            def load(j, q):
                if later(j, BUFS):
                    sp.wait_ge(s["turned"], j - BUFS + 1)
                sp.dma_start(x[:, q, :], xs_d[ds(j * P, P), :]).then_inc(s[f"x{q}"], 16)
            pairs(sp, (0, load))

        @block.scalar
        def _(act):
            def turned(j, q):
                act.wait_ge(s["turned"], j + 1)
                if later(j, 2):
                    act.wait_ge(s["hid_ps"], j - 1)
                act.activation(xT[:, q % 2, :, :].rearrange("p k f -> p (k f)"), psX[:, q % 2, 0:2 * P], ACT.Copy).then_inc(s["xT"], 1)

            def relu(j, q):
                act.wait_ge(s["hid_turned"], j + 1)
                if later(j, 2):
                    act.wait_ge(s["o_ps"], j - 1)
                act.activation(hidT[:, q % 2, :], psT[:, q % 2, :], ACT.Relu).then_inc(s["hidT"], 1)
            pairs(act, (2, relu), (0, turned))

        @block.vector
        def _(dve):
            def bias(j, q):
                e = expert_of(dve, j)
                dve.wait_ge(s["hid_ps"], j + 1)
                if later(j, 2):
                    dve.wait_ge(s["hid_turned"], j - 1)
                dve.tensor_tensor(hid[:, q % 2, :], psH[:, q % 2, :], b1[:, ds(e, 1), :].rearrange("p o f -> p (o f)"), ALU.add).then_inc(s["hid"], 1)

            def result(j, q):
                e = expert_of(dve, j)
                dve.wait_ge(s["o_ps"], j + 1)
                if later(j, BUFS):
                    dve.wait_ge(s[f"st{q}"], (j - q) * 4)
                dve.tensor_tensor(o[:, q, :], psO[:, q % 2, 0:C], b2[:, ds(e, 1), :].rearrange("p o f -> p (o f)"), ALU.add).then_inc(s["o"], 1)
            dve.wait_ge(weights_in, 160)
            pairs(dve, (3, result), (1, bias))

        @block.tensor
        def _(pe):
            def turn(j, q):
                pe.wait_ge(s[f"x{q}"], (j - q) * 4 + 16)
                if later(j, 2):
                    pe.wait_ge(s["xT"], j - 1)
                for kc in range(2):
                    ins = pe.transpose(psX[:, q % 2, kc * P:(kc + 1) * P], x[:, q, kc * P:(kc + 1) * P], ident[:])
                ins.then_inc(s["turned"], 1)

            def up(j, q):
                e = expert_of(pe, j)
                pe.wait_ge(s["xT"], j + 1)
                if later(j, 2):
                    pe.wait_ge(s["hid"], j - 1)
                for kc in range(2):
                    ins = pe.matmul(psH[:, q % 2, :], xT[:, q % 2, kc, :], w1[:, ds(e, 1), kc, :].rearrange("p o f -> p (o f)"), start=(kc == 0), stop=(kc == 1))
                ins.then_inc(s["hid_ps"], 1)

            def turn_hidden(j, q):
                pe.wait_ge(s["hid"], j + 1)
                if later(j, 2):
                    pe.wait_ge(s["hidT"], j - 1)
                for k in range(FF // P):
                    ins = pe.transpose(psT[:, q % 2, k * P:(k + 1) * P], hid[:, q % 2, k * P:(k + 1) * P], ident[:])
                ins.then_inc(s["hid_turned"], 1)

            def down(j, q):
                e = expert_of(pe, j)
                pe.wait_ge(s["hidT"], j + 1)
                if later(j, 2):
                    pe.wait_ge(s["o"], j - 1)
                for k in range(FF // P):
                    ins = pe.matmul(psO[:, q % 2, 0:C], hidT[:, q % 2, k * P:(k + 1) * P], w2[:, ds(e, 1), k, :].rearrange("p o f -> p (o f)"),
                                    start=(k == 0), stop=(k == FF // P - 1))
                ins.then_inc(s["o_ps"], 1)
            pe.wait_ge(weights_in, 160)
            pairs(pe, (3, down), (2, turn_hidden), (1, up), (0, turn))

        @block.gpsimd
        def _(pool):
            def store(j, q):
                pool.wait_ge(s["o"], j + 1)
                pool.dma_start(ys_d[ds(j * P, P), :], o[:, q, :]).then_inc(s[f"st{q}"], 16)
            pairs(pool, (0, store))
            for q in range(BUFS):
                pool.wait_ge(s[f"st{q}"], 16 * uses(q, XT))


def finish(nc, a, y_d, xf_d, ys_d, out, eps, place, share, sem):
    with ExitStack() as ctx:
        def sb(name, shape, dt=F32):
            return ctx.enter_context(nc.sbuf_tensor(name, shape, dt))

        gamma = sb("gamma", [P, C])
        idx = sb("fidx", [P, BUFS, 2], I32)
        y = sb("fy", [P, BUFS, C])
        xf = sb("fxf", [P, BUFS, C])
        e1 = sb("fe1", [P, BUFS, C])
        e2 = sb("fe2", [P, BUFS, C])
        part = sb("fpart", [P, 2, C])
        moe = sb("fmoe", [P, 2, C])
        unit = sb("funit", [P, 2, C])
        st = sb("fst", [P, 2, 6])
        mv = sb("fmv", [P, 2, 2])
        rs = sb("frs", [P, 2, 3])
        o = sb("fo", [P, BUFS, C])
        s = {n: sem("f_" + n) for n in ("loaded", "first", "norm", "last", "y0", "y1", "y2", "y3", "idx", "e0", "e1", "e2", "e3", "moe",
                                        "stats", "root", "scale", "unit", "o", "out0", "out1", "out2", "out3", "tick")}
        block = ctx.enter_context(nc.Block())

        @block.sync
        def _(sp):
            sp.dma_start(gamma[:], a["L0_ffn_gamma"].rearrange("(o e) -> o e", o=1).to_broadcast([P, C])).then_inc(s["loaded"], 16)

            def load(i, q):
                if later(i, BUFS):
                    sp.wait_ge(s["o"], i - BUFS + 1)
                sp.dma_start(y[:, q, :], y_d[ds(i * P, P), :]).then_inc(s[f"y{q}"], 16)
                sp.dma_start(xf[:, q, :], xf_d[ds(i * P, P), :]).then_inc(s[f"y{q}"], 16)
            tiles(sp, (0, load))

        @block.gpsimd
        def _(pool):
            def gather(i, q):
                if later(i, BUFS):
                    pool.wait_ge(s["moe"], i - BUFS + 1)
                hold(pool, s["idx"], i + 1, s["tick"])
                for k, dst in enumerate((e1, e2)):
                    pool.indirect_dma_start(out=dst[:, q, :], out_offset=None, in_=ys_d,
                                            in_offset=bass.IndirectOffsetOnAxis(ap=idx[:, q, k:k + 1], axis=0)).then_inc(s[f"e{q}"], 16)
            tiles(pool, (0, gather))

        @block.scalar
        def _(act):
            def root(i, q):
                act.wait_ge(s["stats"], i + 1)
                act.activation(rs[:, q % 2, 0:1], mv[:, q % 2, 1:2], ACT.Sqrt, bias=eps[:, 0:1]).then_inc(s["root"], 1)

            def unit_rows(i, q):
                act.wait_ge(s["scale"], i + 1)
                if later(i, 2):
                    act.wait_ge(s["o"], i - 1)
                act.activation(unit[:, q % 2, :], moe[:, q % 2, :], ACT.Identity, bias=rs[:, q % 2, 2:3], scale=rs[:, q % 2, 1:2]).then_inc(s["unit"], 1)

            def store(i, q):
                r = rows_of(i)
                act.wait_ge(s["o"], i + 1)
                act.dma_start(out[ds(i * P, r), :], o[0:r, q, :]).then_inc(s[f"out{q}"], 16)
            tiles(act, (2, unit_rows), (1, root), (4, store))
            for q in range(BUFS):
                act.wait_ge(s[f"out{q}"], 16 * uses(q))

        @block.vector
        def _(dve):
            first, norm, last = Chain(dve, s["first"]), Chain(dve, s["norm"]), Chain(dve, s["last"])

            def number(i, q):
                if later(i, BUFS):
                    hold(dve, s[f"e{q}"], (i - q) * 8, s["tick"])
                dve.tensor_copy(idx[:, q, :], place[:, ds(i, 1), :].rearrange("p o f -> p (o f)")).then_inc(s["idx"], 1)

            def add(i, q):
                first.at(i * 2)
                dve.wait_ge(s[f"y{q}"], (i - q) * 8 + 32)
                dve.wait_ge(s[f"e{q}"], (i - q) * 8 + 32)
                first.link(dve.scalar_tensor_tensor(part[:, q % 2, :], e1[:, q, :], share[:, ds(i, 1), 0:1].rearrange("p o f -> p (o f)"), xf[:, q, :], ALU.mult, ALU.add))
                if later(i, 2):
                    dve.wait_ge(s["unit"], i - 1)
                dve.scalar_tensor_tensor(moe[:, q % 2, :], e2[:, q, :], share[:, ds(i, 1), 1:2].rearrange("p o f -> p (o f)"), part[:, q % 2, :], ALU.mult, ALU.add).then_inc(s["moe"], 1)
                hold(dve, s["moe"], i + 1, s["tick"])
                first.hold(dve.bn_stats(st[:, q % 2, :], moe[:, q % 2, :]), s["tick"])
                dve.bn_aggr(mv[:, q % 2, :], st[:, q % 2, :]).then_inc(s["stats"], 1)

            def scales(i, q):
                norm.at(i)
                dve.wait_ge(s["root"], i + 1)
                norm.link(dve.reciprocal(rs[:, q % 2, 1:2], rs[:, q % 2, 0:1]))
                dve.scalar_tensor_tensor(rs[:, q % 2, 2:3], mv[:, q % 2, 0:1], -1.0, rs[:, q % 2, 1:2], ALU.mult, ALU.mult).then_inc(s["scale"], 1)

            def result(i, q):
                last.at(i)
                dve.wait_ge(s["unit"], i + 1)
                if later(i, BUFS):
                    dve.wait_ge(s[f"out{q}"], (i - q) * 4)
                last.link(dve.tensor_tensor(o[:, q, :], unit[:, q % 2, :], gamma[:], ALU.mult))
                dve.tensor_tensor(o[:, q, :], o[:, q, :], y[:, q, :], ALU.add).then_inc(s["o"], 1)
            dve.wait_ge(s["loaded"], 16)
            tiles(dve, (0, number), (4, result), (3, scales), (2, add))


_INS = ["x", "src", "dst", "L0_gnn_W1", "L0_gnn_att_src1", "L0_gnn_att_dst1", "L0_gnn_b1", "L0_gnn_W2", "L0_gnn_att_src2",
        "L0_gnn_att_dst2", "L0_gnn_b2", "L0_mix_Wqkv", "L0_mix_Wout", "L0_mix_bout", "L0_ffn_gate_w", "L0_ffn_gate_b",
        "L0_ffn_w1", "L0_ffn_b1", "L0_ffn_w2", "L0_ffn_b2", "L0_ffn_gamma", "L0_ffn_beta"]


def kernel(**inputs):
    import numpy as _np
    import concourse.bacc as _bacc
    from concourse import mybir as _mybir
    from concourse.bass_utils import run_bass_kernel_spmd as _run

    nc = _bacc.Bacc("TRN2", target_bir_lowering=False, num_devices=1)
    arrays, args = {}, {}
    for name in _INS:
        array = _np.ascontiguousarray(inputs[name])
        arrays[f"in_{name}"] = array
        args[name] = nc.dram_tensor(f"in_{name}", array.shape, _mybir.dt.from_np(array.dtype), kind="ExternalInput").ap()
    out = nc.dram_tensor("out_0", (N, C), _mybir.dt.float32, kind="ExternalOutput").ap()
    build(nc, args, out)
    r = _run(nc, [arrays], core_ids=[0])
    return r.results[0]["out_0"]
```

```python
from contextlib import ExitStack

import numpy as np
import concourse.bass as bass
from concourse import mybir

F32 = mybir.dt.float32
BF16 = mybir.dt.bfloat16
I32 = mybir.dt.int32
U32 = mybir.dt.uint32
ALU = mybir.AluOpType
ACT = mybir.ActivationFunctionType
AX = mybir.AxisListType
ds = bass.ds

P = 128
N = 6250
E = 100000
C = 256
H = 4
CH = C // H
NT = (N + P - 1) // P
LAST = N - (NT - 1) * P
KT = 8
CE = KT * P
SLOTS = 3
NC = -(-E // CE)
FULL = E // CE
REST = (E - FULL * CE) // KT
GW = C + H
HW = C + 2 * H
MH = 8
MD = 64
MI = MH * MD
EPS = 1e-5
SLOPE = 0.2
FAR = 60.0
BIG = 3e38
NX = 16
FF = 512
A2 = 2 * N
XT = (A2 + NX * (P - 1)) // P
ROWS = XT * P
assert (E - FULL * CE) % KT == 0 and REST < P


def hold(eng, sem, value, tick):
    eng.wait_ge(sem, value)
    eng.sem_inc(tick, 1)


class Chain:

    def __init__(self, eng, sem):
        self.eng, self.sem, self.base, self.n = eng, sem, 0, 0

    def link(self, ins):
        self.n += 1
        ins.then_inc(self.sem, 1)
        self.eng.wait_ge(self.sem, self.base + self.n)

    def hold(self, ins, tick):
        self.n += 1
        ins.then_inc(self.sem, 1)
        hold(self.eng, self.sem, self.base + self.n, tick)

    def at(self, base):
        self.base, self.n = base, 0


def rows_of(i):
    return LAST if isinstance(i, int) and i == NT - 1 else P


def skewed(eng, n, period, head, tail, stages):
    most, least = max(o for o, _ in stages), min(o for o, _ in stages)
    start = head + most
    turns = max(0, n - tail + least - start) // period

    def whole(t):
        for o, step in stages:
            if 0 <= t - o < n:
                step(t - o, (t - o) % period, (t - o) // period)
    for t in range(start):
        whole(t)
    if turns:
        with eng.Fori(0, turns) as m:
            for r in range(period):
                for o, step in stages:
                    k = start + r - o
                    step(m * period + k, k % period, m + k // period)
    for t in range(start + turns * period, n + most):
        whole(t)


BUFS = 4


def tiles(eng, *stages):
    def told(step):
        return lambda i, q, u: step(i, q)
    skewed(eng, NT, BUFS, BUFS, 1, [(o, told(step)) for o, step in stages])


def uses(q, n=NT):
    return len(range(q, n, BUFS))


def later(i, n):
    return not isinstance(i, int) or i >= n


def build(nc, a, out):
    dram = {}

    def scratch(name, shape, dt=F32):
        dram[name] = nc.dram_tensor(name, shape, dt, kind="Internal").ap()
        return dram[name]

    srcp = scratch("srcp", (NC * CE,), I32)
    xnT_d = scratch("xnT_d", (NT, P, C))
    table = [scratch("table0", (NT * P, GW)), scratch("table1", (NT * P, GW))]
    dtab_d = scratch("dtab_d", ((NT + 2) * P, 6 * H), BF16)
    peak_d = scratch("peak_d", ((NT + 2) * P, H))
    y_d = scratch("y_d", (NT * P, C))
    xf_d = scratch("xf_d", (NT * P, C))
    xs_d = scratch("xs_d", (ROWS, C))
    ys_d = scratch("ys_d", (ROWS, C))
    weights_in = nc.alloc_semaphore(name="weights_in")

    with ExitStack() as top:
        def sb(name, shape, dt=F32, ctx=top):
            return ctx.enter_context(nc.sbuf_tensor(name, shape, dt))

        def stage(program, *args):
            own = []

            def sem(name):
                own.append(nc.alloc_semaphore(name=name))
                return own[-1]
            program(nc, *args, sem)
            nc.clear_and_free_semaphores(own)
            nc.all_engine_barrier()

        ident = sb("ident", [P, P])
        ones = sb("ones", [P, P])
        eps = sb("eps", [P, 1])
        zero = sb("zero_rows", [P, C])
        place = sb("place", [P, NT, 2], I32)
        share = sb("share", [P, NT, 2])
        expert = sb("expert", [1, XT], I32)
        hot = sb("pair_hot", [P, NT, 2, NX])
        w1 = sb("w1", [P, NX, 2, FF])

        with ExitStack() as gnn:
            identb = sb("identb", [P, P], BF16, gnn)
            iota = sb("iota", [P, P], BF16, gnn)
            distance = sb("distance", [P, 2 * P], F32, gnn)
            mixM = sb("mixM", [P, 2, C], F32, gnn)
            dotsT = sb("dotsT", [P, 4, P], F32, gnn)
            wkvT = w1[:, 0:2]
            sq, ks = w1[:, 2], w1[:, 3, 0]
            vs = [w1[:, 11 + b, 0] for b in range(SLOTS)]
            xnT = [w1[:, 4 + b, 0, 0:C] for b in range(SLOTS)]
            wq, woutT, zmix = (w1[:, e].rearrange("p a (b f) -> p (a b) f", f=C) for e in (8, 9, 10))
            attention = (xs_d, zero, xnT_d, eps, wkvT, wq, woutT, zmix, sq, ks, vs, xnT, dotsT, mixM)
            acc = sb("acc", [P, NT + 2, GW], F32, gnn)
            dtab = sb("dtab", [P, NT + 2, H], F32, gnn)
            dst_rel = sb("dst_rel", [P, NC * KT], F32, gnn)
            dst_r = sb("dst_r", [P, NC * KT], F32, gnn)
            offset = sb("offset", [P, NC], F32, gnn)
            first_node = sb("first_node", [1, NC], I32, gnn)
            window = sb("window", [1, NC], I32, gnn)
            window_tile = sb("window_tile", [1, NC], I32, gnn)
            passes = sb("passes", [1, 1], I32, gnn)
            own = sb("own", [P, NT + 2, H], F32, gnn)
            peak = sb("peak", [P, NT + 2, H], F32, gnn)
            wide = sb("wide", [1, 1], I32, gnn)
            parts = sb("parts", [P, NT + 2, 6, H], BF16, gnn)
            edges = (identb, iota, distance, acc, own, peak, dst_rel, dst_r, offset, first_node, window, window_tile, passes)
            stage(prepare_edges, a, srcp, ident, identb, ones, zero, iota, distance, eps, dst_rel, offset, first_node, passes)
            stage(project_inputs, a, xnT_d, table[0], ident, eps, acc, dtab, dotsT, wkvT, wq, woutT)
            stage(bounds, 0, ident, ones, acc, dtab, own, peak, parts, wide, dtab_d, peak_d)
            stage(maxima, 0, srcp, table[0], dtab_d, peak_d, ident, identb, iota, dst_rel, dst_r, first_node, window, passes, peak, parts, wide)
            stage(gat_edges, 0, srcp, table[0], dtab_d, *edges, attention)
            stage(project_hidden, a, table[1], ident, acc, dtab, w1, weights_in)
            stage(bounds, 1, ident, ones, acc, dtab, own, peak, parts, wide, dtab_d, peak_d)
            stage(maxima, 1, srcp, table[1], dtab_d, peak_d, ident, identb, iota, dst_rel, dst_r, first_node, window, passes, peak, parts, wide)
            stage(gat_edges, 1, srcp, table[1], dtab_d, *edges, None)
            stage(combine, a, xnT_d, y_d, xf_d, ident, eps, acc, mixM, hot, share)
        with ExitStack() as ffn:
            w2 = sb("w2", [P, NX, FF // P, C], F32, ffn)
            stage(order, a, ones, hot, place, expert, w2, weights_in)
            b1T = sb("b1T", [P, NX, FF // P], F32, ffn)
            b2 = sb("b2", [P, NX, C], F32, ffn)
            stage(dispatch, a, xf_d, xs_d, place, b1T, b2, ident, weights_in)
            stage(experts, xs_d, ys_d, ident, expert, w1, w2, b1T, b2, weights_in)
        stage(finish, a, y_d, xf_d, ys_d, out, eps, place, share)
    nc.clear_and_free_semaphores([weights_in])


def prepare_edges(nc, a, srcp, ident, identb, ones, zero, iota, distance, eps, dst_rel, offset, first_node, passes, sem):
    with ExitStack() as ctx:
        def sb(name, shape, dt=F32):
            return ctx.enter_context(nc.sbuf_tensor(name, shape, dt))

        iota_i = sb("iota_i", [P, 2 * P], I32)
        distance_i = sb("distance_i", [P, 2 * P], I32)
        zero_i = sb("zero_i", [P, KT], I32)
        dst_i = sb("dst_i", [P, NC * KT], I32)
        by_chunk_i = sb("by_chunk_i", [NC, CE], I32)
        low = sb("low", [NC, CE])
        high = sb("high", [NC, CE])
        ends = sb("ends", [P, 2])
        rows = sb("rows", [1, 2 * P])
        rows_i = sb("rows_i", [1, P], I32)
        tile_i = sb("tile_i", [1, P], I32)
        spread_row = sb("spread_row", [1, 2, NC])
        span = sb("span", [1, P])
        count = sb("count", [1, 1])
        count_i = sb("count_i", [1, 1], I32)
        base = sb("base", [P, NC])
        ps = ctx.enter_context(nc.psum_tensor("pe_ps", [P, 512], F32))
        ps2 = ctx.enter_context(nc.psum_tensor("pe_ps2", [P, 512], F32))
        s = {n: sem("e_" + n) for n in ("filled", "loaded", "stored", "consts", "steps", "turned", "rowed", "spread", "tiled", "zeroed")}
        block = ctx.enter_context(nc.Block())
        whole = a["dst"][0:FULL * CE].rearrange("(k p t) -> p k t", p=P, t=KT)
        part = a["dst"][FULL * CE:E].rearrange("(p t) -> p t", t=KT)

        @block.sync
        def _(sp):
            sp.dma_start(srcp[0:E].rearrange("(p f) -> p f", p=P // 4), a["src"].rearrange("(p f) -> p f", p=P // 4)).then_inc(s["stored"], 16)
            sp.wait_ge(s["filled"], 3)
            sp.dma_start(srcp[E:NC * CE].rearrange("(p t) -> p t", t=KT), zero_i[0:P - REST, :]).then_inc(s["stored"], 16)
            sp.dma_start(dst_i[:, 0:FULL * KT].rearrange("p (k t) -> p k t", t=KT), whole).then_inc(s["loaded"], 16)
            sp.dma_start(dst_i[0:REST, FULL * KT:NC * KT], part).then_inc(s["loaded"], 16)
            sp.dma_start(by_chunk_i[0:FULL, :], a["dst"][0:FULL * CE].rearrange("(k e) -> k e", e=CE)).then_inc(s["loaded"], 16)
            sp.dma_start(by_chunk_i[FULL:NC, 0:REST * KT], a["dst"][FULL * CE:E].rearrange("(k e) -> k e", k=1)).then_inc(s["loaded"], 16)
            sp.wait_ge(s["stored"], 32)

        @block.gpsimd
        def _(pool):
            pool.memset(ones[:], 1.0)
            pool.memset(eps[:], EPS)
            pool.memset(zero[:], 0.0)
            pool.memset(ident[:], 0.0).then_inc(s["zeroed"], 1)
            pool.iota(iota_i[:], pattern=[[1, 2 * P]], base=0, channel_multiplier=0)
            pool.iota(distance_i[:], pattern=[[1, 2 * P]], base=0, channel_multiplier=-1)
            pool.wait_ge(s["zeroed"], 1)
            pool.affine_select(out=ident[:], in_=ident[:], compare_op=ALU.not_equal, fill=1.0, base=0,
                               pattern=[[-1, P]], channel_multiplier=1).then_inc(s["consts"], 1)

        @block.vector
        def _(dve):
            chain = Chain(dve, s["steps"])
            dve.memset(zero_i[:], 0).then_inc(s["filled"], 1)
            dve.memset(dst_i[:], 1 << 20).then_inc(s["filled"], 1)
            dve.memset(by_chunk_i[:], 1 << 20).then_inc(s["filled"], 1)
            dve.wait_ge(s["consts"], 1)
            dve.tensor_copy(iota[:], iota_i[:, 0:P])
            dve.tensor_copy(distance[:], distance_i[:])
            dve.tensor_copy(identb[:], ident[:])
            dve.wait_ge(s["loaded"], 64)
            dve.tensor_copy(dst_rel[:], dst_i[:])
            dve.tensor_copy(low[:], by_chunk_i[:])
            chain.link(dve.memset(ends[:], 0.0))
            chain.link(dve.tensor_scalar(high[:], low[:], float(1 << 19), -float(1 << 20), ALU.is_ge, ALU.mult))
            chain.link(dve.tensor_tensor(high[:], high[:], low[:], ALU.add))
            chain.link(dve.tensor_reduce(ends[0:NC, 0:1], low[:], AX.X, ALU.min))
            dve.tensor_reduce(ends[0:NC, 1:2], high[:], AX.X, ALU.max).then_inc(s["tiled"], 1)
            dve.wait_ge(s["turned"], 1)
            chain.link(dve.tensor_copy(rows[:], ps[0:1, 0:2 * P]))
            chain.link(dve.tensor_copy(rows_i[:], rows[:, 0:P]))
            chain.link(dve.tensor_copy(first_node[:], rows_i[:, 0:NC]))
            chain.link(dve.tensor_tensor(span[:], rows[:, P:2 * P], rows[:, 0:P], ALU.subtract))
            chain.link(dve.tensor_reduce(count[:], span[:], AX.X, ALU.max))
            chain.link(dve.tensor_copy(count_i[:], count[:]))
            chain.link(dve.tensor_scalar(count_i[:], count_i[:], 7, None, ALU.arith_shift_right))
            chain.link(dve.tensor_scalar(passes[:], count_i[:], 1, None, ALU.add))
            chain.link(dve.tensor_scalar(tile_i[:], rows_i[:], P - 1, None, ALU.bitwise_and))
            chain.link(dve.tensor_copy(spread_row[:, 0, :], rows[:, 0:NC]))
            dve.tensor_copy(spread_row[:, 1, :], tile_i[:, 0:NC]).then_inc(s["rowed"], 1)
            dve.wait_ge(s["spread"], 1)
            chain.link(dve.tensor_copy(base[:], ps2[:, 0:NC]))
            dve.tensor_copy(offset[:], ps2[:, NC:2 * NC])
            rel = dst_rel[:].rearrange("p (k t) -> p k t", t=KT)
            chain.link(dve.tensor_tensor(rel, rel, base[:].rearrange("p (k t) -> p k t", t=1).to_broadcast([P, NC, KT]), ALU.subtract))

        @block.tensor
        def _(pe):
            pe.wait_ge(s["consts"], 1)
            pe.wait_ge(s["tiled"], 1)
            pe.transpose(ps[0:1, 0:P], ends[:, 0:1], ident[:])
            pe.transpose(ps[0:1, P:2 * P], ends[:, 1:2], ident[:]).then_inc(s["turned"], 1)
            pe.wait_ge(s["rowed"], 1)
            pe.matmul(ps2[:, 0:2 * NC], ones[0:1, :], spread_row[:].rearrange("o a k -> o (a k)"), start=True, stop=True).then_inc(s["spread"], 1)


def project_inputs(nc, a, xnT_d, table, ident, eps, acc, dtab, dotsT, wkvT, wq, woutT, sem):
    with ExitStack() as ctx:
        def sb(name, shape, dt=F32):
            return ctx.enter_context(nc.sbuf_tensor(name, shape, dt))

        def pb(name, shape):
            return ctx.enter_context(nc.psum_tensor(name, shape, F32))

        wext = sb("wext0", [P, 2, HW])
        att = sb("att0", [P, 2, C])
        attw = sb("attw0", [P, 2, C])
        wkv = sb("wkv", [P, 8, C])
        wmean = sb("wmean", [P, 2 * MH])
        wout = sb("wout", [P, 2, MI])
        x = sb("x_in", [P, BUFS, C])
        st = sb("st", [P, 2, 6])
        mv = sb("mv", [P, 2, 2])
        rs = sb("rs", [P, 2, 2])
        xn = sb("xn", [P, 2, C])
        xnT = sb("xnT", [P, BUFS, 2, P])
        psX = pb("psX", [P, 2, 512])
        psH = pb("psH", [P, 2, 512])
        psW = pb("psW", [P, 512])
        loaded, steps, turned, moved = sem("i_loaded"), sem("i_steps"), sem("i_turned"), sem("i_moved")
        first_block = ExitStack()
        block = first_block.enter_context(nc.Block())

        @block.sync
        def _(sp):
            sp.dma_start(wext[:, :, 0:C], a["L0_gnn_W1"].rearrange("(k p) n -> p k n", p=P)).then_inc(loaded, 16)
            sp.dma_start(att[:, 0, :], a["L0_gnn_att_src1"].rearrange("(o h) c -> o (h c)", o=1).to_broadcast([P, C])).then_inc(loaded, 16)
            sp.dma_start(att[:, 1, :], a["L0_gnn_att_dst1"].rearrange("(o h) c -> o (h c)", o=1).to_broadcast([P, C])).then_inc(loaded, 16)
            sp.dma_start(wkv[:], a["L0_mix_Wqkv"][MI:3 * MI, :].rearrange("(k p) c -> p k c", p=P)).then_inc(loaded, 16)
            sp.dma_start(wq, a["L0_mix_Wqkv"][0:MI, :].rearrange("(k p) c -> p k c", p=P)).then_inc(loaded, 16)
            sp.dma_start(wout[:], a["L0_mix_Wout"].rearrange("(k p) c -> p k c", p=P)).then_inc(loaded, 16)

        @block.vector
        def _(dve):
            chain = Chain(dve, steps)
            dve.memset(acc[:, NT:NT + 2, :], 0.0)
            dve.memset(dtab[:, NT:NT + 2, :], 0.0)
            dve.memset(dotsT[:], 0.0)
            dve.wait_ge(loaded, 96)
            attention_columns(dve, chain, wext, att, attw)
            for g in range(6):
                dve.wait_ge(turned, g + 1)
                if g < 4:
                    kc, q = g // 2, g % 2
                    dve.tensor_copy(wkvT[:, kc, q, :], psW[:, :]).then_inc(moved, 1)
                else:
                    dve.tensor_copy(woutT[:, :, (g - 4) * P:(g - 3) * P], psW[:, :].rearrange("p (k f) -> p k f", k=4)).then_inc(moved, 1)
            dve.wait_ge(moved, 6)
            for kc in range(2):
                w = wkvT[:, kc, :, :].rearrange("p a (g d) -> p (a g) d", d=MD)
                chain.link(dve.tensor_reduce(wmean[:], w, AX.X, ALU.add))
                chain.link(dve.tensor_scalar(wmean[:], wmean[:], 1.0 / MD, None, ALU.mult))
                chain.link(dve.tensor_tensor(w, w, wmean[:].rearrange("p (g d) -> p g d", d=1).to_broadcast([P, 2 * MH, MD]), ALU.subtract))

        @block.tensor
        def _(pe):
            pe.wait_ge(loaded, 96)
            for g in range(6):
                if g:
                    pe.wait_ge(moved, g)
                for j in range(4):
                    if g < 4:
                        kc, q = g // 2, g % 2
                        ins = pe.transpose(psW[:, j * P:(j + 1) * P], wkv[:, 4 * q + j, kc * P:(kc + 1) * P], ident[:])
                    else:
                        ins = pe.transpose(psW[:, j * P:(j + 1) * P], wout[:, g - 4, j * P:(j + 1) * P], ident[:])
                ins.then_inc(turned, 1)

        first_block.close()
        s = {n: sem("i_" + n) for n in ("x_in0", "x_in1", "x_in2", "x_in3", "xT_out0", "xT_out1", "xT_out2", "xT_out3", "xT_ps", "xT", "h_ps", "h_out",
                                        "h_stored", "stats", "root", "xn", "first", "norm", "tick")}
        block2 = ctx.enter_context(nc.Block())

        @block2.sync
        def _(sp):
            def load(i, q):
                r = rows_of(i)
                if later(i, BUFS):
                    sp.wait_ge(s["xn"], i - BUFS + 1)
                sp.dma_start(x[0:r, q, :], a["x"][ds(i * P, r), :]).then_inc(s[f"x_in{q}"], 16)
            tiles(sp, (0, load))

        @block2.gpsimd
        def _(pool):
            def store_h(i, q):
                pool.wait_ge(s["h_out"], i * 2 + 2)
                pool.dma_start(table[ds(i * P, P), :], acc[:, ds(i, 1), :].rearrange("p o f -> p (o f)")).then_inc(s["h_stored"], 16)
            tiles(pool, (0, store_h))
            pool.wait_ge(s["h_stored"], 16 * NT)

        @block2.vector
        def _(dve):
            first, norm = Chain(dve, s["first"]), Chain(dve, s["norm"])

            def stats(i, q):
                first.at(i)
                dve.wait_ge(s[f"x_in{q}"], (i - q) * 16 // BUFS + 16)
                first.hold(dve.bn_stats(st[:, q % 2, :], x[:, q, :]), s["tick"])
                dve.bn_aggr(mv[:, q % 2, :], st[:, q % 2, :]).then_inc(s["stats"], 1)

            def normalise(i, q):
                norm.at(i)
                dve.wait_ge(s["root"], i + 1)
                norm.link(dve.reciprocal(rs[:, q % 2, 1:2], rs[:, q % 2, 0:1]))
                if later(i, 2):
                    dve.wait_ge(s["xT_ps"], i - 1)
                dve.tensor_scalar(xn[:, q % 2, :], x[:, q, :], mv[:, q % 2, 0:1], rs[:, q % 2, 1:2], ALU.subtract, ALU.mult).then_inc(s["xn"], 1)

            tiles(dve, (1, normalise), (0, stats))

        @block2.scalar
        def _(act):
            def project(i, q):
                act.wait_ge(s["h_ps"], i + 1)
                act.activation(acc[:, ds(i, 1), :].rearrange("p o f -> p (o f)"), psH[:, q % 2, 0:GW], ACT.Copy).then_inc(s["h_out"], 1)
                act.activation(dtab[:, ds(i, 1), :].rearrange("p o f -> p (o f)"), psH[:, q % 2, GW:HW], ACT.Copy).then_inc(s["h_out"], 1)

            def root(i, q):
                act.wait_ge(s["stats"], i + 1)
                act.activation(rs[:, q % 2, 0:1], mv[:, q % 2, 1:2], ACT.Sqrt, bias=eps[:, 0:1]).then_inc(s["root"], 1)

            def turned(i, q):
                act.wait_ge(s["xT_ps"], i + 1)
                if later(i, BUFS):
                    act.wait_ge(s[f"xT_out{q}"], (i - q) * 16 // BUFS)
                act.activation(xnT[:, q, :, :].rearrange("p k f -> p (k f)"), psX[:, q % 2, 0:2 * P], ACT.Copy).then_inc(s["xT"], 1)
            def store_x(i, q):
                act.wait_ge(s["xT"], i + 1)
                act.dma_start(xnT_d[ds(i, 1), :, :].rearrange("o p f -> (o p) f"), xnT[:, q, :, :].rearrange("p k f -> p (k f)")).then_inc(s[f"xT_out{q}"], 16)

            tiles(act, (0, root), (1, turned), (1, store_x), (2, project))
            for q in range(BUFS):
                act.wait_ge(s[f"xT_out{q}"], 16 * uses(q))

        @block2.tensor
        def _(pe):
            def project(i, q):
                pe.wait_ge(s["xT"], i + 1)
                if later(i, 2):
                    pe.wait_ge(s["h_out"], i * 2 - 2)
                for kc in range(2):
                    ins = pe.matmul(psH[:, q % 2, 0:HW], xnT[:, q, kc, :], wext[:, kc, :], start=(kc == 0), stop=(kc == 1))
                ins.then_inc(s["h_ps"], 1)

            def turn(i, q):
                pe.wait_ge(s["xn"], i + 1)
                if later(i, 2):
                    pe.wait_ge(s["xT"], i - 1)
                for kc in range(2):
                    ins = pe.transpose(psX[:, q % 2, kc * P:(kc + 1) * P], xn[:, q % 2, kc * P:(kc + 1) * P], ident[:])
                ins.then_inc(s["xT_ps"], 1)
            tiles(pe, (1, turn), (2, project))


def attention_columns(dve, chain, wext, att, attw):
    for j in range(2):
        for kc in range(2):
            chain.link(dve.tensor_tensor(attw[:, kc, :], wext[:, kc, 0:C], att[:, j, :], ALU.mult))
            chain.link(dve.tensor_reduce(wext[:, kc, C + j * H:C + (j + 1) * H], attw[:, kc, :].rearrange("p (h c) -> p h c", h=H), AX.X, ALU.add))


def split(chain, parts, x, rest, at):
    chain.link(chain.eng.tensor_copy(parts[:, :, at, :], x[:]))
    chain.link(chain.eng.tensor_tensor(rest[:], x[:], parts[:, :, at, :], ALU.subtract))
    chain.link(chain.eng.tensor_copy(parts[:, :, at + 1, :], rest[:]))
    chain.link(chain.eng.tensor_tensor(rest[:], rest[:], parts[:, :, at + 1, :], ALU.subtract))
    chain.link(chain.eng.tensor_copy(parts[:, :, at + 2, :], rest[:]))


def bounds(nc, layer, ident, ones, acc, dtab, own, peak, parts, wide, dtab_d, peak_d, sem):
    with ExitStack() as ctx:
        def sb(name, shape, dt=F32):
            return ctx.enter_context(nc.sbuf_tensor(f"{name}_{layer}", shape, dt))

        low = sb("bd_low", [P, H])
        ends = sb("bd_ends", [P, 2 * H])
        head = sb("bd_head", [2 * H, 1])
        diag = sb("bd_diag", [2 * H, 2 * H])
        ends_all = sb("bd_all", [P, 2 * H])
        spread = sb("bd_spread", [P, H])
        most = sb("bd_most", [P, 1])
        rest = sb("bd_rest", [P, NT + 2, H])
        ps = ctx.enter_context(nc.psum_tensor(f"bd_ps{layer}", [P, 512], F32))
        s = {n: sem(f"bd{layer}_{n}") for n in ("steps", "ends", "turned", "diagonal", "spread", "own", "split", "stored")}
        block = ctx.enter_context(nc.Block())

        @block.sync
        def _(sp):
            sp.wait_ge(s["own"], 1)
            sp.dma_start(peak_d.rearrange("(t p) h -> p t h", p=P), own[:]).then_inc(s["stored"], 16)
            sp.wait_ge(s["split"], 1)
            sp.dma_start(dtab_d.rearrange("(t p) f -> p t f", p=P), parts[:].rearrange("p t c h -> p t (c h)")).then_inc(s["stored"], 16)
            sp.wait_ge(s["stored"], 32)

        @block.vector
        def _(dve):
            chain = Chain(dve, s["steps"])
            full = acc[:, 0:NT - 1, C:GW].rearrange("p i h -> p h i")
            chain.link(dve.tensor_reduce(low[:], full, AX.X, ALU.min))
            chain.link(dve.tensor_reduce(ends[:, 0:H], full, AX.X, ALU.max))
            chain.link(dve.tensor_tensor(low[0:LAST, :], low[0:LAST, :], acc[0:LAST, NT - 1, C:GW], ALU.min))
            chain.link(dve.tensor_tensor(ends[0:LAST, 0:H], ends[0:LAST, 0:H], acc[0:LAST, NT - 1, C:GW], ALU.max))
            dve.tensor_scalar(ends[:, H:2 * H], low[:], -1.0, None, ALU.mult).then_inc(s["ends"], 1)
            dve.wait_ge(s["turned"], 1)
            chain.link(dve.tensor_reduce(head[:], ps[0:2 * H, 0:P], AX.X, ALU.max))
            dve.tensor_scalar(diag[:], ident[0:2 * H, 0:2 * H], head[:, 0:1], None, ALU.mult).then_inc(s["diagonal"], 1)
            chain.link(dve.tensor_tensor(own[:], acc[:, :, C:GW], dtab[:], ALU.add))
            dve.scalar_tensor_tensor(own[:], own[:], SLOPE, own[:], ALU.mult, ALU.max).then_inc(s["own"], 1)
            split(chain, parts, dtab, rest, 0)
            dve.wait_ge(s["spread"], 1)
            chain.link(dve.tensor_copy(ends_all[:], ps[:, 256:256 + 2 * H]))
            chain.link(dve.tensor_tensor(spread[:], ends_all[:, 0:H], ends_all[:, H:2 * H], ALU.add))
            chain.link(dve.tensor_reduce(most[:], spread[:], AX.X, ALU.max))
            chain.link(dve.tensor_scalar(most[:], most[:], FAR, None, ALU.is_gt))
            dve.tensor_copy(wide[:], most[0:1, :])
            chain.link(dve.tensor_tensor(peak[:], dtab[:], ends_all[:, 0:H].rearrange("p (o h) -> p o h", o=1).to_broadcast([P, NT + 2, H]), ALU.add))
            chain.link(dve.scalar_tensor_tensor(peak[:], peak[:], SLOPE, peak[:], ALU.mult, ALU.max))
            split(chain, parts, peak, rest, 3)
            dve.sem_inc(s["split"], 1)

        @block.tensor
        def _(pe):
            pe.wait_ge(s["ends"], 1)
            pe.transpose(ps[0:2 * H, 0:P], ends[:], ident[:]).then_inc(s["turned"], 1)
            pe.wait_ge(s["diagonal"], 1)
            pe.matmul(ps[:, 256:256 + 2 * H], ones[0:2 * H, :], diag[:], start=True, stop=True).then_inc(s["spread"], 1)


def maxima(nc, layer, srcp, table, dtab_d, peak_d, ident, identb, iota, dst_rel, dst_r, first_node, window, passes, peak, parts, wide, sem):
    with ExitStack() as ctx:
        def sb(name, shape, dt=F32):
            return ctx.enter_context(nc.sbuf_tensor(f"{name}_{layer}", shape, dt))

        def pb(name, shape, dt=F32):
            return ctx.enter_context(nc.psum_tensor(f"{name}_{layer}", shape, dt))

        idx = sb("mx_idx", [P, KT], I32)
        dwin = sb("mx_dwin", [P, 6 * H], BF16)
        before = sb("mx_before", [P, H])
        G = sb("mx_gathered", [P, KT, GW])
        hot = sb("mx_hot", [P, KT, P], BF16)
        hotT = sb("mx_hotT", [P, KT, P], BF16)
        away = sb("mx_away", [P, KT, P])
        target = sb("mx_target", [P, KT, H])
        z = sb("mx_z", [P, KT, H])
        placed = sb("mx_placed", [P, H, P])
        found = sb("mx_found", [P, KT, H])
        best = sb("mx_best", [P, H])
        rest = sb("mx_rest", [P, NT + 2, H])
        psT = pb("mx_psT", [P, KT, P], BF16)
        psD = pb("mx_psD", [P, 2 * KT, 3, H])
        psV = pb("mx_psV", [P, H, P])
        s = {n: sem(f"m{layer}_{n}") for n in ("idx_in", "win_in", "g_in", "pass", "hot", "turned", "hotT", "targets", "placed", "placedT",
                                               "best", "peak_out", "peak_in", "split", "stored", "steps", "folded", "ends", "tick")}
        block = ctx.enter_context(nc.Block())

        def passes_over(eng, begin, step, end=None):
            rounds = eng.value_load(passes[0:1, 0:1], min_val=1, max_val=NT)
            with eng.Fori(0, rounds) as r:
                begin(r)
                with eng.Fori(0, NC) as c:
                    step(r * NC + c, c)
                if end:
                    end(r)

        def far(eng):
            return eng.If(eng.value_load(wide[0:1, 0:1], min_val=0, max_val=1) > 0)

        @block.sync
        def _(sp):
            def begin(r):
                hold(sp, s["pass"], r * 2 + 2, s["tick"])

            def step(g, c):
                node = sp.value_load(window[0:1, ds(c, 1)], min_val=0, max_val=NT * P)
                sp.dma_start(idx[:], srcp[ds(c * CE, CE)].rearrange("(p t) -> p t", t=KT)).then_inc(s["idx_in"], 16)
                sp.dma_start(dwin[:], dtab_d[ds(node, P), :]).then_inc(s["win_in"], 16)
                sp.dma_start(before[:], peak_d[ds(node, P), :]).then_inc(s["win_in"], 16)
                sp.wait_ge(s["best"], g + 1)
                sp.dma_start(peak_d[ds(node, P), :], best[:]).then_inc(s["peak_out"], 16)
                hold(sp, s["peak_out"], g * 16 + 16, s["tick"])
            with far(sp):
                passes_over(sp, begin, step)
                sp.dma_start(peak[:], peak_d.rearrange("(t p) h -> p t h", p=P)).then_inc(s["peak_in"], 16)
                sp.wait_ge(s["split"], 1)
                sp.dma_start(dtab_d.rearrange("(t p) f -> p t f", p=P), parts[:].rearrange("p t c h -> p t (c h)")).then_inc(s["stored"], 16)
                sp.wait_ge(s["stored"], 16)

        @block.gpsimd
        def _(pool):
            def step(g, c):
                hold(pool, s["idx_in"], g * 16 + 16, s["tick"])
                for k in range(KT):
                    pool.indirect_dma_start(out=G[:, k, :], out_offset=None, in_=table,
                                            in_offset=bass.IndirectOffsetOnAxis(ap=idx[:, k:k + 1], axis=0)).then_inc(s["g_in"], 16)
            with far(pool):
                passes_over(pool, lambda r: None, step)

        @block.vector
        def _(dve):
            chain = Chain(dve, s["steps"])
            STEPS = 5

            def begin(r):
                hold(dve, s["pass"], r * 2 + 2, s["tick"])

            def step(g, c):
                chain.at(g * STEPS)
                for k in range(KT):
                    dve.tensor_scalar(hot[:, k, :], iota[:], dst_r[:, ds(c * KT + k, 1)], None, ALU.is_equal).then_inc(s["hot"], 1)
                dve.wait_ge(s["hot"], g * KT + KT)
                chain.link(dve.tensor_scalar(away[:], hot[:], BIG, -BIG, ALU.mult, ALU.add))
                dve.wait_ge(s["targets"], g + 1)
                chain.link(dve.tensor_reduce(target[:], psD[:].rearrange("p (k g) c h -> p k g h c", g=2)[:, :, 0, :, :], AX.X, ALU.add))
                dve.wait_ge(s["g_in"], g * 16 * KT + 16 * KT)
                chain.link(dve.tensor_tensor(z[:], target[:], G[:, :, C:GW], ALU.add))
                chain.link(dve.scalar_tensor_tensor(z[:], z[:], SLOPE, z[:], ALU.mult, ALU.max))
                for k in range(KT):
                    for h in range(H):
                        dve.scalar_tensor_tensor(placed[:, h, :], hot[:, k, :], z[:, k, h:h + 1], away[:, k, :], ALU.mult, ALU.add).then_inc(s["placed"], 1)
                    dve.wait_ge(s["placedT"], g * KT + k + 1)
                    ins = dve.tensor_reduce(found[:, k, :], psV[:], AX.X, ALU.max)
                    if k == KT - 1:
                        chain.link(ins)
                    else:
                        ins.then_inc(s["tick"], 1)
                dve.wait_ge(s["win_in"], g * 32 + 32)
                dve.tensor_reduce(best[:], found[:].rearrange("p k h -> p h k"), AX.X, ALU.max).then_inc(s["folded"], 1)
                dve.wait_ge(s["folded"], g + 1)
                dve.tensor_tensor(best[:], best[:], before[:], ALU.max).then_inc(s["best"], 1)
                assert chain.n == STEPS

            def end(r):
                dve.tensor_scalar(dst_r[:], dst_r[:], -float(P), None, ALU.add).then_inc(s["pass"], 1)
                dve.tensor_scalar(window[:], window[:], P, NT * P, ALU.add, ALU.min).then_inc(s["pass"], 1)
            with far(dve):
                dve.tensor_copy(dst_r[:], dst_rel[:]).then_inc(s["pass"], 1)
                dve.tensor_copy(window[:], first_node[:]).then_inc(s["pass"], 1)
                passes_over(dve, begin, step, end)
                dve.wait_ge(s["peak_in"], 16)
                chain = Chain(dve, s["ends"])
                split(chain, parts, peak, rest, 3)
                dve.sem_inc(s["split"], 1)

        @block.scalar
        def _(act):
            def step(g, c):
                act.wait_ge(s["turned"], g + 1)
                act.activation(hotT[:], psT[:], ACT.Copy).then_inc(s["hotT"], 1)
            with far(act):
                passes_over(act, lambda r: None, step)

        @block.tensor
        def _(pe):
            def step(g, c):
                pe.wait_ge(s["hot"], g * KT + KT)
                for k in range(KT):
                    ins = pe.transpose(psT[:, k, :], hot[:, k, :], identb[:])
                ins.then_inc(s["turned"], 1)
                pe.wait_ge(s["hotT"], g + 1)
                pe.wait_ge(s["win_in"], g * 32 + 32)
                for k in range(KT):
                    ins = pe.matmul(psD[:, 2 * k:2 * k + 2, :, :].rearrange("p g c h -> p (g c h)"), hotT[:, k, :], dwin[:], start=True, stop=True)
                ins.then_inc(s["targets"], 1)
                for k in range(KT):
                    pe.wait_ge(s["placed"], (g * KT + k) * H + H)
                    for h in range(H):
                        ins = pe.transpose(psV[:, h, :], placed[:, h, :], ident[:])
                    ins.then_inc(s["placedT"], 1)
            with far(pe):
                passes_over(pe, lambda r: None, step)


def gat_edges(nc, layer, srcp, table, dtab_d, identb, iota, distance, acc, own, peak, dst_rel, dst_r, offset, first_node, window, window_tile, passes, attention, sem):
    with ExitStack() as ctx:
        def sb(name, shape, dt=F32):
            return ctx.enter_context(nc.sbuf_tensor(f"{name}_{layer}", shape, dt))

        def pb(name, shape, dt=F32):
            return ctx.enter_context(nc.psum_tensor(f"{name}_{layer}", shape, dt))

        idx = sb("idx", [P, SLOTS, KT], I32)
        dwin = sb("dwin", [P, SLOTS, 6 * H], BF16)
        G = sb("gathered", [P, SLOTS, KT, GW])
        hot = sb("hot", [P, SLOTS, KT, P], BF16)
        hotf = sb("hotf", [P, SLOTS, KT, P])
        hotT = sb("hotT", [P, SLOTS, KT, P], BF16)
        shift = sb("shift", [P, SLOTS, 2 * P])
        win = sb("win", [P, GW])
        both = sb("both_e", [P, 2 * KT, H])
        z = sb("z_e", [P, KT, H])
        t = sb("t_e", [P, KT, H])
        psT = pb("psT", [P, KT, P], BF16)
        psD = pb("psD_e", [P, 2 * KT, 3, H])
        psA = pb("psA_e", [P, 512])
        psB = pb("psB_e", [P, 2, 512])
        if attention:
            xs_d, zero, xnT_d, eps, wkvT, wq, woutT, zmix, sq, ks, vs, xnT, dotsT, mixM = attention
            ss = sb("ss", [P, 3, 2 * MH])
            rkv = sb("rkv", [P, MH])
            psKV = pb("psKV", [P, 2, MI])
            psM = pb("psM", [P, 512])
        names = ("cleared", "xn_in0", "xn_in1", "xn_in2", "keys_ps", "values_ps", "squared", "kvsum", "kvroot", "ks", "vs", "dots", "key", "end", "idx_in0", "idx_in1", "idx_in2", "d_in0", "d_in1", "d_in2", "g_in0", "g_in1", "g_in2", "hot", "turned", "hotT", "hotf", "targets", "shift", "own", "own_weights", "own_terms",
                 "target_read", "logits", "weights", "scaled", "added", "win", "shifted", "acc", "pass", "vsteps", "tick")
        s = {n: sem(f"g{layer}_{n}") for n in names}
        block = ctx.enter_context(nc.Block())

        def chunks(eng, begin, end, *stages):
            rounds = eng.value_load(passes[0:1, 0:1], min_val=1, max_val=NT)
            with eng.Fori(0, rounds) as r:
                def told(step):
                    return lambda c, k, u: step(r * NC + c, c, k % SLOTS, r * len(range(k % SLOTS, NC, SLOTS)) + u * 2 + k // SLOTS)

                def tile_of(step):
                    def even(c, k, u):
                        if attention and k % 2 == 0:
                            b = k // 2
                            step(r * NT + (u * SLOTS + b), u * SLOTS + b, b, r * len(range(b, NT, SLOTS)) + u)
                    return even
                begin(r)
                skewed(eng, NC, 2 * SLOTS, 2, 2, [(o, tile_of(step) if by_tile else told(step)) for o, step, *by_tile in stages])
                end(r)
            return rounds

        def nothing(r):
            pass

        def new_pass(eng):
            return lambda r: hold(eng, s["pass"], r * 3 + 3, s["tick"])

        @block.sync
        def _(sp):
            def load(g, c, q, use):
                node = sp.value_load(window[0:1, ds(c, 1)], min_val=0, max_val=NT * P)
                sp.wait_ge(s["logits"], g + 1)
                sp.dma_start(idx[:, q, :], srcp[ds(c * CE, CE)].rearrange("(p t) -> p t", t=KT)).then_inc(s[f"idx_in{q}"], 16)
                sp.dma_start(dwin[:, q, :], dtab_d[ds(node, P), :]).then_inc(s[f"d_in{q}"], 16)

            def load_x(t, i, b, use):
                sp.wait_ge(s["values_ps"], t + 1)
                sp.wait_ge(s["keys_ps"], t + 1)
                sp.dma_start(xnT[b], xnT_d[ds(i, 1), :, :].rearrange("o p f -> (o p) f")).then_inc(s[f"xn_in{b}"], 16)
                clear(i * 2, 2)

            def clear(first, n):
                sp.dma_start(xs_d[ds(first * P, n * P), :].rearrange("(t p) c -> p t c", p=P), zero[:].rearrange("p (o c) -> p o c", o=1).to_broadcast([P, n, C])).then_inc(s["cleared"], 16)
            rounds = chunks(sp, new_pass(sp), nothing, (0, load), (0, load_x, True))
            if attention:
                clear(2 * NT, XT - 2 * NT)
                hold(sp, s["cleared"], rounds * (16 * NT) + 16, s["tick"])

        @block.gpsimd
        def _(pool):
            def gather(g, c, q, use):
                pool.wait_ge(s[f"idx_in{q}"], 16 * use + 16)
                hold(pool, s["added"], g + 1, s["tick"])
                for k in range(KT):
                    pool.indirect_dma_start(out=G[:, q, k, :], out_offset=None, in_=table,
                                            in_offset=bass.IndirectOffsetOnAxis(ap=idx[:, q, k:k + 1], axis=0)).then_inc(s[f"g_in{q}"], 16)
            chunks(pool, nothing, nothing, (0, gather))

        @block.vector
        def _(dve):
            dve.sem_inc(s["logits"], SLOTS)
            dve.sem_inc(s["target_read"], 1)
            dve.sem_inc(s["acc"], 1)
            dve.tensor_copy(dst_r[:], dst_rel[:]).then_inc(s["pass"], 1)
            dve.tensor_copy(window[:], first_node[:]).then_inc(s["pass"], 1)
            dve.tensor_scalar(window_tile[:], first_node[:], 7, None, ALU.arith_shift_right).then_inc(s["pass"], 1)
            dve.tensor_tensor(own[:], own[:], peak[:], ALU.subtract).then_inc(s["own"], 1)
            dve.wait_ge(s["own_weights"], 1)
            for h in range(H):
                f = acc[:, 0:NT, h * CH:(h + 1) * CH]
                dve.tensor_tensor(f, f, acc[:, 0:NT, C + h:C + h + 1].to_broadcast([P, NT, CH]), ALU.mult).then_inc(s["own_terms"], 1)
            dve.wait_ge(s["own_terms"], H)
            chain = Chain(dve, s["vsteps"])
            STEPS = 2
            target, maximum = (both[:].rearrange("p (k g) h -> p k g h", g=2)[:, :, g, :] for g in range(2))

            def one_hot(g, c, q, use):
                for k in range(KT):
                    dve.tensor_scalar(hot[:, q, k, :], iota[:], dst_r[:, ds(c * KT + k, 1)], None, ALU.is_equal).then_inc(s["hot"], 1)

            def weigh(g, c, q, use):
                chain.at(g * STEPS)
                dve.tensor_scalar(shift[:, q, :], distance[:], offset[:, ds(c, 1)], None, ALU.is_equal).then_inc(s["shift"], 1)
                dve.wait_ge(s["targets"], g + 1)
                dve.tensor_reduce(both[:], psD[:].rearrange("p k c h -> p k h c"), AX.X, ALU.add).then_inc(s["target_read"], 1)
                dve.wait_ge(s["target_read"], g + 2)
                dve.wait_ge(s[f"g_in{q}"], 16 * KT * use + 16 * KT)
                chain.link(dve.tensor_tensor(z[:], target, G[:, q, :, C:GW], ALU.add))
                chain.link(dve.scalar_tensor_tensor(z[:], z[:], SLOPE, z[:], ALU.mult, ALU.max))
                dve.tensor_tensor(t[:], z[:], maximum, ALU.subtract).then_inc(s["logits"], 1)
                dve.wait_ge(s["weights"], g + 1)
                f = G[:, q, :, 0:C].rearrange("p k (h c) -> p k h c", h=H)
                w = G[:, q, :, C:GW].rearrange("p k (h c) -> p k h c", c=1).to_broadcast([P, KT, H, CH])
                dve.tensor_tensor(f, f, w, ALU.mult).then_inc(s["scaled"], 1)
                assert chain.n == STEPS

            def gain(g, c, q, use):
                first = dve.value_load(window_tile[0:1, ds(c, 1)], min_val=0, max_val=NT)
                dve.wait_ge(s["acc"], g + 1)
                dve.wait_ge(s["shifted"], g + 1)
                dve.tensor_tensor(acc[:, ds(first, 2), :], acc[:, ds(first, 2), :], psB[:, :, 0:GW], ALU.add).then_inc(s["acc"], 1)

            def next_pass(r):
                dve.wait_ge(s["acc"], r * NC + NC + 1)
                dve.tensor_scalar(dst_r[:], dst_r[:], -float(P), None, ALU.add).then_inc(s["pass"], 1)
                dve.tensor_scalar(window[:], window[:], P, NT * P, ALU.add, ALU.min).then_inc(s["pass"], 1)
                dve.wait_ge(s["pass"], r * 3 + 5)
                dve.tensor_scalar(window_tile[:], window[:], 7, None, ALU.arith_shift_right).then_inc(s["pass"], 1)

            def sums(t, i, b, use):
                dve.wait_ge(s["squared"], t + 1)
                dve.tensor_reduce(ss[:, 0, :], sq.rearrange("p a (g d) -> p (a g) d", d=MD), AX.X, ALU.add).then_inc(s["kvsum"], 1)

            def keys(t, i, b, use):
                key.at(t * 2)
                dve.wait_ge(s["kvroot"], t + 1)
                key.link(dve.reciprocal(ss[:, 2, :], ss[:, 1, :]))
                key.link(dve.tensor_tensor(rkv[:], ss[:, 2, 0:MH], ss[:, 2, MH:2 * MH], ALU.mult))
                dve.wait_ge(s["dots"], t + SLOTS)
                dve.tensor_tensor(ks.rearrange("p (g d) -> p g d", d=MD), psKV[:, 0, :].rearrange("p (g d) -> p g d", d=MD),
                                  rkv[:].rearrange("p (g d) -> p g d", d=1).to_broadcast([P, MH, MD]), ALU.mult).then_inc(s["ks"], 1)
            key = Chain(dve, s["key"])
            if attention:
                dve.sem_inc(s["kvsum"], 1)
                dve.sem_inc(s["ks"], 1)
            rounds = chunks(dve, new_pass(dve), next_pass, (0, one_hot), (4, keys, True), (1, weigh), (3, gain), (3, sums, True))
            if attention:
                hold(dve, s["dots"], rounds * NT + SLOTS, s["tick"])
                for hp in range(4):
                    for h in range(2):
                        dve.tensor_scalar(dotsT[h * MD:(h + 1) * MD, hp, h * MD:(h + 1) * MD], psM[h * MD:(h + 1) * MD, hp * P + h * MD:hp * P + (h + 1) * MD],
                                          1.0 / N, None, ALU.mult).then_inc(s["end"], 1)
                dve.wait_ge(s["end"], 9)
                dve.tensor_copy(zmix.rearrange("p k f -> p (k f)"), psKV[:].rearrange("p a f -> p (a f)")).then_inc(s["end"], 1)
                dve.wait_ge(s["end"], 11)
                dve.tensor_copy(mixM[:].rearrange("p k f -> p (k f)"), psM[:, 0:2 * C])

        @block.scalar
        def _(act):
            act.sem_inc(s["hotT"], 1)
            act.wait_ge(s["own"], 1)
            act.activation(acc[:, 0:NT, C:GW], own[:, 0:NT, :], ACT.Exp).then_inc(s["own_weights"], 1)

            def floats(g, c, q, use):
                act.wait_ge(s["hot"], g * KT + KT)
                act.wait_ge(s["added"], g + 1)
                act.activation(hotf[:, q, :, :], hot[:, q, :, :], ACT.Copy).then_inc(s["hotf"], 1)

            def turned(g, c, q, use):
                act.wait_ge(s["turned"], g + 1)
                act.activation(hotT[:, q, :, :], psT[:], ACT.Copy).then_inc(s["hotT"], 1)

            def exps(g, c, q, use):
                act.wait_ge(s["logits"], g + 1 + SLOTS)
                act.activation(G[:, q, :, C:GW], t[:], ACT.Exp).then_inc(s["weights"], 1)

            def windows(g, c, q, use):
                act.wait_ge(s["added"], g + 1 + SLOTS)
                act.activation(win[:], psA[:, 0:GW], ACT.Copy).then_inc(s["win"], 1)

            def squares(t, i, b, use):
                act.wait_ge(s["keys_ps"], t + 1 + SLOTS)
                act.wait_ge(s["values_ps"], t + 1 + SLOTS)
                act.wait_ge(s["kvsum"], t + 1)
                act.activation(sq, psKV[:], ACT.Square).then_inc(s["squared"], 1)
                act.wait_ge(s["dots"], t + 1)
                act.activation(vs[b], psKV[:, 1, :], ACT.Copy).then_inc(s["vs"], 1)

            def roots(t, i, b, use):
                act.wait_ge(s["kvsum"], t + 2)
                act.activation(ss[:, 1, :], ss[:, 0, :], ACT.Sqrt, bias=eps[:, 0:1], scale=1.0 / MD).then_inc(s["kvroot"], 1)
            if attention:
                act.sem_inc(s["vs"], 1)
            chunks(act, nothing, nothing, (3, windows), (4, roots, True), (0, floats), (0, turned), (3, squares, True), (1, exps))

        @block.tensor
        def _(pe):
            pe.sem_inc(s["added"], SLOTS)

            def targets(g, c, q, use):
                pe.wait_ge(s[f"d_in{q}"], 16 * use + 16)
                pe.wait_ge(s["hotT"], g + 2)
                pe.wait_ge(s["target_read"], g + 1)
                for k in range(KT):
                    ins = pe.matmul(psD[:, 2 * k:2 * k + 2, :, :].rearrange("p g c h -> p (g c h)"), hotT[:, q, k, :], dwin[:, q, :], start=True, stop=True)
                ins.then_inc(s["targets"], 1)

            def turn(g, c, q, use):
                pe.wait_ge(s["hot"], g * KT + KT)
                pe.wait_ge(s["hotT"], g + 1)
                for k in range(KT):
                    ins = pe.transpose(psT[:, k, :], hot[:, q, k, :], identb[:])
                ins.then_inc(s["turned"], 1)

            def shifts(g, c, q, use):
                pe.wait_ge(s["shift"], g + 1)
                pe.wait_ge(s["win"], g + 1)
                pe.wait_ge(s["acc"], g + 1)
                for j in range(2):
                    ins = pe.matmul(psB[:, j, 0:GW], shift[:, q, j * P:(j + 1) * P], win[:], start=True, stop=True)
                ins.then_inc(s["shifted"], 1)

            def add(g, c, q, use):
                pe.wait_ge(s["hotf"], g + 1)
                pe.wait_ge(s["scaled"], g + 1)
                for k in range(KT):
                    ins = pe.matmul(psA[:, 0:GW], hotf[:, q, k, :], G[:, q, k, :], start=(k == 0), stop=(k == KT - 1))
                ins.then_inc(s["added"], 1)

            def values(t, i, b, use):
                pe.wait_ge(s[f"xn_in{b}"], 16 * use + 16)
                pe.wait_ge(s["vs"], t + 1)
                for kc in range(2):
                    ins = pe.matmul(psKV[:, 1, :], xnT[b][:, kc * P:(kc + 1) * P], wkvT[:, kc, 1, :], start=(kc == 0), stop=(kc == 1))
                ins.then_inc(s["values_ps"], 1)

            def keys(t, i, b, use):
                pe.wait_ge(s["ks"], t + 1)
                for kc in range(2):
                    ins = pe.matmul(psKV[:, 0, :], xnT[b][:, kc * P:(kc + 1) * P], wkvT[:, kc, 0, :], start=(kc == 0), stop=(kc == 1))
                ins.then_inc(s["keys_ps"], 1)

            def dots(t, i, b, use):
                pe.wait_ge(s["ks"], t + 2)
                pe.wait_ge(s["vs"], t + 2)
                r = rows_of(i)
                for hp in range(4):
                    ins = pe.matmul(psM[:, hp * P:(hp + 1) * P], vs[b][0:r, hp * P:(hp + 1) * P], ks[0:r, hp * P:(hp + 1) * P],
                                    start=(not later(i, 1) and hp == 0), stop=(r == LAST), skip_group_check=True)
                ins.then_inc(s["dots"], 1)
            if attention:
                pe.sem_inc(s["dots"], SLOTS)
                pe.sem_inc(s["values_ps"], SLOTS)
                pe.sem_inc(s["keys_ps"], SLOTS)
            chunks(pe, nothing, nothing, (5, dots, True), (1, targets), (0, turn), (3, shifts), (2, add), (1, values, True), (2, keys, True))
            if attention:
                pe.wait_ge(s["end"], 8)
                for hp in range(4):
                    ins = pe.matmul(psKV[:, hp // 2, (hp % 2) * C:(hp % 2 + 1) * C], dotsT[:, hp, :], woutT[:, hp, :], start=True, stop=True)
                ins.then_inc(s["end"], 1)
                pe.wait_ge(s["end"], 10)
                for kc in range(2):
                    for hp in range(4):
                        ins = pe.matmul(psM[:, kc * C:(kc + 1) * C], wq[:, hp, kc * P:(kc + 1) * P], zmix[:, hp, :], start=(hp == 0), stop=(hp == 3))
                ins.then_inc(s["end"], 1)


def project_hidden(nc, a, table, ident, acc, dtab, w1, weights_in, sem):
    with ExitStack() as ctx:
        def sb(name, shape, dt=F32):
            return ctx.enter_context(nc.sbuf_tensor(name, shape, dt))

        wext = sb("wext1", [P, 2, HW])
        att = sb("att1", [P, 2, C])
        attw = sb("attw1", [P, 2, C])
        bias = sb("bias1", [P, 2])
        rden = sb("rden1", [P, NT, H])
        h = sb("h1", [P, 2, C])
        hT = sb("hT1", [P, 2, 2, P])
        psX = ctx.enter_context(nc.psum_tensor("psX1", [P, 2, 512], F32))
        psH = ctx.enter_context(nc.psum_tensor("psH1", [P, 2, 512], F32))
        s = {n: sem("h_" + n) for n in ("loaded", "steps", "hidden", "turned", "relu", "projected", "out", "stored")}
        block = ctx.enter_context(nc.Block())

        @block.sync
        def _(sp):
            sp.dma_start(wext[:, :, 0:C], a["L0_gnn_W2"].rearrange("(k p) n -> p k n", p=P)).then_inc(s["loaded"], 16)
            sp.dma_start(att[:, 0, :], a["L0_gnn_att_src2"].rearrange("(o h) c -> o (h c)", o=1).to_broadcast([P, C])).then_inc(s["loaded"], 16)
            sp.dma_start(att[:, 1, :], a["L0_gnn_att_dst2"].rearrange("(o h) c -> o (h c)", o=1).to_broadcast([P, C])).then_inc(s["loaded"], 16)
            for kc in range(2):
                sp.dma_start(bias[:, kc:kc + 1], a["L0_gnn_b1"][kc * P:(kc + 1) * P].rearrange("(p o) -> p o", o=1)).then_inc(s["loaded"], 16)

            def store(i, q):
                sp.wait_ge(s["out"], i * 2 + 2)
                sp.dma_start(table[ds(i * P, P), :], acc[:, ds(i, 1), :].rearrange("p o f -> p (o f)")).then_inc(s["stored"], 16)
            tiles(sp, (0, store))
            sp.wait_ge(s["stored"], 16 * NT)

        @block.vector
        def _(dve):
            chain = Chain(dve, s["steps"])
            dve.wait_ge(s["loaded"], 80)
            attention_columns(dve, chain, wext, att, attw)
            chain.link(dve.reciprocal(rden[:], acc[:, 0:NT, C:GW]))

            def scale(i, q):
                if later(i, 2):
                    dve.wait_ge(s["turned"], i - 1)
                dve.tensor_tensor(h[:, q % 2, :].rearrange("p (h c) -> p h c", h=H), acc[:, ds(i, 1), 0:C].rearrange("p o (h c) -> p (o h) c", h=H),
                                  rden[:, ds(i, 1), :].rearrange("p o (h c) -> p (o h) c", c=1).to_broadcast([P, H, CH]), ALU.mult).then_inc(s["hidden"], 1)
            tiles(dve, (0, scale))

        @block.scalar
        def _(act):
            act.wait_ge(s["loaded"], 80)
            for e in range(0, NX, 4):
                act.dma_start(w1[:, e:e + 4, :, :], a["L0_ffn_w1"][e:e + 4].rearrange("e (k p) f -> p e k f", p=P)).then_inc(weights_in, 16)

            def relu(i, q):
                act.wait_ge(s["turned"], i + 1)
                if later(i, 2):
                    act.wait_ge(s["projected"], i - 1)
                for kc in range(2):
                    act.activation(hT[:, q % 2, kc, :], psX[:, q % 2, kc * P:(kc + 1) * P], ACT.Relu, bias=bias[:, kc:kc + 1]).then_inc(s["relu"], 1)

            def copies(i, q):
                act.wait_ge(s["projected"], i + 1)
                act.activation(acc[:, ds(i, 1), :].rearrange("p o f -> p (o f)"), psH[:, q % 2, 0:GW], ACT.Copy).then_inc(s["out"], 1)
                act.activation(dtab[:, ds(i, 1), :].rearrange("p o f -> p (o f)"), psH[:, q % 2, GW:HW], ACT.Copy).then_inc(s["out"], 1)
            tiles(act, (0, relu), (1, copies))

        @block.tensor
        def _(pe):
            def turn(i, q):
                pe.wait_ge(s["hidden"], i + 1)
                if later(i, 2):
                    pe.wait_ge(s["relu"], i * 2 - 2)
                for kc in range(2):
                    ins = pe.transpose(psX[:, q % 2, kc * P:(kc + 1) * P], h[:, q % 2, kc * P:(kc + 1) * P], ident[:])
                ins.then_inc(s["turned"], 1)

            def project(i, q):
                pe.wait_ge(s["relu"], i * 2 + 2)
                if later(i, 2):
                    pe.wait_ge(s["out"], i * 2 - 2)
                for kc in range(2):
                    ins = pe.matmul(psH[:, q % 2, 0:HW], hT[:, q % 2, kc, :], wext[:, kc, :], start=(kc == 0), stop=(kc == 1))
                ins.then_inc(s["projected"], 1)
            tiles(pe, (0, turn), (1, project))


def combine(nc, a, xnT_d, y_d, xf_d, ident, eps, acc, mixM, hot, share, sem):
    with ExitStack() as ctx:
        def sb(name, shape, dt=F32):
            return ctx.enter_context(nc.sbuf_tensor(name, shape, dt))

        bias = sb("cbias", [P, 2, C])
        beta = sb("cbeta", [P, C])
        gate = sb("gate", [P, 2, NX])
        gbias = sb("gbias", [P, NX])
        x = sb("cx", [P, BUFS, C])
        xb = sb("cxb", [P, BUFS, C])
        xnT = sb("cxnT", [P, BUFS, 2, P])
        rden = sb("crden", [P, NT, H])
        gat = sb("cgat", [P, BUFS, C])
        y = sb("cy", [P, BUFS, C])
        yb = sb("cyb", [P, BUFS, C])
        st = sb("cst", [P, BUFS, 6])
        mv = sb("cmv", [P, BUFS, 2])
        rs = sb("crs", [P, BUFS, 2])
        xf = sb("cxf", [P, BUFS, C])
        xfT = sb("cxfT", [P, 2, 2, P])
        logits = sb("logits", [P, NT, NX])
        masked = sb("masked", [P, NT, NX])
        number_i = sb("number_i", [P, NX], I32)
        number = sb("number", [P, NX])
        top = sb("top", [P, NT, 2])
        which = sb("which", [P, NT, 2])
        gap = sb("gap", [P, NT])
        one = sb("one", [P, NT])
        ps = ctx.enter_context(nc.psum_tensor("cps", [P, 2, 512], F32))
        psT = ctx.enter_context(nc.psum_tensor("cpsT", [P, 2, 512], F32))
        psG = ctx.enter_context(nc.psum_tensor("cpsG", [P, 2, 512], F32))
        s = {n: sem("c_" + n) for n in ("loaded", "steps", "x0", "x1", "x2", "x3", "mixed", "gat", "y", "yb", "stored0", "stored1", "stored2", "stored3",
                                        "divided", "halves", "inverse", "stats", "root", "xf", "xf_out0", "xf_out1", "xf_out2", "xf_out3", "turned", "xfT",
                                        "gated", "logits", "number", "bias", "xb", "gap", "exp", "tick")}
        block = ctx.enter_context(nc.Block())

        @block.sync
        def _(sp):
            sp.dma_start(bias[:, 0, :], a["L0_gnn_b2"].rearrange("(o c) -> o c", o=1).to_broadcast([P, C])).then_inc(s["loaded"], 16)
            sp.dma_start(bias[:, 1, :], a["L0_mix_bout"].rearrange("(o c) -> o c", o=1).to_broadcast([P, C])).then_inc(s["loaded"], 16)
            sp.dma_start(beta[:], a["L0_ffn_beta"].rearrange("(o c) -> o c", o=1).to_broadcast([P, C])).then_inc(s["loaded"], 16)
            sp.dma_start(gate[:], a["L0_ffn_gate_w"].rearrange("(k p) e -> p k e", p=P)).then_inc(s["loaded"], 16)
            sp.dma_start(gbias[:], a["L0_ffn_gate_b"].rearrange("(o e) -> o e", o=1).to_broadcast([P, NX])).then_inc(s["loaded"], 16)

            def load(i, q):
                r = rows_of(i)
                if later(i, BUFS):
                    sp.wait_ge(s["xb"], i - BUFS + 1)
                    sp.wait_ge(s["mixed"], i - BUFS + 1)
                sp.dma_start(x[0:r, q, :], a["x"][ds(i * P, r), :]).then_inc(s[f"x{q}"], 16)
                sp.dma_start(xnT[:, q, :, :].rearrange("p k f -> p (k f)"), xnT_d[ds(i, 1), :, :].rearrange("o p f -> (o p) f")).then_inc(s[f"x{q}"], 16)

            tiles(sp, (0, load))

        @block.tensor
        def _(pe):
            pe.wait_ge(s["loaded"], 80)

            def mix(i, q):
                pe.wait_ge(s[f"x{q}"], (i - q) * 8 + 32)
                if later(i, 2):
                    pe.wait_ge(s["y"], i - 1)
                for kc in range(2):
                    ins = pe.matmul(ps[:, q % 2, 0:C], xnT[:, q, kc, :], mixM[:, kc, :], start=(kc == 0), stop=(kc == 1))
                ins.then_inc(s["mixed"], 1)

            def turn(i, q):
                pe.wait_ge(s["xf"], i + 1)
                if later(i, 2):
                    pe.wait_ge(s["xfT"], i - 1)
                for kc in range(2):
                    ins = pe.transpose(psT[:, q % 2, kc * P:(kc + 1) * P], xf[:, q, kc * P:(kc + 1) * P], ident[:])
                ins.then_inc(s["turned"], 1)

            def gates(i, q):
                pe.wait_ge(s["xfT"], i + 1)
                if later(i, 2):
                    pe.wait_ge(s["logits"], i - 1)
                for kc in range(2):
                    ins = pe.matmul(psG[:, q % 2, 0:NX], xfT[:, q % 2, kc, :], gate[:, kc, :], start=(kc == 0), stop=(kc == 1))
                ins.then_inc(s["gated"], 1)
            tiles(pe, (2, mix), (7, gates), (6, turn))

        @block.gpsimd
        def _(pool):
            pool.iota(number_i[:], pattern=[[1, NX]], base=0, channel_multiplier=0).then_inc(s["number"], 1)
            pool.wait_ge(s["loaded"], 80)
            pool.tensor_tensor(bias[:, 0, :], bias[:, 0, :], bias[:, 1, :], ALU.add).then_inc(s["bias"], 1)
            pool.wait_ge(s["bias"], 1)

            def with_bias(i, q):
                pool.wait_ge(s[f"x{q}"], (i - q) * 8 + 32)
                if later(i, BUFS):
                    pool.wait_ge(s["gat"], i - BUFS + 1)
                pool.tensor_tensor(xb[:, q, :], x[:, q, :], bias[:, 0, :], ALU.add).then_inc(s["xb"], 1)

            def with_beta(i, q):
                pool.wait_ge(s["y"], i + 1)
                if later(i, BUFS):
                    pool.wait_ge(s[f"stored{q}"], (i - q) * 4)
                pool.tensor_tensor(yb[:, q, :], y[:, q, :], beta[:], ALU.add).then_inc(s["yb"], 1)
            tiles(pool, (1, with_bias), (4, with_beta))

        @block.vector
        def _(dve):
            chain = Chain(dve, s["steps"])
            dve.wait_ge(s["number"], 1)
            chain.link(dve.tensor_copy(number[:], number_i[:]))
            chain.link(dve.reciprocal(rden[:], acc[:, 0:NT, C:GW]))

            def divide(i, q):
                if later(i, BUFS):
                    dve.wait_ge(s["y"], i - BUFS + 1)
                dve.tensor_tensor(gat[:, q, :].rearrange("p (h c) -> p h c", h=H), acc[:, ds(i, 1), 0:C].rearrange("p o (h c) -> p (o h) c", h=H),
                                  rden[:, ds(i, 1), :].rearrange("p o (h c) -> p (o h) c", c=1).to_broadcast([P, H, CH]), ALU.mult).then_inc(s["divided"], 1)

            def add_x(i, q):
                dve.wait_ge(s["divided"], i + 1)
                dve.wait_ge(s["xb"], i + 1)
                dve.tensor_tensor(gat[:, q, :], gat[:, q, :], xb[:, q, :], ALU.add).then_inc(s["gat"], 1)

            def add_mix(i, q):
                dve.wait_ge(s["gat"], i + 1)
                dve.wait_ge(s["mixed"], i + 1)
                if later(i, BUFS):
                    dve.wait_ge(s["xf"], i - BUFS + 1)
                    dve.wait_ge(s["yb"], i - BUFS + 1)
                dve.tensor_tensor(y[:, q, :], gat[:, q, :], ps[:, q % 2, 0:C], ALU.add).then_inc(s["y"], 1)

            def stats(i, q):
                hold(dve, s["y"], i + 1, s["tick"])
                dve.bn_stats(st[:, q, :], y[:, q, :]).then_inc(s["halves"], 1)

            def moments(i, q):
                hold(dve, s["halves"], i + 1, s["tick"])
                dve.bn_aggr(mv[:, q, :], st[:, q, :]).then_inc(s["stats"], 1)

            def invert(i, q):
                dve.wait_ge(s["root"], i + 1)
                dve.reciprocal(rs[:, q, 1:2], rs[:, q, 0:1]).then_inc(s["inverse"], 1)

            def normalise(i, q):
                dve.wait_ge(s["inverse"], i + 1)
                if later(i, BUFS):
                    dve.wait_ge(s["turned"], i - BUFS + 1)
                    dve.wait_ge(s[f"xf_out{q}"], (i - q) * 4)
                dve.tensor_scalar(xf[:, q, :], y[:, q, :], mv[:, q, 0:1], rs[:, q, 1:2], ALU.subtract, ALU.mult).then_inc(s["xf"], 1)
            tiles(dve, (3, add_mix), (1, divide), (3, stats), (2, add_x), (3, moments), (4, invert), (5, normalise))
            dve.wait_ge(s["logits"], NT)
            chain.link(dve.tensor_tensor(logits[:], logits[:], gbias[:].rearrange("p (t e) -> p t e", t=1).to_broadcast([P, NT, NX]), ALU.add))
            wide = number[:].rearrange("p (t e) -> p t e", t=1).to_broadcast([P, NT, NX])
            for k in range(2):
                l = masked if k else logits
                h = hot[:, :, k, :]
                chain.link(dve.tensor_reduce(top[:, :, k], l[:], AX.X, ALU.max))
                chain.link(dve.tensor_tensor(h, l[:], top[:, :, k:k + 1].to_broadcast([P, NT, NX]), ALU.not_equal))
                chain.link(dve.scalar_tensor_tensor(h, h, float(NX), wide, ALU.mult, ALU.add))
                chain.link(dve.tensor_reduce(which[:, :, k], h, AX.X, ALU.min))
                chain.link(dve.tensor_tensor(h, wide, which[:, :, k:k + 1].to_broadcast([P, NT, NX]), ALU.is_equal))
                if k == 0:
                    chain.link(dve.scalar_tensor_tensor(masked[:], h, -3e38, logits[:], ALU.mult, ALU.add))
            dve.tensor_tensor(gap[:], top[:, :, 1], top[:, :, 0], ALU.subtract).then_inc(s["gap"], 1)
            dve.wait_ge(s["exp"], 1)
            chain.link(dve.tensor_scalar(one[:], gap[:], 1.0, None, ALU.add))
            chain.link(dve.reciprocal(share[:, :, 0], one[:]))
            chain.link(dve.tensor_tensor(share[:, :, 1], share[:, :, 0], gap[:], ALU.mult))

        @block.scalar
        def _(act):
            def root(i, q):
                act.wait_ge(s["stats"], i + 1)
                act.activation(rs[:, q, 0:1], mv[:, q, 1:2], ACT.Sqrt, bias=eps[:, 0:1]).then_inc(s["root"], 1)

            def turned(i, q):
                act.wait_ge(s["turned"], i + 1)
                if later(i, 2):
                    act.wait_ge(s["gated"], i - 1)
                act.activation(xfT[:, q % 2, :, :].rearrange("p k f -> p (k f)"), psT[:, q % 2, 0:2 * P], ACT.Copy).then_inc(s["xfT"], 1)

            def gates(i, q):
                act.wait_ge(s["gated"], i + 1)
                act.activation(logits[:, ds(i, 1), :].rearrange("p o f -> p (o f)"), psG[:, q % 2, 0:NX], ACT.Copy).then_inc(s["logits"], 1)
            def store(i, q):
                act.wait_ge(s["yb"], i + 1)
                act.dma_start(y_d[ds(i * P, P), :], yb[:, q, :]).then_inc(s[f"stored{q}"], 16)
                act.wait_ge(s["xf"], i + 1)
                act.dma_start(xf_d[ds(i * P, P), :], xf[:, q, :]).then_inc(s[f"xf_out{q}"], 16)
            tiles(act, (7, gates), (3, root), (6, turned), (6, store))
            act.wait_ge(s["gap"], 1)
            act.activation(gap[:], gap[:], ACT.Exp).then_inc(s["exp"], 1)
            for q in range(BUFS):
                act.wait_ge(s[f"stored{q}"], 16 * uses(q))
                act.wait_ge(s[f"xf_out{q}"], 16 * uses(q))


def order(nc, a, ones, hot, place, expert, w2, weights_in, sem):
    with ExitStack() as ctx:
        def sb(name, shape, dt=F32):
            return ctx.enter_context(nc.sbuf_tensor(name, shape, dt))

        before = sb("before", [P, P])
        both = sb("both", [P, NT, NX])
        rank = sb("rank", [P, NT, NX])
        total = sb("total", [P, NX, NT])
        carry = sb("carry", [P, NX, NT])
        keep = sb("keep", [P, NX, NT])
        count = sb("xcount", [P, NX])
        count_i = sb("xcount_i", [P, NX], I32)
        ntiles = sb("ntiles", [P, NX])
        upto = sb("upto", [P, NX])
        first = sb("xfirst", [P, NX])
        picked = sb("picked", [P, NT, NX])
        row = sb("row", [P, NT, 2])
        numbers_i = sb("numbers_i", [1, XT], I32)
        numbers = sb("numbers", [1, XT])
        past = sb("past", [1, XT, NX])
        owner = sb("owner", [1, XT])
        ps = [ctx.enter_context(nc.psum_tensor(f"ops{n}", [P, 512], F32)) for n in range(4)]
        s = {n: sem("o_" + n) for n in ("consts", "steps", "both", "ranked", "pads")}
        block = ctx.enter_context(nc.Block())
        HALF = (NT + 1) // 2
        parts = ((0, HALF), (HALF, NT))

        @block.scalar
        def _(act):
            for e in range(0, NX, 4):
                act.dma_start(w2[:, e:e + 4, :, :], a["L0_ffn_w2"][e:e + 4].rearrange("e (k p) f -> p e k f", p=P)).then_inc(weights_in, 16)

        @block.gpsimd
        def _(pool):
            pool.memset(before[:], 1.0).then_inc(s["pads"], 1)
            pool.iota(numbers_i[:], pattern=[[1, XT]], base=0, channel_multiplier=0).then_inc(s["consts"], 1)
            pool.wait_ge(s["pads"], 1)
            pool.affine_select(out=before[:], in_=before[:], compare_op=ALU.is_gt, fill=0.0, base=0,
                               pattern=[[1, P]], channel_multiplier=-1).then_inc(s["consts"], 1)

        @block.vector
        def _(dve):
            chain = Chain(dve, s["steps"])
            dve.wait_ge(s["consts"], 2)
            chain.link(dve.tensor_copy(numbers[:], numbers_i[:]))
            end = hot[:, NT - 1, :, :].rearrange("p s e -> p (s e)")
            chain.link(dve.tensor_scalar(end, end, before[:, LAST:LAST + 1], None, ALU.mult))
            chain.link(dve.tensor_tensor(both[:], hot[:, :, 0, :], hot[:, :, 1, :], ALU.add))
            chain.link(dve.memset(keep[:], 1.0))
            dve.memset(keep[:, :, 0], 0.0).then_inc(s["both"], 1)
            dve.wait_ge(s["ranked"], 1)
            for n, (lo, hi) in enumerate(parts):
                w = (hi - lo) * NX
                chain.link(dve.tensor_copy(rank[:, lo:hi, :].rearrange("p t e -> p (t e)"), ps[n][:, 0:w]))
                chain.link(dve.tensor_copy(total[:, :, lo:hi].rearrange("p e t -> p t e"), ps[2 + n][:, 0:w].rearrange("p (t e) -> p t e", e=NX)))
            chain.link(dve.tensor_tensor_scan(carry[:].rearrange("p e t -> p (e t)"), keep[:].rearrange("p e t -> p (e t)"),
                                              total[:].rearrange("p e t -> p (e t)"), 0.0, ALU.mult, ALU.add))
            chain.link(dve.tensor_scalar(count[:], carry[:, :, NT - 1], float(P - 1), None, ALU.add))
            chain.link(dve.tensor_tensor(carry[:], carry[:], total[:], ALU.subtract))
            chain.link(dve.tensor_copy(count_i[:], count[:]))
            chain.link(dve.tensor_scalar(count_i[:], count_i[:], 7, None, ALU.arith_shift_right))
            chain.link(dve.tensor_copy(ntiles[:], count_i[:]))
            chain.link(dve.memset(first[:], 1.0))
            chain.link(dve.tensor_tensor_scan(upto[:], first[:], ntiles[:], 0.0, ALU.mult, ALU.add))
            chain.link(dve.tensor_tensor(first[:], upto[:], ntiles[:], ALU.subtract))
            chain.link(dve.tensor_scalar(first[:], first[:], float(P), None, ALU.mult))
            chain.link(dve.tensor_tensor(rank[:], rank[:], carry[:].rearrange("p e t -> p t e"), ALU.add))
            chain.link(dve.tensor_tensor(rank[:], rank[:], first[:].rearrange("p (o e) -> p o e", o=1).to_broadcast([P, NT, NX]), ALU.add))
            for k in range(2):
                chain.link(dve.tensor_tensor(picked[:], rank[:], hot[:, :, k, :], ALU.mult))
                chain.link(dve.tensor_reduce(row[:, :, k], picked[:], AX.X, ALU.add))
            chain.link(dve.tensor_copy(place[:], row[:]))
            chain.link(dve.tensor_tensor(past[:], numbers[:].rearrange("o (t e) -> o t e", e=1).to_broadcast([1, XT, NX]),
                                         upto[0:1, :].rearrange("o (t e) -> o t e", t=1).to_broadcast([1, XT, NX]), ALU.is_ge))
            chain.link(dve.tensor_reduce(owner[:], past[:], AX.X, ALU.add))
            chain.link(dve.tensor_scalar(owner[:], owner[:], float(NX - 1), None, ALU.min))
            chain.link(dve.tensor_copy(expert[:], owner[:]))

        @block.tensor
        def _(pe):
            pe.wait_ge(s["consts"], 2)
            pe.wait_ge(s["both"], 1)
            for n, (lo, hi) in enumerate(parts):
                w = (hi - lo) * NX
                rhs = both[:, lo:hi, :].rearrange("p t e -> p (t e)")
                pe.matmul(ps[n][:, 0:w], before[:], rhs, start=True, stop=True)
                ins = pe.matmul(ps[2 + n][:, 0:w], ones[:], rhs, start=True, stop=True)
            ins.then_inc(s["ranked"], 1)


def dispatch(nc, a, xf_d, xs_d, place, b1T, b2, ident, weights_in, sem):
    with ExitStack() as ctx:
        rows = ctx.enter_context(nc.sbuf_tensor("disp_rows", [P, BUFS, C], F32))
        idx = ctx.enter_context(nc.sbuf_tensor("disp_idx", [P, BUFS, 2], I32))
        b1 = ctx.enter_context(nc.sbuf_tensor("b1_rows", [NX * FF // P, P], F32))
        ps = ctx.enter_context(nc.psum_tensor("disp_ps", [P, 512], F32))
        s = {n: sem("d_" + n) for n in ("row0", "row1", "row2", "row3", "idx", "sent0", "sent1", "sent2", "sent3", "b1", "b1T", "tick")}
        block = ctx.enter_context(nc.Block())

        @block.sync
        def _(sp):
            def load(i, q):
                if later(i, BUFS):
                    sp.wait_ge(s[f"sent{q}"], (i - q) * 8)
                sp.dma_start(rows[:, q, :], xf_d[ds(i * P, P), :]).then_inc(s[f"row{q}"], 16)
            tiles(sp, (0, load))

        @block.scalar
        def _(act):
            act.dma_start(b1[:], a["L0_ffn_b1"].rearrange("e (k p) -> (e k) p", p=P)).then_inc(s["b1"], 16)
            act.dma_start(b2[:].rearrange("p e f -> p (e f)"), a["L0_ffn_b2"].rearrange("(o e) f -> o (e f)", o=1).to_broadcast([P, NX * C])).then_inc(weights_in, 16)
            act.wait_ge(s["b1T"], 1)
            act.activation(b1T[:].rearrange("p e k -> p (e k)"), ps[:, 0:NX * FF // P], ACT.Copy)

        @block.tensor
        def _(pe):
            pe.wait_ge(s["b1"], 16)
            pe.transpose(ps[:, 0:NX * FF // P], b1[:], ident[0:NX * FF // P, 0:NX * FF // P]).then_inc(s["b1T"], 1)

        @block.vector
        def _(dve):
            def number(i, q):
                if later(i, BUFS):
                    hold(dve, s[f"sent{q}"], (i - q) * 8, s["tick"])
                dve.tensor_copy(idx[:, q, :], place[:, ds(i, 1), :].rearrange("p o f -> p (o f)")).then_inc(s["idx"], 1)
            tiles(dve, (0, number))

        @block.gpsimd
        def _(pool):
            def send(i, q):
                r = rows_of(i)
                pool.wait_ge(s[f"row{q}"], (i - q) * 4 + 16)
                hold(pool, s["idx"], i + 1, s["tick"])
                for k in range(2):
                    pool.indirect_dma_start(out=xs_d, out_offset=bass.IndirectOffsetOnAxis(ap=idx[0:r, q, k:k + 1], axis=0),
                                            in_=rows[0:r, q, :], in_offset=None).then_inc(s[f"sent{q}"], 16)
            tiles(pool, (0, send))
            for q in range(BUFS):
                pool.wait_ge(s[f"sent{q}"], 32 * uses(q))


def experts(nc, xs_d, ys_d, ident, expert, w1, w2, b1T, b2, weights_in, sem):
    with ExitStack() as ctx:
        def sb(name, shape, dt=F32):
            return ctx.enter_context(nc.sbuf_tensor(name, shape, dt))

        def pb(name):
            return ctx.enter_context(nc.psum_tensor(name, [P, 2, 512], F32))

        x = sb("xx", [P, BUFS, C])
        xT = sb("xxT", [P, 2, 2, P])
        w1e = sb("w1e", [P, 2, 2, FF])
        hidT = sb("hidT", [P, 2, FF])
        o = sb("xo", [P, BUFS, C])
        psX, psH, psO = pb("xpsX"), pb("xpsH"), pb("xpsO")
        s = {n: sem("x_" + n) for n in ("x0", "x1", "x2", "x3", "turned", "xT", "w1e", "hid_ps", "hidT", "o_ps", "o",
                                        "st0", "st1", "st2", "st3")}
        block = ctx.enter_context(nc.Block())

        def pairs(eng, *stages):
            def told(step):
                return lambda j, q, u: step(j, q)
            skewed(eng, XT, BUFS, BUFS, 0, [(n, told(step)) for n, step in stages])

        def expert_of(eng, j):
            return eng.value_load(expert[0:1, ds(j, 1)], min_val=0, max_val=NX - 1)

        @block.sync
        def _(sp):
            def load(j, q):
                if later(j, BUFS):
                    sp.wait_ge(s["turned"], j - BUFS + 1)
                sp.dma_start(x[:, q, :], xs_d[ds(j * P, P), :]).then_inc(s[f"x{q}"], 16)
            pairs(sp, (0, load))

        @block.scalar
        def _(act):
            def turned(j, q):
                act.wait_ge(s["turned"], j + 1)
                if later(j, 2):
                    act.wait_ge(s["hid_ps"], j - 1)
                act.activation(xT[:, q % 2, :, :].rearrange("p k f -> p (k f)"), psX[:, q % 2, 0:2 * P], ACT.Copy).then_inc(s["xT"], 1)

            def weights(j, q):
                e = expert_of(act, j)
                if later(j, 2):
                    act.wait_ge(s["hid_ps"], j - 1)
                act.activation(w1e[:, q % 2, :, :].rearrange("p k f -> p (k f)"), w1[:, ds(e, 1), :, :].rearrange("p o k f -> p (o k f)"), ACT.Copy).then_inc(s["w1e"], 1)
            act.wait_ge(weights_in, 144)
            pairs(act, (0, weights), (0, turned))

        @block.vector
        def _(dve):
            def relu(j, q):
                e = expert_of(dve, j)
                dve.wait_ge(s["hid_ps"], j + 1)
                if later(j, 2):
                    dve.wait_ge(s["o_ps"], j - 1)
                for k in range(FF // P):
                    dve.tensor_scalar(hidT[:, q % 2, k * P:(k + 1) * P], psH[:, q % 2, k * P:(k + 1) * P],
                                      b1T[:, ds(e, 1), k:k + 1].rearrange("p o k -> p (o k)"), 0.0, ALU.add, ALU.max).then_inc(s["hidT"], 1)

            def result(j, q):
                e = expert_of(dve, j)
                dve.wait_ge(s["o_ps"], j + 1)
                if later(j, BUFS):
                    dve.wait_ge(s[f"st{q}"], (j - q) * 4)
                dve.tensor_tensor(o[:, q, :], psO[:, q % 2, 0:C], b2[:, ds(e, 1), :].rearrange("p o f -> p (o f)"), ALU.add).then_inc(s["o"], 1)
            dve.wait_ge(weights_in, 144)
            pairs(dve, (3, result), (1, relu))

        @block.tensor
        def _(pe):
            def turn(j, q):
                pe.wait_ge(s[f"x{q}"], (j - q) * 4 + 16)
                if later(j, 2):
                    pe.wait_ge(s["xT"], j - 1)
                for kc in range(2):
                    ins = pe.transpose(psX[:, q % 2, kc * P:(kc + 1) * P], x[:, q, kc * P:(kc + 1) * P], ident[:])
                ins.then_inc(s["turned"], 1)

            def up(j, q):
                pe.wait_ge(s["xT"], j + 1)
                pe.wait_ge(s["w1e"], j + 1)
                if later(j, 2):
                    pe.wait_ge(s["hidT"], (j - 1) * (FF // P))
                for k in range(FF // P):
                    for kc in range(2):
                        ins = pe.matmul(psH[:, q % 2, k * P:(k + 1) * P], w1e[:, q % 2, kc, k * P:(k + 1) * P], xT[:, q % 2, kc, :], start=(kc == 0), stop=(kc == 1))
                ins.then_inc(s["hid_ps"], 1)

            def down(j, q):
                e = expert_of(pe, j)
                pe.wait_ge(s["hidT"], (j + 1) * (FF // P))
                if later(j, 2):
                    pe.wait_ge(s["o"], j - 1)
                for k in range(FF // P):
                    ins = pe.matmul(psO[:, q % 2, 0:C], hidT[:, q % 2, k * P:(k + 1) * P], w2[:, ds(e, 1), k, :].rearrange("p o f -> p (o f)"),
                                    start=(k == 0), stop=(k == FF // P - 1))
                ins.then_inc(s["o_ps"], 1)
            pe.wait_ge(weights_in, 144)
            pairs(pe, (0, turn), (3, down), (1, up))

        @block.gpsimd
        def _(pool):
            def store(j, q):
                pool.wait_ge(s["o"], j + 1)
                pool.dma_start(ys_d[ds(j * P, P), :], o[:, q, :]).then_inc(s[f"st{q}"], 16)
            pairs(pool, (0, store))
            for q in range(BUFS):
                pool.wait_ge(s[f"st{q}"], 16 * uses(q, XT))


def finish(nc, a, y_d, xf_d, ys_d, out, eps, place, share, sem):
    with ExitStack() as ctx:
        def sb(name, shape, dt=F32):
            return ctx.enter_context(nc.sbuf_tensor(name, shape, dt))

        gamma = sb("gamma", [P, C])
        idx = sb("fidx", [P, BUFS, 2], I32)
        y = sb("fy", [P, BUFS, C])
        xf = sb("fxf", [P, BUFS, C])
        e1 = sb("fe1", [P, BUFS, C])
        e2 = sb("fe2", [P, BUFS, C])
        part = sb("fpart", [P, BUFS, C])
        moe = sb("fmoe", [P, BUFS, C])
        unit = sb("funit", [P, BUFS, C])
        st = sb("fst", [P, BUFS, 6])
        mv = sb("fmv", [P, BUFS, 2])
        rs = sb("frs", [P, BUFS, 3])
        o = sb("fo", [P, BUFS, C])
        s = {n: sem("f_" + n) for n in ("loaded", "part", "halves", "inverse", "scaled", "y0", "y1", "y2", "y3", "xf0", "xf1", "xf2", "xf3", "idx", "e0", "e1", "e2", "e3", "moe",
                                        "stats", "root", "scale", "unit", "o", "out0", "out1", "out2", "out3", "tick")}
        block = ctx.enter_context(nc.Block())

        @block.sync
        def _(sp):
            sp.dma_start(gamma[:], a["L0_ffn_gamma"].rearrange("(o e) -> o e", o=1).to_broadcast([P, C])).then_inc(s["loaded"], 16)

            def load_xf(i, q):
                if later(i, BUFS):
                    sp.wait_ge(s["part"], i - BUFS + 1)
                sp.dma_start(xf[:, q, :], xf_d[ds(i * P, P), :]).then_inc(s[f"xf{q}"], 16)

            def load_y(i, q):
                if later(i, BUFS):
                    sp.wait_ge(s["o"], i - BUFS + 1)
                sp.dma_start(y[:, q, :], y_d[ds(i * P, P), :]).then_inc(s[f"y{q}"], 16)
            tiles(sp, (0, load_xf), (3, load_y))

        @block.gpsimd
        def _(pool):
            def gather(i, q):
                if later(i, BUFS):
                    pool.wait_ge(s["moe"], i - BUFS + 1)
                hold(pool, s["idx"], i + 1, s["tick"])
                for k, dst in enumerate((e1, e2)):
                    pool.indirect_dma_start(out=dst[:, q, :], out_offset=None, in_=ys_d,
                                            in_offset=bass.IndirectOffsetOnAxis(ap=idx[:, q, k:k + 1], axis=0)).then_inc(s[f"e{q}"], 16)
            tiles(pool, (0, gather))

        @block.scalar
        def _(act):
            def root(i, q):
                act.wait_ge(s["stats"], i + 1)
                act.activation(rs[:, q, 0:1], mv[:, q, 1:2], ACT.Sqrt, bias=eps[:, 0:1]).then_inc(s["root"], 1)

            def unit_rows(i, q):
                act.wait_ge(s["scale"], i + 1)
                if later(i, BUFS):
                    act.wait_ge(s["scaled"], i - BUFS + 1)
                act.activation(unit[:, q, :], moe[:, q, :], ACT.Identity, bias=rs[:, q, 2:3], scale=rs[:, q, 1:2]).then_inc(s["unit"], 1)

            def store(i, q):
                r = rows_of(i)
                act.wait_ge(s["o"], i + 1)
                act.dma_start(out[ds(i * P, r), :], o[0:r, q, :]).then_inc(s[f"out{q}"], 16)
            tiles(act, (5, unit_rows), (3, root), (8, store))
            for q in range(BUFS):
                act.wait_ge(s[f"out{q}"], 16 * uses(q))

        @block.vector
        def _(dve):
            def number(i, q):
                if later(i, BUFS):
                    hold(dve, s[f"e{q}"], (i - q) * 8, s["tick"])
                dve.tensor_copy(idx[:, q, :], place[:, ds(i, 1), :].rearrange("p o f -> p (o f)")).then_inc(s["idx"], 1)

            def add_first(i, q):
                dve.wait_ge(s[f"xf{q}"], (i - q) * 4 + 16)
                dve.wait_ge(s[f"e{q}"], (i - q) * 8 + 32)
                dve.scalar_tensor_tensor(part[:, q, :], e1[:, q, :], share[:, ds(i, 1), 0:1].rearrange("p o f -> p (o f)"), xf[:, q, :], ALU.mult, ALU.add).then_inc(s["part"], 1)

            def add_second(i, q):
                dve.wait_ge(s["part"], i + 1)
                if later(i, BUFS):
                    dve.wait_ge(s["unit"], i - BUFS + 1)
                dve.scalar_tensor_tensor(moe[:, q, :], e2[:, q, :], share[:, ds(i, 1), 1:2].rearrange("p o f -> p (o f)"), part[:, q, :], ALU.mult, ALU.add).then_inc(s["moe"], 1)

            def stats(i, q):
                hold(dve, s["moe"], i + 1, s["tick"])
                dve.bn_stats(st[:, q, :], moe[:, q, :]).then_inc(s["halves"], 1)

            def moments(i, q):
                hold(dve, s["halves"], i + 1, s["tick"])
                dve.bn_aggr(mv[:, q, :], st[:, q, :]).then_inc(s["stats"], 1)

            def invert(i, q):
                dve.wait_ge(s["root"], i + 1)
                dve.reciprocal(rs[:, q, 1:2], rs[:, q, 0:1]).then_inc(s["inverse"], 1)

            def shift(i, q):
                dve.wait_ge(s["inverse"], i + 1)
                dve.scalar_tensor_tensor(rs[:, q, 2:3], mv[:, q, 0:1], -1.0, rs[:, q, 1:2], ALU.mult, ALU.mult).then_inc(s["scale"], 1)

            def times_gamma(i, q):
                dve.wait_ge(s["unit"], i + 1)
                if later(i, BUFS):
                    dve.wait_ge(s[f"out{q}"], (i - q) * 4)
                dve.tensor_tensor(o[:, q, :], unit[:, q, :], gamma[:], ALU.mult).then_inc(s["scaled"], 1)

            def add_y(i, q):
                dve.wait_ge(s["scaled"], i + 1)
                dve.wait_ge(s[f"y{q}"], (i - q) * 4 + 16)
                dve.tensor_tensor(o[:, q, :], o[:, q, :], y[:, q, :], ALU.add).then_inc(s["o"], 1)
            dve.wait_ge(s["loaded"], 16)
            tiles(dve, (3, add_second), (6, times_gamma), (3, stats), (2, add_first), (3, moments), (7, add_y), (4, invert), (0, number), (4, shift))


_INS = ["x", "src", "dst", "L0_gnn_W1", "L0_gnn_att_src1", "L0_gnn_att_dst1", "L0_gnn_b1", "L0_gnn_W2", "L0_gnn_att_src2",
        "L0_gnn_att_dst2", "L0_gnn_b2", "L0_mix_Wqkv", "L0_mix_Wout", "L0_mix_bout", "L0_ffn_gate_w", "L0_ffn_gate_b",
        "L0_ffn_w1", "L0_ffn_b1", "L0_ffn_w2", "L0_ffn_b2", "L0_ffn_gamma", "L0_ffn_beta"]


def kernel(**inputs):
    import numpy as _np
    import concourse.bacc as _bacc
    from concourse import mybir as _mybir
    from concourse.bass_utils import run_bass_kernel_spmd as _run

    nc = _bacc.Bacc("TRN2", target_bir_lowering=False, num_devices=1)
    arrays, args = {}, {}
    for name in _INS:
        array = _np.ascontiguousarray(inputs[name])
        arrays[f"in_{name}"] = array
        args[name] = nc.dram_tensor(f"in_{name}", array.shape, _mybir.dt.from_np(array.dtype), kind="ExternalInput").ap()
    out = nc.dram_tensor("out_0", (N, C), _mybir.dt.float32, kind="ExternalOutput").ap()
    build(nc, args, out)
    r = _run(nc, [arrays], core_ids=[0])
    return r.results[0]["out_0"]
```
